# Optimizing a Trainium2 kernel written in Bass

```python
import numpy as np
import jax
import jax.numpy as jnp

def _softmax(x, axis=-1):
    return jax.nn.softmax(x, axis=axis)

def _gelu(x):
    return jax.nn.gelu(x, approximate=True)

def _silu(x):
    return jax.nn.silu(x)

def _sigmoid(x):
    return jax.nn.sigmoid(x)

def _layernorm(x, axis=-1, eps=1e-05):
    m = jnp.mean(x, axis=axis, keepdims=True)
    v = jnp.var(x, axis=axis, keepdims=True)
    return (x - m) / jnp.sqrt(v + eps)

def _scatter_add(tgt, idx, src, axis=0):
    return tgt.at[idx].add(src)

def _segment_sum(src, seg, n):
    return jax.ops.segment_sum(src, seg, n)
kernel_name = 'mk_audio_tower_d2_tok_aud1d768_r4_7f87b1'

def setup_inputs(seed: int=0):
    np.random.seed(seed)
    _w = jnp.asarray

    def _rec_inputs():
        import jax
        import jax.numpy as jnp
        _rk = jax.random.key(seed)
        x = 8.9527e-05 + 1.00009 * jax.random.normal(jax.random.fold_in(_rk, 1), (16, 40000), jnp.float32)
        return x
    x = _rec_inputs()

    def _L0_tok_setup():
        import jax, jax.numpy as jnp
        import numpy as np
        from jax import lax
        CONV_LAYERS = [(128, 10, 5), (128, 3, 2), (128, 3, 2), (128, 3, 2), (128, 3, 2), (128, 2, 2)]
        NUM_GROUPS = 32
        EPS = 1e-05
        EMBED_DIM = 192

        def _block(x, cw, cb, gw, gb, stride):
            y = lax.conv_general_dilated(x, cw, (stride,), 'VALID', dimension_numbers=('NCH', 'OIH', 'NCH'))
            y = y + cb[None, :, None]
            B, C, T = y.shape
            yg = y.reshape(B, NUM_GROUPS, C // NUM_GROUPS * T)
            mu = yg.mean(axis=-1, keepdims=True)
            var = yg.var(axis=-1, keepdims=True)
            yn = ((yg - mu) * lax.rsqrt(var + EPS)).reshape(B, C, T)
            yn = yn * gw[None, :, None] + gb[None, :, None]
            return jax.nn.gelu(yn)

        def _forward(x, conv_params, pw, pb):
            h = x[:, None, :]
            for (cw, cb, gw, gb), (_, _, s) in zip(conv_params, CONV_LAYERS):
                h = _block(h, cw, cb, gw, gb, s)
            h = jnp.transpose(h, (0, 2, 1))
            return jnp.einsum('bfc,ec->bfe', h, pw) + pb
        key = jax.random.key(seed)
        ks = jax.random.split(key, 16)
        inp = {'x': jax.random.normal(ks[0], (2, 80000), dtype=jnp.float32)}
        in_c = 1
        for li, (oc, k, s) in enumerate(CONV_LAYERS):
            lim = 1.0 / np.sqrt(in_c * k)
            inp[f'cw{li}'] = jax.random.uniform(jax.random.fold_in(ks[1], li), (oc, in_c, k), jnp.float32, -lim, lim)
            inp[f'cb{li}'] = jax.random.uniform(jax.random.fold_in(ks[2], li), (oc,), jnp.float32, -lim, lim)
            inp[f'gw{li}'] = jnp.ones((oc,), jnp.float32)
            inp[f'gb{li}'] = jnp.zeros((oc,), jnp.float32)
            in_c = oc
        lim = 1.0 / np.sqrt(128)
        inp['pw'] = jax.random.uniform(ks[3], (EMBED_DIM, 128), jnp.float32, -lim, lim)
        inp['pb'] = jax.random.uniform(ks[4], (EMBED_DIM,), jnp.float32, -lim, lim)
        return inp
    _L0_tok_all = _L0_tok_setup()
    _L0_tok_in = {k: v for k, v in _L0_tok_all.items() if k in ('cw0', 'cb0', 'gw0', 'gb0', 'cw1', 'cb1', 'gw1', 'gb1', 'cw2', 'cb2', 'gw2', 'gb2', 'cw3', 'cb3', 'gw3', 'gb3', 'cw4', 'cb4', 'gw4', 'gb4', 'cw5', 'cb5', 'gw5', 'gb5', 'pw', 'pb')}
    del _L0_tok_all

    def _L0_attn_setup():
        import jax, jax.numpy as jnp
        import numpy as np
        ALPHA = 0.35

        def _round_ln_pow2(x):
            y = jnp.floor(jnp.log2(x))
            up = x - 2.0 ** y > 2.0 ** (y + 1.0) - x
            return 2.0 ** (y + up.astype(x.dtype))
        key = jax.random.key(seed)
        k1, k2, k3, k4, k5 = jax.random.split(key, 5)
        B, N, C = (64, 197, 192)
        return {'x': jax.random.normal(k1, (B, N, C), dtype=jnp.float32), 'qkv_weight': jax.random.normal(k2, (3 * C, C), dtype=jnp.float32) * 0.02, 'qkv_bias': jax.random.normal(k3, (3 * C,), dtype=jnp.float32) * 0.02, 'proj_weight': jax.random.normal(k4, (C, C), dtype=jnp.float32) * 0.02, 'proj_bias': jax.random.normal(k5, (C,), dtype=jnp.float32) * 0.02}
    _L0_attn_all = _L0_attn_setup()
    _L0_attn_in = {k: v for k, v in _L0_attn_all.items() if k in ('qkv_weight', 'qkv_bias', 'proj_weight', 'proj_bias')}
    del _L0_attn_all

    def _L0_ffn_setup():
        import jax, jax.numpy as jnp
        import numpy as np
        EPS = 1e-06

        def l2_normalize(x, axis):
            norm = jnp.sqrt(jnp.square(x).sum(axis=axis, keepdims=True))
            return x * (1.0 / (norm + EPS))
        key = jax.random.key(seed)
        ks = jax.random.split(key, 8)
        b, m, d = (32, 256, 192)
        n, p = (8, 4)
        h = d // 8
        X = jax.random.normal(ks[0], (b, m, d), dtype=jnp.float32)
        std_slot = float(np.sqrt(2.0 / (d + n * p)))
        slot_params = jax.random.normal(ks[1], (d, n, p), dtype=jnp.float32) * std_slot
        scale = jnp.ones((), dtype=jnp.float32)
        W_down = jax.random.normal(ks[2], (n, d, h), dtype=jnp.float32) * float(np.sqrt(1.0 / d))
        b_down = jnp.zeros((n, h), dtype=jnp.float32)
        W_up = jax.random.normal(ks[3], (n, h, d), dtype=jnp.float32) * float(np.sqrt(1.0 / h))
        b_up = jnp.zeros((n, d), dtype=jnp.float32)
        return {'X': X, 'slot_params': slot_params, 'scale': scale, 'W_down': W_down, 'b_down': b_down, 'W_up': W_up, 'b_up': b_up}
    _L0_ffn_all = _L0_ffn_setup()
    _L0_ffn_in = {k: v for k, v in _L0_ffn_all.items() if k in ('slot_params', 'scale', 'W_down', 'b_down', 'W_up', 'b_up')}
    del _L0_ffn_all

    def _L1_attn_setup():
        import jax, jax.numpy as jnp
        import numpy as np
        B, S, E, H = (1, 512, 192, 12)
        D = E // H
        EPS = 1.0
        N_IT = 3
        LN_EPS = 1e-12

        def _sinkhorn_plan(scores):
            C = -scores
            n = scores.shape[-1]
            log_mu = -jnp.log(jnp.asarray(n, scores.dtype))

            def M(u, v):
                return (-C + u[..., :, None] + v[..., None, :]) / EPS
            u = jnp.zeros(scores.shape[:-1], scores.dtype)
            v = jnp.zeros(scores.shape[:-1], scores.dtype)

            def step(carry, _):
                u, v = carry
                u = EPS * (log_mu - jax.scipy.special.logsumexp(M(u, v), axis=-1)) + u
                v = EPS * (log_mu - jax.scipy.special.logsumexp(M(u, v), axis=-2)) + v
                return ((u, v), None)
            (u, v), _ = jax.lax.scan(step, (u, v), None, length=N_IT)
            return jnp.exp(M(u, v))
        key = jax.random.key(seed)
        ks = jax.random.split(key, 9)
        s = 0.02
        return {'hidden_states': jax.random.normal(ks[0], (B, S, E), jnp.float32), 'Wq': jax.random.normal(ks[1], (E, E), jnp.float32) * s, 'bq': jnp.zeros((E,), jnp.float32), 'Wk': jax.random.normal(ks[2], (E, E), jnp.float32) * s, 'bk': jnp.zeros((E,), jnp.float32), 'Wv': jax.random.normal(ks[3], (E, E), jnp.float32) * s, 'bv': jnp.zeros((E,), jnp.float32), 'Wo': jax.random.normal(ks[4], (E, E), jnp.float32) * s, 'bo': jnp.zeros((E,), jnp.float32), 'ln_g': jnp.ones((E,), jnp.float32), 'ln_b': jnp.zeros((E,), jnp.float32)}
    _L1_attn_all = _L1_attn_setup()
    _L1_attn_in = {k: v for k, v in _L1_attn_all.items() if k in ('Wq', 'bq', 'Wk', 'bk', 'Wv', 'bv', 'Wo', 'bo', 'ln_g', 'ln_b')}
    del _L1_attn_all

    def _L1_ffn_setup():
        import jax, jax.numpy as jnp
        import numpy as np
        B, L, D, H, F = (4, 512, 192, 12, 768)
        ROUTE_FRAC = 0.15
        LN_EPS = 1e-05

        def _ln(x, g, b):
            m = jnp.mean(x, axis=-1, keepdims=True)
            v = jnp.mean((x - m) ** 2, axis=-1, keepdims=True)
            return (x - m) * jax.lax.rsqrt(v + LN_EPS) * g + b
        key = jax.random.key(seed)
        ks = jax.random.split(key, 20)
        s = 0.02
        return {'hidden_states': jax.random.normal(ks[0], (B, L, D), dtype=jnp.float32), 'g1': jnp.ones((D,), jnp.float32), 'b1': jnp.zeros((D,), jnp.float32), 'g2': jnp.ones((D,), jnp.float32), 'b2': jnp.zeros((D,), jnp.float32), 'Wr': jax.random.normal(ks[1], (D,), jnp.float32) * s, 'br': jnp.zeros((), jnp.float32), 'Wq': jax.random.normal(ks[2], (D, D), jnp.float32) * s, 'bq': jnp.zeros((D,), jnp.float32), 'Wk': jax.random.normal(ks[3], (D, D), jnp.float32) * s, 'bk': jnp.zeros((D,), jnp.float32), 'Wv': jax.random.normal(ks[4], (D, D), jnp.float32) * s, 'bv': jnp.zeros((D,), jnp.float32), 'Wo': jax.random.normal(ks[5], (D, D), jnp.float32) * s, 'bo': jnp.zeros((D,), jnp.float32), 'Wm': jax.random.normal(ks[6], (D, D), jnp.float32) * s, 'bm': jnp.zeros((D,), jnp.float32), 'W1': jax.random.normal(ks[7], (D, F), jnp.float32) * s, 'bf1': jnp.zeros((F,), jnp.float32), 'W2': jax.random.normal(ks[8], (F, D), jnp.float32) * s, 'bf2': jnp.zeros((D,), jnp.float32)}
    _L1_ffn_all = _L1_ffn_setup()
    _L1_ffn_in = {k: v for k, v in _L1_ffn_all.items() if k in ('g1', 'b1', 'g2', 'b2', 'Wr', 'br', 'Wq', 'bq', 'Wk', 'bk', 'Wv', 'bv', 'Wo', 'bo', 'Wm', 'bm', 'W1', 'bf1', 'W2', 'bf2')}
    del _L1_ffn_all
    return {'x': x, 'L0_tok_cw0': _L0_tok_in['cw0'], 'L0_tok_cb0': _L0_tok_in['cb0'], 'L0_tok_gw0': _L0_tok_in['gw0'], 'L0_tok_gb0': _L0_tok_in['gb0'], 'L0_tok_cw1': _L0_tok_in['cw1'], 'L0_tok_cb1': _L0_tok_in['cb1'], 'L0_tok_gw1': _L0_tok_in['gw1'], 'L0_tok_gb1': _L0_tok_in['gb1'], 'L0_tok_cw2': _L0_tok_in['cw2'], 'L0_tok_cb2': _L0_tok_in['cb2'], 'L0_tok_gw2': _L0_tok_in['gw2'], 'L0_tok_gb2': _L0_tok_in['gb2'], 'L0_tok_cw3': _L0_tok_in['cw3'], 'L0_tok_cb3': _L0_tok_in['cb3'], 'L0_tok_gw3': _L0_tok_in['gw3'], 'L0_tok_gb3': _L0_tok_in['gb3'], 'L0_tok_cw4': _L0_tok_in['cw4'], 'L0_tok_cb4': _L0_tok_in['cb4'], 'L0_tok_gw4': _L0_tok_in['gw4'], 'L0_tok_gb4': _L0_tok_in['gb4'], 'L0_tok_cw5': _L0_tok_in['cw5'], 'L0_tok_cb5': _L0_tok_in['cb5'], 'L0_tok_gw5': _L0_tok_in['gw5'], 'L0_tok_gb5': _L0_tok_in['gb5'], 'L0_tok_pw': _L0_tok_in['pw'], 'L0_tok_pb': _L0_tok_in['pb'], 'L0_attn_qkv_weight': _L0_attn_in['qkv_weight'], 'L0_attn_qkv_bias': _L0_attn_in['qkv_bias'], 'L0_attn_proj_weight': _L0_attn_in['proj_weight'], 'L0_attn_proj_bias': _L0_attn_in['proj_bias'], 'L0_ffn_slot_params': _L0_ffn_in['slot_params'], 'L0_ffn_scale': _L0_ffn_in['scale'], 'L0_ffn_W_down': _L0_ffn_in['W_down'], 'L0_ffn_b_down': _L0_ffn_in['b_down'], 'L0_ffn_W_up': _L0_ffn_in['W_up'], 'L0_ffn_b_up': _L0_ffn_in['b_up'], 'L1_attn_Wq': _L1_attn_in['Wq'], 'L1_attn_bq': _L1_attn_in['bq'], 'L1_attn_Wk': _L1_attn_in['Wk'], 'L1_attn_bk': _L1_attn_in['bk'], 'L1_attn_Wv': _L1_attn_in['Wv'], 'L1_attn_bv': _L1_attn_in['bv'], 'L1_attn_Wo': _L1_attn_in['Wo'], 'L1_attn_bo': _L1_attn_in['bo'], 'L1_attn_ln_g': _L1_attn_in['ln_g'], 'L1_attn_ln_b': _L1_attn_in['ln_b'], 'L1_ffn_g1': _L1_ffn_in['g1'], 'L1_ffn_b1': _L1_ffn_in['b1'], 'L1_ffn_g2': _L1_ffn_in['g2'], 'L1_ffn_b2': _L1_ffn_in['b2'], 'L1_ffn_Wr': _L1_ffn_in['Wr'], 'L1_ffn_br': _L1_ffn_in['br'], 'L1_ffn_Wq': _L1_ffn_in['Wq'], 'L1_ffn_bq': _L1_ffn_in['bq'], 'L1_ffn_Wk': _L1_ffn_in['Wk'], 'L1_ffn_bk': _L1_ffn_in['bk'], 'L1_ffn_Wv': _L1_ffn_in['Wv'], 'L1_ffn_bv': _L1_ffn_in['bv'], 'L1_ffn_Wo': _L1_ffn_in['Wo'], 'L1_ffn_bo': _L1_ffn_in['bo'], 'L1_ffn_Wm': _L1_ffn_in['Wm'], 'L1_ffn_bm': _L1_ffn_in['bm'], 'L1_ffn_W1': _L1_ffn_in['W1'], 'L1_ffn_bf1': _L1_ffn_in['bf1'], 'L1_ffn_W2': _L1_ffn_in['W2'], 'L1_ffn_bf2': _L1_ffn_in['bf2']}

def reference(x, L0_tok_cw0, L0_tok_cb0, L0_tok_gw0, L0_tok_gb0, L0_tok_cw1, L0_tok_cb1, L0_tok_gw1, L0_tok_gb1, L0_tok_cw2, L0_tok_cb2, L0_tok_gw2, L0_tok_gb2, L0_tok_cw3, L0_tok_cb3, L0_tok_gw3, L0_tok_gb3, L0_tok_cw4, L0_tok_cb4, L0_tok_gw4, L0_tok_gb4, L0_tok_cw5, L0_tok_cb5, L0_tok_gw5, L0_tok_gb5, L0_tok_pw, L0_tok_pb, L0_attn_qkv_weight, L0_attn_qkv_bias, L0_attn_proj_weight, L0_attn_proj_bias, L0_ffn_slot_params, L0_ffn_scale, L0_ffn_W_down, L0_ffn_b_down, L0_ffn_W_up, L0_ffn_b_up, L1_attn_Wq, L1_attn_bq, L1_attn_Wk, L1_attn_bk, L1_attn_Wv, L1_attn_bv, L1_attn_Wo, L1_attn_bo, L1_attn_ln_g, L1_attn_ln_b, L1_ffn_g1, L1_ffn_b1, L1_ffn_g2, L1_ffn_b2, L1_ffn_Wr, L1_ffn_br, L1_ffn_Wq, L1_ffn_bq, L1_ffn_Wk, L1_ffn_bk, L1_ffn_Wv, L1_ffn_bv, L1_ffn_Wo, L1_ffn_bo, L1_ffn_Wm, L1_ffn_bm, L1_ffn_W1, L1_ffn_bf1, L1_ffn_W2, L1_ffn_bf2):
    import jax
    import jax.numpy as jnp

    def _L0_tok_ref(x, cw0, cb0, gw0, gb0, cw1, cb1, gw1, gb1, cw2, cb2, gw2, gb2, cw3, cb3, gw3, gb3, cw4, cb4, gw4, gb4, cw5, cb5, gw5, gb5, pw, pb):
        import jax, jax.numpy as jnp
        import numpy as np
        from jax import lax
        CONV_LAYERS = [(128, 10, 5), (128, 3, 2), (128, 3, 2), (128, 3, 2), (128, 3, 2), (128, 2, 2)]
        NUM_GROUPS = 32
        EPS = 1e-05
        EMBED_DIM = 192

        def _block(x, cw, cb, gw, gb, stride):
            y = lax.conv_general_dilated(x, cw, (stride,), 'VALID', dimension_numbers=('NCH', 'OIH', 'NCH'))
            y = y + cb[None, :, None]
            B, C, T = y.shape
            yg = y.reshape(B, NUM_GROUPS, C // NUM_GROUPS * T)
            mu = yg.mean(axis=-1, keepdims=True)
            var = yg.var(axis=-1, keepdims=True)
            yn = ((yg - mu) * lax.rsqrt(var + EPS)).reshape(B, C, T)
            yn = yn * gw[None, :, None] + gb[None, :, None]
            return jax.nn.gelu(yn)

        def _forward(x, conv_params, pw, pb):
            h = x[:, None, :]
            for (cw, cb, gw, gb), (_, _, s) in zip(conv_params, CONV_LAYERS):
                h = _block(h, cw, cb, gw, gb, s)
            h = jnp.transpose(h, (0, 2, 1))
            return jnp.einsum('bfc,ec->bfe', h, pw) + pb
        conv_params = [(cw0, cb0, gw0, gb0), (cw1, cb1, gw1, gb1), (cw2, cb2, gw2, gb2), (cw3, cb3, gw3, gb3), (cw4, cb4, gw4, gb4), (cw5, cb5, gw5, gb5)]
        return _forward(x, conv_params, pw, pb)

    def _L0_attn_ref(x, qkv_weight, qkv_bias, proj_weight, proj_bias):
        import jax, jax.numpy as jnp
        import numpy as np
        ALPHA = 0.35

        def _round_ln_pow2(x):
            y = jnp.floor(jnp.log2(x))
            up = x - 2.0 ** y > 2.0 ** (y + 1.0) - x
            return 2.0 ** (y + up.astype(x.dtype))
        B, N, C = x.shape
        num_heads = 12
        head_dim = C // num_heads
        scale = head_dim ** (-0.5)
        global_max_x = jnp.abs(x).max(axis=(0, 1))
        max_weight = jnp.abs(qkv_weight).max(axis=0)
        channel_scale = _round_ln_pow2(global_max_x ** ALPHA / max_weight ** (1.0 - ALPHA))
        x_smoothed = x / channel_scale[None, None, :]
        weight_smoothed = qkv_weight * channel_scale[None, :]
        h = jnp.einsum('bnc,mc->bnm', x_smoothed, weight_smoothed) + qkv_bias
        qkv = h.reshape(B, N, 3, num_heads, head_dim).transpose(2, 0, 3, 1, 4)
        q, k, v = (qkv[0], qkv[1], qkv[2])
        attn = jnp.einsum('bhnd,bhmd->bhnm', q, k) * scale
        attn = jax.nn.softmax(attn, axis=-1)
        out = jnp.einsum('bhnm,bhmd->bhnd', attn, v)
        out = out.transpose(0, 2, 1, 3).reshape(B, N, C)
        out = jnp.einsum('bnc,mc->bnm', out, proj_weight) + proj_bias
        return out

    def _L0_ffn_ref(X, slot_params, scale, W_down, b_down, W_up, b_up):
        import jax, jax.numpy as jnp
        import numpy as np
        EPS = 1e-06

        def l2_normalize(x, axis):
            norm = jnp.sqrt(jnp.square(x).sum(axis=axis, keepdims=True))
            return x * (1.0 / (norm + EPS))
        b, m, d = X.shape
        _, n, p = slot_params.shape
        Xn = l2_normalize(X, axis=-1)
        sp = l2_normalize(slot_params, axis=1) * scale
        logits = jnp.einsum('bmd,dnp->bmnp', Xn, sp)
        D = jax.nn.softmax(logits, axis=1)
        C = jax.nn.softmax(logits.reshape(b, m, n * p), axis=2).reshape(b, m, n, p)
        X_tilde = jnp.einsum('bmd,bmnp->bnpd', Xn, D)
        H = jax.nn.gelu(jnp.einsum('bnpd,ndh->bnph', X_tilde, W_down) + b_down[None, :, None, :], approximate=False)
        Y_tilde = jnp.einsum('bnph,nhd->bnpd', H, W_up) + b_up[None, :, None, :]
        Y = jnp.einsum('bnpd,bmnp->bmd', Y_tilde, C)
        return Y

    def _L1_attn_ref(hidden_states, Wq, bq, Wk, bk, Wv, bv, Wo, bo, ln_g, ln_b):
        import jax, jax.numpy as jnp
        import numpy as np
        B, S, E, H = (1, 512, 192, 12)
        D = E // H
        EPS = 1.0
        N_IT = 3
        LN_EPS = 1e-12

        def _sinkhorn_plan(scores):
            C = -scores
            n = scores.shape[-1]
            log_mu = -jnp.log(jnp.asarray(n, scores.dtype))

            def M(u, v):
                return (-C + u[..., :, None] + v[..., None, :]) / EPS
            u = jnp.zeros(scores.shape[:-1], scores.dtype)
            v = jnp.zeros(scores.shape[:-1], scores.dtype)

            def step(carry, _):
                u, v = carry
                u = EPS * (log_mu - jax.scipy.special.logsumexp(M(u, v), axis=-1)) + u
                v = EPS * (log_mu - jax.scipy.special.logsumexp(M(u, v), axis=-2)) + v
                return ((u, v), None)
            (u, v), _ = jax.lax.scan(step, (u, v), None, length=N_IT)
            return jnp.exp(M(u, v))
        b, s, e = hidden_states.shape

        def heads(x):
            return x.reshape(b, s, H, D).transpose(0, 2, 1, 3)
        q = heads(hidden_states @ Wq + bq)
        k = heads(hidden_states @ Wk + bk)
        v = heads(hidden_states @ Wv + bv)
        scores = jnp.einsum('bhsd,bhtd->bhst', q, k) / np.sqrt(D).astype(np.float32)
        attn = _sinkhorn_plan(scores) * jnp.asarray(s, scores.dtype)
        ctx = jnp.einsum('bhst,bhtd->bhsd', attn, v)
        ctx = ctx.transpose(0, 2, 1, 3).reshape(b, s, e)
        y = ctx @ Wo + bo + hidden_states
        mu = jnp.mean(y, axis=-1, keepdims=True)
        var = jnp.mean(jnp.square(y - mu), axis=-1, keepdims=True)
        return ln_g * (y - mu) / jnp.sqrt(var + LN_EPS) + ln_b

    def _L1_ffn_ref(hidden_states, g1, b1, g2, b2, Wr, br, Wq, bq, Wk, bk, Wv, bv, Wo, bo, Wm, bm, W1, bf1, W2, bf2):
        import jax, jax.numpy as jnp
        import numpy as np
        B, L, D, H, F = (4, 512, 192, 12, 768)
        ROUTE_FRAC = 0.15
        LN_EPS = 1e-05

        def _ln(x, g, b):
            m = jnp.mean(x, axis=-1, keepdims=True)
            v = jnp.mean((x - m) ** 2, axis=-1, keepdims=True)
            return (x - m) * jax.lax.rsqrt(v + LN_EPS) * g + b
        b, l, d = hidden_states.shape
        dh = d // H
        normed = _ln(hidden_states, g1, b1)
        scores = jax.nn.sigmoid(jnp.einsum('bld,d->bl', normed, Wr) + br)
        k = max(1, int(round(ROUTE_FRAC * l)))
        _, idx = jax.lax.top_k(-scores, k)
        attn_mask = jnp.zeros((b, l), bool).at[jnp.arange(b)[:, None], idx].set(True)
        q = (normed @ Wq + bq).reshape(b, l, H, dh)
        kk = (normed @ Wk + bk).reshape(b, l, H, dh)
        v = (normed @ Wv + bv).reshape(b, l, H, dh)
        logits = jnp.einsum('blhd,bmhd->bhlm', q, kk) / jnp.sqrt(jnp.float32(dh))
        probs = jax.nn.softmax(logits, axis=-1)
        ctx = jnp.einsum('bhlm,bmhd->blhd', probs, v).reshape(b, l, d)
        attn_out = ctx @ Wo + bo
        w = scores / (jnp.sum(scores, axis=1, keepdims=True) + 1e-06)
        pooled = jnp.einsum('bl,bld->bd', w, normed)
        mix_out = (normed + scores[..., None] * pooled[:, None, :]) @ Wm + bm
        merged = jnp.where(attn_mask[..., None], attn_out, mix_out)
        h = hidden_states + merged
        n2 = _ln(h, g2, b2)
        ffn = jax.nn.gelu(n2 @ W1 + bf1, approximate=False) @ W2 + bf2
        return h + ffn
    h = _L0_tok_ref(x, L0_tok_cw0, L0_tok_cb0, L0_tok_gw0, L0_tok_gb0, L0_tok_cw1, L0_tok_cb1, L0_tok_gw1, L0_tok_gb1, L0_tok_cw2, L0_tok_cb2, L0_tok_gw2, L0_tok_gb2, L0_tok_cw3, L0_tok_cb3, L0_tok_gw3, L0_tok_gb3, L0_tok_cw4, L0_tok_cb4, L0_tok_gw4, L0_tok_gb4, L0_tok_cw5, L0_tok_cb5, L0_tok_gw5, L0_tok_gb5, L0_tok_pw, L0_tok_pb)
    h = h + _L0_attn_ref(_layernorm(h, axis=-1), L0_attn_qkv_weight, L0_attn_qkv_bias, L0_attn_proj_weight, L0_attn_proj_bias)
    h = h + _L0_ffn_ref(_layernorm(h, axis=-1), L0_ffn_slot_params, L0_ffn_scale, L0_ffn_W_down, L0_ffn_b_down, L0_ffn_W_up, L0_ffn_b_up)
    h = h + _L1_attn_ref(_layernorm(h, axis=-1), L1_attn_Wq, L1_attn_bq, L1_attn_Wk, L1_attn_bk, L1_attn_Wv, L1_attn_bv, L1_attn_Wo, L1_attn_bo, L1_attn_ln_g, L1_attn_ln_b)
    h = h + _L1_ffn_ref(_layernorm(h, axis=-1), L1_ffn_g1, L1_ffn_b1, L1_ffn_g2, L1_ffn_b2, L1_ffn_Wr, L1_ffn_br, L1_ffn_Wq, L1_ffn_bq, L1_ffn_Wk, L1_ffn_bk, L1_ffn_Wv, L1_ffn_bv, L1_ffn_Wo, L1_ffn_bo, L1_ffn_Wm, L1_ffn_bm, L1_ffn_W1, L1_ffn_bf1, L1_ffn_W2, L1_ffn_bf2)
    return h

_drawn_inputs = setup_inputs


def setup_inputs(seed=0):
    import zlib

    import numpy as np

    out = dict(_drawn_inputs(seed))
    spreads = {'L0_tok_gw0': (1.0, 0.2),
     'L0_tok_gb0': (0.0, 0.1),
     'L0_tok_gw1': (1.0, 0.2),
     'L0_tok_gb1': (0.0, 0.1),
     'L0_tok_gw2': (1.0, 0.2),
     'L0_tok_gb2': (0.0, 0.1),
     'L0_tok_gw3': (1.0, 0.2),
     'L0_tok_gb3': (0.0, 0.1),
     'L0_tok_gw4': (1.0, 0.2),
     'L0_tok_gb4': (0.0, 0.1),
     'L0_tok_gw5': (1.0, 0.2),
     'L0_tok_gb5': (0.0, 0.1),
     'L0_ffn_b_down': (0.0, 0.1),
     'L0_ffn_b_up': (0.0, 0.1),
     'L1_attn_bq': (0.0, 0.8),
     'L1_attn_bk': (0.0, 0.8),
     'L1_attn_bv': (0.0, 0.384),
     'L1_attn_bo': (0.0, 0.1),
     'L1_attn_ln_g': (1.0, 0.2),
     'L1_attn_ln_b': (0.0, 0.1),
     'L1_ffn_g1': (1.0, 0.2),
     'L1_ffn_b1': (0.0, 0.46),
     'L1_ffn_g2': (1.0, 0.6),
     'L1_ffn_b2': (0.0, 0.8),
     'L1_ffn_bq': (0.0, 0.8),
     'L1_ffn_bk': (0.0, 0.8),
     'L1_ffn_bv': (0.0, 0.8),
     'L1_ffn_bo': (0.0, 0.551),
     'L1_ffn_bm': (0.0, 0.1),
     'L1_ffn_bf1': (0.0, 0.688),
     'L1_ffn_bf2': (0.0, 0.1)}
    factors = {'L0_attn_qkv_bias': 3.933,
     'L0_ffn_slot_params': 3.194,
     'L0_ffn_W_down': 2.703,
     'L1_attn_Wq': 8.0,
     'L1_attn_Wk': 8.0,
     'L1_ffn_Wq': 8.0,
     'L1_ffn_Wk': 8.0,
     'L1_ffn_Wv': 6.747,
     'L1_ffn_Wo': 6.353}
    for name, (base, spread) in spreads.items():
        noise = np.random.default_rng([zlib.crc32(name.encode()), seed]).standard_normal(out[name].shape)
        drawn = base * np.exp(spread * noise) if base else spread * noise
        out[name] = jnp.asarray(drawn.astype(out[name].dtype))
    for name, factor in factors.items():
        out[name] = (out[name] * factor).astype(out[name].dtype)
    return out
```

```python
from contextlib import ExitStack

import concourse.bass as bass
from concourse import mybir

ALU = mybir.AluOpType
ACT = mybir.ActivationFunctionType
F32 = mybir.dt.float32
BF16 = mybir.dt.bfloat16
U32 = mybir.dt.uint32
AX_X = mybir.AxisListType.X

CLIPS = 16
SAMPLES = 40000
LANES = (0, 1)
PAIRS = CLIPS // len(LANES)
P = 128
BANK = 512
LANE_BANKS = 4

CH = 128
GROUP = 4
GN_EPS = 1e-5
K0, S0 = 10, 5
LEN0 = (SAMPLES - K0) // S0 + 1
CONVS = [(3, 2), (3, 2), (3, 2), (3, 2), (2, 2)]
LENS = [LEN0]
for _k, _s in CONVS:
    LENS.append((LENS[-1] - _k) // _s + 1)
TOK = LENS[-1]
HT = 125
TP = 2 * HT
TILE_TOK = (HT, TOK - HT)
ROWS0 = 64
RUN0 = ROWS0 * S0
WIN = 3
WROWS = WIN + 1
WTAPS = WROWS * S0
COPIES = 6
WK = COPIES * WTAPS
WT = HT + 1
WGROUPS = ROWS0 // WIN + 1
XW = (WGROUPS - 1) * WIN * S0 + WTAPS
X_PART = (0, 0, 0, 1, 1, 2)
W_PART = (0, 1, 2, 0, 1, 0)

C = 192
CT = (128, 64)
HEADS = 12
D = C // HEADS
SLOT = 32
HG = P // SLOT
NG = HEADS // HG
ROW_MAX = D
LN_EPS = 1e-5
SC = 2 * HG


def blocks_of(n, size=500):
    return [(a, min(size, n - a)) for a in range(0, n, size)]


class Chain:

    def __init__(self, eng, sem, per, before=0, spare=None):
        self.eng, self.sem, self.per, self.before, self.n = eng, sem, per, before, 0
        self.base, self.spare = 0, spare

    def begin(self, it):
        self.base, self.n = it * self.per + self.before, 0

    def link(self, ins):
        self.n += 1
        ins.then_inc(self.sem, 1)
        self.eng.wait_ge(self.sem, self.base + self.n)

    def link_before_aggregate(self, ins):
        self.link(ins)
        self.eng.memset(self.spare, 0.0)

    def end(self):
        assert self.n == self.per, self.n


class Alloc:

    def __init__(self, nc, stack, tag, all_sems=None):
        self.nc, self.stack, self.tag = nc, stack, tag
        self.all_sems = all_sems
        if all_sems is None:
            self.all_sems = []
            stack.callback(self.clear)

    def clear(self):
        self.nc.clear_and_free_semaphores(self.all_sems)
        self.nc.all_engine_barrier()

    def sb(self, name, shape, dt=F32):
        return self.stack.enter_context(self.nc.sbuf_tensor(self.tag + name, shape, dt))

    def psum(self):
        return self.stack.enter_context(self.nc.psum_tensor(self.tag + "psum", [P, 8, BANK], F32))

    def sem(self, name):
        self.all_sems.append(self.nc.alloc_semaphore(name=self.tag + name))
        return self.all_sems[-1]

    def sems(self, *names):
        return [self.sem(n) for n in names]

    def of_lane(self, lane):
        return Alloc(self.nc, self.stack, f"{self.tag}{lane}_", self.all_sems)


class TokenizerLane:

    def __init__(self, a, ps):
        self.ps = ps
        sizes = [ROWS0 * HT] + LENS[1:-1] + [TP]
        self.h = [a.sb(f"h{i}", [CH, n]) for i, n in enumerate(sizes)]
        self.x = a.sb("x", [HT, XW])
        self.rest = a.sb("rest", [HT, XW])
        self.part = a.sb("part", [HT, 3, XW], BF16)
        self.win = a.sb("win", [HT, WGROUPS, WK], BF16)
        self.winT = a.sb("winT", [WK, WGROUPS, HT], BF16)
        self.stats = a.sb("stats", [CH, 16, 6])
        self.mv = a.sb("mv", [CH, 2])
        self.dev = a.sb("dev", [CH, 2])
        self.var = a.sb("var", [CH, 1])
        self.rstd = a.sb("rstd", [CH, 1])
        self.aff = a.sb("aff", [CH, 3])
        self.lnst = a.sb("lnst", [HT, 2, 6])
        self.lnmv = a.sb("lnmv", [HT, 2, 2])
        self.lnr = a.sb("lnr", [HT, 2])
        self.hx = a.sb("hx", [HT, 2, C])
        self.xn = a.sb("xn", [HT, 2, C])
        self.cm = a.sb("cm", [P, 2])
        self.zeroed, self.x_in, self.x_split = a.sems("zeroed", "x_in", "x_split")
        self.windows, self.window_t, self.conv = a.sems("windows", "window_t", "conv")
        self.evac, self.stats_in, self.gmean = a.sems("evac", "stats_in", "gmean")
        self.dev_in, self.gvar, self.var_in = a.sems("dev_in", "gvar", "var_in")
        self.rsqrt, self.normed, self.gelu = a.sems("rsqrt", "normed", "gelu")
        self.proj, self.ln_in, self.ln_rstd = a.sems("proj", "ln_in", "ln_rstd")
        self.xn_in, self.xn_t, self.cm_done = a.sems("xn_in", "xn_t", "cm_done")


def phase_tokenizer(nc, w, hres, gmax):
    chunks = []
    for layer, n in enumerate(LENS[1:], 1):
        chunks += [(layer, a, m) for a, m in blocks_of(n)]
    first_chunk = {l: min(i for i, c in enumerate(chunks) if c[0] == l) for l in range(1, 6)}
    n_chunks = {l: len(blocks_of(LENS[l])) for l in range(1, 6)}
    pieces = {}
    for l in range(5):
        ends = [min(2 * (a + m - 1) + CONVS[l][0], LENS[l]) for a, m in blocks_of(LENS[l + 1])]
        ends[-1] = LENS[l]
        pieces[l] = list(zip([0] + ends[:-1], ends))
    pieces[5] = [(0, TOK)]
    piece_at, n_pieces = {}, 0
    for l in range(6):
        piece_at[l] = n_pieces
        n_pieces += len(pieces[l])
    conv0 = []
    for v in range(WIN):
        groups = WGROUPS if v == 0 else WGROUPS - 1
        conv0 += [(v, g, min(4, groups - g)) for g in range(0, groups, 4)]
    window_banks = [(0, 8), (8, 8), (16, WGROUPS - 16)]
    n_evac = len(window_banks) + len(conv0) + len(chunks)
    at_conv0 = len(window_banks)
    at_convs = at_conv0 + len(conv0)

    n_conv = len(conv0) + len(chunks)
    stat_pieces = {l: blocks_of(LENS[l]) for l in range(6)}
    DVE_LINKS = 2 * (4 + 5 * 6 + 4)

    with ExitStack() as st:
        A = Alloc(nc, st, "tok_")
        psum = A.psum()
        w0_all = A.sb("w0_all", [WK, WIN * CH])
        w0_rest = A.sb("w0_rest", [WK, WIN * CH])
        w0_part = A.sb("w0_part", [WK, 3, WIN * CH], BF16)
        w0 = A.sb("w0", [WK, WIN * CH], BF16)
        cw = A.sb("cw", [CH, 14, CH])
        vecs = A.sb("vecs", [CH, 6, 3])
        pw = A.sb("pw", [CH, C])
        pb = A.sb("pb", [P, 2 * C])
        masks = A.sb("masks", [WK, 3])
        gavg = A.sb("gavg", [CH, CH])
        ident = A.sb("ident", [P, P])
        identb = A.sb("identb", [P, P], BF16)
        half = A.sb("half", [P, 1])
        spare = A.sb("spare", [1, 1])
        loaded, consts, parts, dve_chain = (A.sem(n) for n in ("loaded", "consts", "parts", "dve_chain"))
        L = [TokenizerLane(A.of_lane(lane), psum[:, lane * LANE_BANKS:(lane + 1) * LANE_BANKS, :]) for lane in LANES]
        block = st.enter_context(nc.Block())

        @block.sync
        def _(sp):
            for dst, src in ((w0_all[:], w["w0"]), (masks[:], w["w0_masks"]), (cw[:], w["cw"]),
                             (vecs[:], w["conv_vecs"]), (pw[:], w["pw"]), (pb[:], w["pb"]),
                             (gavg[:], w["gavg"]), (ident[:], w["ident"])):
                sp.dma_start(dst, src).then_inc(loaded, 16)
            for l in L:
                sp.wait_ge(l.zeroed, 2)
            with sp.Fori(0, PAIRS) as it:
                for lane, l in enumerate(L):
                    sp.wait_ge(l.x_split, it)
                    clip = it * len(LANES) + lane
                    src = w["x"][bass.ds(clip, 1), 0:SAMPLES]
                    body = bass.AP(src.tensor, src.offset, [[RUN0, HT - 1], [1, RUN0 + S0]])
                    tail = bass.AP(src.tensor, src.offset + RUN0 * (HT - 1), [[RUN0, 1], [1, RUN0]])
                    sp.dma_start(l.x[0:HT - 1, 0:RUN0 + S0], body).then_inc(l.x_in, 16)
                    sp.dma_start(l.x[HT - 1:HT, 0:RUN0], tail).then_inc(l.x_in, 16)

        @block.gpsimd
        def _(pool):
            pool.memset(half[:], -0.5).then_inc(consts, 1)
            pool.wait_ge(consts, 1)
            with pool.Fori(0, PAIRS) as it:
                for layer in range(6):
                    for l in L:
                        pool.wait_ge(l.var_in, it * 6 + layer + 1)
                        pool.tensor_tensor(l.rstd[:], l.var[:], half[0:CH, :], ALU.pow).then_inc(l.rsqrt, 1)
                for l in L:
                    pool.wait_ge(l.ln_in, it + 1)
                    pool.tensor_tensor(l.lnr[:], l.lnmv[:, :, 1], half[0:HT, :].to_broadcast([HT, 2]),
                                       ALU.pow).then_inc(l.ln_rstd, 1)

        @block.scalar
        def _(act):
            act.wait_ge(loaded, 8 * 16)
            with act.Fori(0, PAIRS) as it:
                for l in L:
                    for b, (g, n) in enumerate(window_banks):
                        act.wait_ge(l.window_t, it * 3 + b + 1)
                        src = l.ps[0:WK, b, :].bitcast(BF16)[:, 0:n * WT].rearrange("k (g t) -> k g t", t=WT)
                        act.activation(l.winT[:, g:g + n, :], src[:, :, 0:HT], ACT.Copy).then_inc(l.evac, 1)
                for l in L:
                    for i, (v, g, n) in enumerate(conv0):
                        act.wait_ge(l.conv, it * n_conv + i + 1)
                        dst = l.h[0][:].rearrange("c (p r) -> c r p", r=ROWS0)[
                            :, WIN * g + v:WIN * (g + n - 1) + v + 1:WIN, :]
                        act.activation(dst, l.ps[:, i % 4, 0:n * HT].rearrange("c (g p) -> c g p", p=HT),
                                       ACT.Identity, bias=vecs[:, 0, 0:1]).then_inc(l.evac, 1)
                for layer in range(6):
                    if layer:
                        for l in L:
                            for c in range(n_chunks[layer]):
                                k = first_chunk[layer] + c
                                _, a, m = chunks[k]
                                act.wait_ge(l.conv, it * n_conv + len(conv0) + k + 1)
                                act.activation(l.h[layer][:, a:a + m], l.ps[:, (len(conv0) + k) % 4, 0:m],
                                               ACT.Identity, bias=vecs[:, layer, 0:1]).then_inc(l.evac, 1)
                    for l in L:
                        act.wait_ge(l.normed, it * 6 + layer + 1)
                        for a, b in pieces[layer]:
                            act.activation(l.h[layer][:, a:b], l.h[layer][:, a:b], ACT.Gelu_apprx_tanh,
                                           bias=l.aff[:, 1:2], scale=l.aff[:, 0:1]).then_inc(l.gelu, 1)

        @block.tensor
        def _(pe):
            pe.wait_ge(loaded, 8 * 16)
            pe.wait_ge(parts, 2)

            def group_stats(it, layer):
                for l in L:
                    pe.wait_ge(l.stats_in, it * 6 + layer + 1)
                    pe.matmul(l.ps[:, 0, 0:1], gavg[:], l.mv[:, 0:1], start=True, stop=True).then_inc(l.gmean, 1)
                for l in L:
                    pe.wait_ge(l.dev_in, it * 6 + layer + 1)
                    pe.matmul(l.ps[:, 1, 0:1], gavg[:], l.dev[:, 1:2], start=True, stop=True).then_inc(l.gvar, 1)

            with pe.Fori(0, PAIRS) as it:
                for l in L:
                    pe.wait_ge(l.windows, it + 1)
                    pe.wait_ge(l.cm_done, it)
                    for b, (g0, n) in enumerate(window_banks):
                        bank = l.ps[0:WK, b, :].bitcast(BF16)
                        for g in range(n):
                            last = pe.transpose(bank[:, g * WT:g * WT + HT], l.win[:, g0 + g, :],
                                                identb[0:HT, 0:HT])
                        last.then_inc(l.window_t, 1)
                for l in L:
                    for i, (v, g, n) in enumerate(conv0):
                        pe.wait_ge(l.evac, it * n_evac + (at_conv0 if i < 4 else at_conv0 + i - 3))
                        pe.matmul(l.ps[:, i % 4, 0:n * HT], w0[:, v * CH:(v + 1) * CH],
                                  l.winT[:, g:g + n, :].rearrange("k g t -> k (g t)"),
                                  start=True, stop=True).then_inc(l.conv, 1)
                group_stats(it, 0)
                for layer in range(1, 6):
                    taps, stride = CONVS[layer - 1]
                    for l in L:
                        for c in range(n_chunks[layer]):
                            k = first_chunk[layer] + c
                            _, a, m = chunks[k]
                            i = len(conv0) + k
                            pe.wait_ge(l.evac, it * n_evac + at_conv0 + i - 3)
                            pe.wait_ge(l.gelu, it * n_pieces + piece_at[layer - 1] + c + 1)
                            for t in range(taps):
                                first = stride * a + t
                                rhs = l.h[layer - 1][:, first:first + stride * (m - 1) + 1:stride]
                                last = pe.matmul(l.ps[:, i % 4, 0:m], cw[:, 3 * (layer - 1) + t, :], rhs,
                                                 start=(t == 0), stop=(t == taps - 1))
                            last.then_inc(l.conv, 1)
                    group_stats(it, layer)
                for l in L:
                    pe.wait_ge(l.gelu, it * n_pieces + n_pieces)
                    for t in range(2):
                        last = pe.matmul(l.ps[0:HT, 2, t * C:(t + 1) * C], l.h[5][:, t * HT:(t + 1) * HT],
                                         pw[:], start=True, stop=True)
                    last.then_inc(l.proj, 1)
                for l in L:
                    pe.wait_ge(l.xn_in, it + 1)
                    for t in range(2):
                        for c, rows in enumerate(CT):
                            at = c * TP + t * HT
                            last = pe.transpose(l.ps[0:rows, 3, at:at + HT], l.xn[:, t, c * P:c * P + rows],
                                                ident[0:HT, 0:HT])
                    last.then_inc(l.xn_t, 1)

        @block.vector
        def _(dve):
            dve.memset(gmax[:], 0.0)
            for l in L:
                dve.memset(l.x[:, RUN0:XW], 0.0).then_inc(l.zeroed, 1)
                dve.memset(l.h[5][:, TOK:TP], 0.0).then_inc(l.zeroed, 1)
            dve.wait_ge(loaded, 8 * 16)
            pre = Chain(dve, dve_chain, 0)
            pre.link(dve.tensor_copy(w0_part[:, 0, :], w0_all[:]))
            pre.link(dve.tensor_tensor(w0_rest[:], w0_all[:], w0_part[:, 0, :], ALU.subtract))
            pre.link(dve.tensor_copy(w0_part[:, 1, :], w0_rest[:]))
            pre.link(dve.tensor_tensor(w0_all[:], w0_rest[:], w0_part[:, 1, :], ALU.subtract))
            pre.link(dve.tensor_copy(w0_part[:, 2, :], w0_all[:]))
            pre.link(dve.tensor_scalar(w0[:], w0_part[:, 0, :], masks[:, 0:1], None, ALU.mult))
            pre.link(dve.scalar_tensor_tensor(w0[:], w0_part[:, 1, :], masks[:, 1:2], w0[:], ALU.mult, ALU.add))
            dve.scalar_tensor_tensor(w0[:], w0_part[:, 2, :], masks[:, 2:3], w0[:], ALU.mult, ALU.add)\
               .then_inc(parts, 1)
            dve.tensor_copy(identb[:], ident[:]).then_inc(parts, 1)
            chain = Chain(dve, dve_chain, DVE_LINKS, pre.n, spare[:])

            def split_samples(it, l):
                dve.wait_ge(l.x_in, it * 32 + 32)
                dve.wait_ge(l.window_t, it * 3)
                chain.link(dve.tensor_copy(l.part[:, 0, :], l.x[:]))
                chain.link(dve.tensor_tensor(l.rest[:], l.x[:], l.part[:, 0, :], ALU.subtract))
                chain.link(dve.tensor_copy(l.part[:, 1, :], l.rest[:]))
                chain.link(dve.tensor_tensor(l.rest[:], l.rest[:], l.part[:, 1, :], ALU.subtract))
                dve.tensor_copy(l.part[:, 2, :], l.rest[:]).then_inc(l.x_split, 1)
                dve.wait_ge(l.x_split, it + 1)
                for c, part in enumerate(X_PART):
                    src = l.part[:, part, :]
                    src = bass.AP(src.tensor, src.offset, [list(src.ap[0]), [WIN * S0, WGROUPS], [1, WTAPS]])
                    last = dve.tensor_copy(l.win[:, :, c * WTAPS:(c + 1) * WTAPS], src)
                last.then_inc(l.windows, 1)

            def norm_stats(it, l, layer):
                done = at_conv0 + len(conv0) + sum(n_chunks[k] for k in range(1, layer + 1))
                for j, (a, m) in enumerate(stat_pieces[layer]):
                    dve.wait_ge(l.evac, it * n_evac + (done if layer == 0 else done - n_chunks[layer] + j + 1))
                    last = dve.bn_stats(l.stats[:, j, :], l.h[layer][:, a:a + m])
                chain.link_before_aggregate(last)
                dve.bn_aggr(l.mv[:], l.stats[:, 0:len(stat_pieces[layer]), :]).then_inc(l.stats_in, 1)

            def norm_deviation(it, l, layer):
                dve.wait_ge(l.gmean, it * 6 + layer + 1)
                dve.wait_ge(l.stats_in, it * 6 + layer + 1)
                chain.link(dve.tensor_tensor(l.dev[:, 0:1], l.mv[:, 0:1], l.ps[:, 0, 0:1], ALU.subtract))
                dve.scalar_tensor_tensor(l.dev[:, 1:2], l.dev[:, 0:1], l.dev[:, 0:1], l.mv[:, 1:2],
                                         ALU.mult, ALU.add).then_inc(l.dev_in, 1)

            def norm_variance(it, l, layer):
                dve.wait_ge(l.gvar, it * 6 + layer + 1)
                dve.tensor_scalar(l.var[:], l.ps[:, 1, 0:1], GN_EPS, None, ALU.add).then_inc(l.var_in, 1)
                chain.link(dve.tensor_copy(l.aff[:, 2:3], l.ps[:, 0, 0:1]))

            def norm_affine(it, l, layer):
                dve.wait_ge(l.rsqrt, it * 6 + layer + 1)
                chain.link(dve.tensor_tensor(l.aff[:, 0:1], l.rstd[:], vecs[:, layer, 1:2], ALU.mult))
                chain.link(dve.tensor_tensor(l.aff[:, 1:2], l.aff[:, 2:3], l.aff[:, 0:1], ALU.mult))
                dve.tensor_tensor(l.aff[:, 1:2], vecs[:, layer, 2:3], l.aff[:, 1:2], ALU.subtract)\
                   .then_inc(l.normed, 1)

            with dve.Fori(0, PAIRS) as it:
                chain.begin(it)
                for l in L:
                    split_samples(it, l)
                for layer in range(6):
                    for step in (norm_stats, norm_deviation, norm_variance, norm_affine):
                        for l in L:
                            step(it, l, layer)
                for lane, l in enumerate(L):
                    dve.wait_ge(l.proj, it + 1)
                    clip = it * len(LANES) + lane
                    dve.tensor_tensor(hres[:, bass.ds(clip, 1), :, :].rearrange("p b t c -> p (b t c)"),
                                      l.ps[0:HT, 2, 0:2 * C], pb[0:HT, :], ALU.add)
                    chain.link(dve.tensor_tensor(l.hx[:].rearrange("p t c -> p (t c)"), l.ps[0:HT, 2, 0:2 * C],
                                                 pb[0:HT, :], ALU.add))
                    for t in range(2):
                        last = dve.bn_stats(l.lnst[:, t, :], l.hx[:, t, :])
                    chain.link_before_aggregate(last)
                    for t in range(2):
                        last = dve.bn_aggr(l.lnmv[:, t, :], l.lnst[:, t, :])
                    chain.link(last)
                    dve.tensor_scalar(l.lnmv[:, :, 1], l.lnmv[:, :, 1], LN_EPS, None, ALU.add).then_inc(l.ln_in, 1)
                for l in L:
                    dve.wait_ge(l.ln_rstd, it + 1)
                    for t in range(2):
                        last = dve.tensor_scalar(l.xn[:, t, :], l.hx[:, t, :], l.lnmv[:, t, 0:1], l.lnr[:, t:t + 1],
                                                 ALU.subtract, ALU.mult)
                    last.then_inc(l.xn_in, 1)
                for l in L:
                    dve.wait_ge(l.xn_t, it + 1)
                    for c, rows in enumerate(CT):
                        last = dve.tensor_reduce(l.cm[0:rows, c:c + 1], l.ps[0:rows, 3, c * TP:c * TP + TOK],
                                                 AX_X, ALU.max, apply_absolute_value=True)
                    chain.link(last)
                    for c, rows in enumerate(CT):
                        last = dve.tensor_tensor(gmax[0:rows, c:c + 1], gmax[0:rows, c:c + 1],
                                                 l.cm[0:rows, c:c + 1], ALU.max)
                    last.then_inc(l.cm_done, 1)
                chain.end()


V_ONE = D


def pe_transpose_tokens(pe, l, src, ident, banks=(0, 1)):
    for t in range(2):
        for c, rows in enumerate(CT):
            last = pe.transpose(l.ps[0:rows, banks[c], t * HT:(t + 1) * HT], src[:, t, c * P:c * P + rows],
                                ident[0:HT, 0:HT])
    return last


def pe_project_padded(pe, l, wt, out_banks):
    for g in range(NG):
        for c, rows in enumerate(CT):
            b, at = out_banks[g]
            last = pe.matmul(l.ps[:, b, at:at + TP], wt[0:rows, c, g, :], l.xt[0:rows, c, :],
                             start=(c == 0), stop=(c == 1))
    return last


def pe_project_values(pe, l, wt, bank):
    for t in range(2):
        for c, rows in enumerate(CT):
            last = pe.matmul(l.ps[0:HT, bank, t * C:(t + 1) * C], l.xt[0:rows, c, t * HT:(t + 1) * HT],
                             wt[0:rows, c, :], start=(c == 0), stop=(c == 1))
    return last


def pe_scores(pe, l, g, q_tiles):
    for hq in range(HG):
        for t in range(q_tiles):
            last = pe.matmul(l.ps[0:HT, hq, t * TP:(t + 1) * TP], l.q[:, g, t * HT:(t + 1) * HT],
                             l.kpad[:, HG * g + hq, :], start=True, stop=True)
    return last


def pe_scores_t(pe, l, g):
    for hq in range(HG):
        for t in range(2):
            last = pe.matmul(l.ps[0:HT, hq, t * TP:(t + 1) * TP],
                             l.kpad[:, HG * g + hq, t * HT:(t + 1) * HT], l.q[:, g, :], start=True, stop=True)
    return last


def pe_shift_rows(pe, l, src, ident):
    for g in range(NG):
        for t in range(2):
            last = pe.matmul(l.ps[:, g, t * HT:(t + 1) * HT], src[:, g, t, :], ident[0:HT, 0:HT],
                             start=True, stop=True)
    return last


def pe_transpose_scores(pe, l, g, src, ident):
    for hq in range(HG):
        for t in range(2):
            for u in range(2):
                last = pe.transpose(l.ps[0:HT, hq, u * TP + t * HT:u * TP + (t + 1) * HT],
                                    src[:, g, hq, t, u * HT:(u + 1) * HT], ident[0:HT, 0:HT])
    return last


def pe_column_sums(pe, l, col, k):
    for g in range(NG):
        for t, n in enumerate(TILE_TOK):
            for hq in range(HG):
                h = HG * g + hq
                last = pe.matmul(l.ps[SLOT * hq:SLOT * (hq + 1), g, 0:TP],
                                 col[0:n, t, h:h + 1].to_broadcast([n, SLOT]), k[0:n, g, hq, t, :],
                                 start=(t == 0), stop=(t == 1), skip_group_check=True)
    return last


def pe_columns_to_rows(pe, l, col, ident, banks):
    for g in range(NG):
        b, at = banks[g]
        for t in range(2):
            for hq in range(HG):
                h = HG * g + hq
                last = pe.matmul(l.ps[SLOT * hq:SLOT * (hq + 1), b, at + t * HT:at + (t + 1) * HT],
                                 col[:, t, h:h + 1].to_broadcast([HT, SLOT]), ident[0:HT, 0:HT],
                                 start=True, stop=True, skip_group_check=True)
    return last


def act_group_exp(act, l, g, dst, shift, sums=None):
    for hq in range(HG):
        for t in range(2):
            h = HG * g + hq
            acc = {} if sums is None else {"accum_out": sums[:, t, h:h + 1]}
            last = act.activation(dst[:, g, hq, t, 0:TOK], l.ps[0:HT, hq, t * TP:t * TP + TOK], ACT.Exp,
                                  bias=shift[:, t, h:h + 1], **acc)
    return last


def dve_group_max(dve, l, g, dst):
    src = l.ps[0:HT, :, 0:2 * TP].rearrange("p q (t j) -> p t q j", t=2)[:, :, :, 0:TOK]
    return dve.tensor_reduce(dst[:, :, HG * g:HG * (g + 1)], src, AX_X, ALU.max, negate=True)


def dve_copy_group(dve, l, g, dst):
    return dve.tensor_copy(dst[:, g, :, :, :].rearrange("p q t i -> p q (t i)"), l.ps[0:HT, :, 0:2 * TP])


def act_copy_group(act, l, g, dst):
    return act.activation(dst[:, g, :, :, :].rearrange("p q t i -> p q (t i)"), l.ps[0:HT, :, 0:2 * TP], ACT.Copy)


BANKS_ROWS = ((1, 0), (1, TP), (2, 0))


def act_rows(act, l, dst):
    act.activation(dst[:, 0:2, :], l.ps[:, 1, 0:2 * TP].rearrange("p (g i) -> p g i", g=2), ACT.Copy)
    return act.activation(dst[:, 2, :], l.ps[:, 2, 0:TP], ACT.Copy)


def pe_weighted_sum(pe, l, vals, e, width=TP):
    for g in range(NG):
        for t, keys in enumerate(TILE_TOK):
            for hq in range(HG):
                last = pe.matmul(l.ps[SLOT * hq:SLOT * (hq + 1), g, 0:width], vals[0:keys, t, HG * g + hq, :],
                                 e[0:keys, g, hq, t, :], start=(t == 0), stop=(t == 1), skip_group_check=True)
    return last


def pe_project_back(pe, l, ctx, wt, bank):
    for t in range(2):
        for g in range(NG):
            last = pe.matmul(l.ps[0:HT, bank, t * C:(t + 1) * C], ctx[:, g, t * HT:(t + 1) * HT], wt[:, g, :],
                             start=(g == 0), stop=(g == NG - 1))
    return last


def dve_read_pair(dve, L, hres, it):
    for lane, l in enumerate(L):
        clip = it * len(LANES) + lane
        last = dve.tensor_copy(l.h[:].rearrange("p t c -> p (t c)"),
                               hres[:, bass.ds(clip, 1), :, :].rearrange("p b t c -> p (b t c)"))
    return last


def dve_norm_stats(dve, chain, l, src, eps, sem):
    for t in range(2):
        last = dve.bn_stats(l.lnst[:, t, :], src[:, t, :])
    chain.link_before_aggregate(last)
    for t in range(2):
        last = dve.bn_aggr(l.lnmv[:, t, :], l.lnst[:, t, :])
    chain.link(last)
    dve.tensor_scalar(l.lnmv[:, :, 1], l.lnmv[:, :, 1], eps, None, ALU.add).then_inc(sem, 1)


def dve_norm_apply(dve, l, dst, src):
    for t in range(2):
        last = dve.tensor_scalar(dst[:, t, :], src[:, t, :], l.lnmv[:, t, 0:1], l.lnr[:, t:t + 1],
                                 ALU.subtract, ALU.mult)
    return last


def pool_rstd(pool, l, half):
    return pool.tensor_tensor(l.lnr[:], l.lnmv[:, :, 1], half[0:HT, 0:1].to_broadcast([HT, 2]), ALU.pow)


def act_keys(act, l, bias, banks):
    for g in range(NG):
        b, at = banks[g]
        for hq in range(HG):
            rows = slice(SLOT * hq, SLOT * (hq + 1))
            last = act.activation(l.kpad[rows, HG * g + hq, :], l.ps[rows, b, at:at + TP], ACT.Identity,
                                  bias=bias[rows, g:g + 1])
    return last


def dve_queries(dve, l, bias, banks, scale):
    for g in range(NG):
        b, at = banks[g]
        last = dve.tensor_scalar(l.q[:, g, :], l.ps[:, b, at:at + TP], scale, bias[:, g:g + 1], ALU.mult, ALU.add)
    return last


def dve_values(dve, l, bias, bank):
    return dve.tensor_tensor(l.v[:, :, :, 0:D],
                             l.ps[0:HT, bank, 0:2 * C].rearrange("p (t h d) -> p t h d", t=2, d=D),
                             bias[0:HT, :].rearrange("p (t h d) -> p t h d", t=2, d=D), ALU.add)


def dve_score_max(dve, l, g, dst, row, n=TOK):
    src = l.ps[0:HT, :, 0:2 * TP].rearrange("p q (t j) -> p q t j", t=2)[:, :, :, 0:n]
    out = dst[:, g, :, :].rearrange("p t (q s) -> p q t s", s=SLOT)[:, :, :, row]
    return dve.tensor_reduce(out, src, AX_X, ALU.max, negate=True)


def load_all(sp, pairs, sem):
    for dst, src in pairs:
        sp.dma_start(dst, src).then_inc(sem, 16)


BANKS_Q = ((2, 0), (2, TP), (3, 0))
BANKS_K = ((0, 0), (0, TP), (1, 0))
ALPHA = 0.35


class AttentionLane:

    def __init__(self, a, ps):
        self.ps = ps
        self.h = a.sb("h", [HT, 2, C])
        self.lnst = a.sb("lnst", [HT, 2, 6])
        self.lnmv = a.sb("lnmv", [HT, 2, 2])
        self.lnr = a.sb("lnr", [HT, 2])
        self.xn = a.sb("xn", [HT, 2, C])
        self.xt = a.sb("xt", [P, 2, TP])
        self.q = a.sb("q", [P, NG, TP])
        self.kpad = a.sb("kpad", [P, HEADS, TP])
        self.v = a.sb("v", [HT, 2, HEADS, SLOT])
        self.neg = a.sb("neg", [HT, 2, HEADS])
        self.den = a.sb("den", [HT, 2, HEADS])
        self.eq = a.sb("eq", [HT, NG, HG, 2, TP])
        self.e = a.sb("e", [HT, NG, HG, 2, TP])
        self.ctx = a.sb("ctx", [P, NG, TP])
        self.rden = a.sb("rden", [P, NG, TP])
        self.ln_in, self.ln_rstd, self.xn_in = a.sems("ln_in", "ln_rstd", "xn_in")
        self.xn_t, self.xt_in, self.q_out = a.sems("xn_t", "xt_in", "q_out")
        self.k_out, self.v_out, self.q_in = a.sems("k_out", "v_out", "q_in")
        self.k_in, self.v_in, self.s_out = a.sems("k_in", "v_in", "s_out")
        self.s_max, self.eq_in, self.e_out = a.sems("s_max", "eq_in", "e_out")
        self.e_in, self.den_in, self.den_out = a.sems("e_in", "den_in", "den_out")
        self.rden_in, self.pv_out, self.ctx_in = a.sems("rden_in", "pv_out", "ctx_in")
        self.proj_out, self.zeroed, self.h_done = a.sems("proj_out", "zeroed", "h_done")


def phase_attention(nc, w, hres, gmax):
    DVE_LINKS = 1 + 2 * 2
    with ExitStack() as st:
        A = Alloc(nc, st, "att_")
        psum = A.psum()
        wq, wk = (A.sb(n, [P, 2, NG, P]) for n in ("wq", "wk"))
        wv = A.sb("wv", [P, 2, C])
        wo = A.sb("wo", [P, NG, C])
        vb = A.sb("vb", [P, 2 * C])
        qb, kb = A.sb("qb", [P, NG]), A.sb("kb", [P, NG])
        ident = A.sb("ident", [P, P])
        spare = A.sb("spare", [1, 1])
        half = A.sb("half", [P, 1])
        expo = A.sb("expo", [P, 2])
        wmax = A.sb("wmax", [P, 2, 3])
        cs = A.sb("cs", [P, 2, 6])
        inv_cs = A.sb("inv_cs", [P, 2])
        loaded, consts, ready, dve_chain, wmax_in, ratio_in = (
            A.sem(n) for n in ("loaded", "consts", "ready", "dve_chain", "wmax_in", "ratio_in"))
        L = [AttentionLane(A.of_lane(lane), psum[:, lane * LANE_BANKS:(lane + 1) * LANE_BANKS, :]) for lane in LANES]
        block = st.enter_context(nc.Block())

        @block.sync
        def _(sp):
            load_all(sp, ((wq[:], w["a_wq"]), (wk[:], w["a_wk"]), (wv[:], w["a_wv"]), (wo[:], w["a_wo"]),
                          (vb[:], w["a_vb"]), (qb[:], w["a_qb"]), (kb[:], w["a_kb"]),
                          (ident[:], w["ident"])), loaded)

        @block.gpsimd
        def _(pool):
            pool.memset(half[:], -0.5).then_inc(consts, 1)
            pool.memset(expo[:, 0:1], ALPHA).then_inc(consts, 1)
            pool.memset(expo[:, 1:2], 1.0 - ALPHA).then_inc(consts, 1)
            pool.wait_ge(consts, 3)
            pool.wait_ge(wmax_in, 2)
            for c, n in enumerate(CT):
                pool.tensor_tensor(cs[0:n, c, 0:1], gmax[0:n, c:c + 1], expo[0:n, 0:1], ALU.pow).then_inc(ratio_in, 1)
                pool.tensor_tensor(cs[0:n, c, 1:2], wmax[0:n, c, 2:3], expo[0:n, 1:2], ALU.pow).then_inc(ratio_in, 1)
            with pool.Fori(0, PAIRS) as it:
                for l in L:
                    pool.wait_ge(l.ln_in, it + 1)
                    pool_rstd(pool, l, half).then_inc(l.ln_rstd, 1)

        @block.tensor
        def _(pe):
            pe.wait_ge(loaded, 8 * 16)
            pe.wait_ge(ready, 2)
            for l in L:
                pe.wait_ge(l.zeroed, 4)
            with pe.Fori(0, PAIRS) as it:
                for l in L:
                    pe.wait_ge(l.xn_in, it + 1)
                    pe.wait_ge(l.h_done, it)
                    pe_transpose_tokens(pe, l, l.xn, ident).then_inc(l.xn_t, 1)
                for l in L:
                    pe.wait_ge(l.xt_in, it * 2 + 2)
                    pe_project_padded(pe, l, wq, BANKS_Q).then_inc(l.q_out, 1)
                    pe_project_padded(pe, l, wk, BANKS_K).then_inc(l.k_out, 1)
                for l in L:
                    pe.wait_ge(l.q_in, it + 1)
                    pe_project_values(pe, l, wv, 2).then_inc(l.v_out, 1)
                for g in range(NG):
                    for l in L:
                        if g == 0:
                            pe.wait_ge(l.k_in, it + 1)
                            pe.wait_ge(l.v_in, it + 1)
                        else:
                            pe.wait_ge(l.eq_in, it * NG + g)
                        pe_scores(pe, l, g, 2).then_inc(l.s_out, 1)
                for g in range(NG):
                    for l in L:
                        pe.wait_ge(l.eq_in, it * NG + NG)
                        if g:
                            pe.wait_ge(l.e_in, it * NG + g)
                        pe_transpose_scores(pe, l, g, l.eq, ident).then_inc(l.e_out, 1)
                for l in L:
                    pe.wait_ge(l.den_in, it + 1)
                    pe.wait_ge(l.e_in, it * NG + NG)
                    pe_columns_to_rows(pe, l, l.den, ident, BANKS_ROWS).then_inc(l.den_out, 1)
                for l in L:
                    pe.wait_ge(l.rden_in, it + 1)
                    pe_weighted_sum(pe, l, l.v, l.e).then_inc(l.pv_out, 1)
                for l in L:
                    pe.wait_ge(l.ctx_in, it + 1)
                    pe_project_back(pe, l, l.ctx, wo, 3).then_inc(l.proj_out, 1)

        @block.scalar
        def _(act):
            act.wait_ge(ready, 2)
            for l in L:
                act.wait_ge(l.zeroed, 4)
            with act.Fori(0, PAIRS) as it:
                for l in L:
                    act.wait_ge(l.xn_t, it + 1)
                    for c, n in enumerate(CT):
                        act.activation(l.xt[0:n, c, :], l.ps[0:n, c, 0:TP], ACT.Copy, scale=inv_cs[0:n, c:c + 1])\
                           .then_inc(l.xt_in, 1)
                for l in L:
                    act.wait_ge(l.k_out, it + 1)
                    act_keys(act, l, kb, BANKS_K).then_inc(l.k_in, 1)
                for g in range(NG):
                    for l in L:
                        act.wait_ge(l.s_max, it * NG + g + 1)
                        act_group_exp(act, l, g, l.eq, l.neg, l.den).then_inc(l.eq_in, 1)
                for l in L:
                    for g in range(1, NG):
                        act.wait_ge(l.e_out, it * NG + g + 1)
                        act_copy_group(act, l, g, l.e).then_inc(l.e_in, 1)
                for l in L:
                    act.wait_ge(l.den_out, it + 1)
                    act_rows(act, l, l.rden).then_inc(l.rden_in, 1)

        @block.vector
        def _(dve):
            for l in L:
                dve.memset(l.kpad[:], 0.0).then_inc(l.zeroed, 1)
                dve.memset(l.eq[:, :, :, :, TOK:TP], 1.0).then_inc(l.zeroed, 1)
                dve.memset(l.v[:, :, :, D + 1:SLOT], 0.0).then_inc(l.zeroed, 1)
                dve.memset(l.v[:, :, :, V_ONE], 1.0).then_inc(l.zeroed, 1)
            dve.wait_ge(loaded, 8 * 16)
            pre = Chain(dve, dve_chain, 0)
            for c, n in enumerate(CT):
                for j, part in enumerate((wq[0:n, c, :, :].rearrange("p g m -> p (g m)"),
                                          wk[0:n, c, :, :].rearrange("p g m -> p (g m)"), wv[0:n, c, :])):
                    last = dve.tensor_reduce(wmax[0:n, c, j:j + 1], part, AX_X, ALU.max, apply_absolute_value=True)
                pre.link(last)
                pre.link(dve.tensor_tensor(wmax[0:n, c, 0:1], wmax[0:n, c, 0:1], wmax[0:n, c, 1:2], ALU.max))
                dve.tensor_tensor(wmax[0:n, c, 2:3], wmax[0:n, c, 2:3], wmax[0:n, c, 0:1], ALU.max).then_inc(wmax_in, 1)
            dve.wait_ge(ratio_in, 4)
            for c, n in enumerate(CT):
                r = lambda j: cs[0:n, c, j:j + 1]
                pre.link(dve.reciprocal(r(1), r(1)))
                pre.link(dve.tensor_tensor(r(0), r(0), r(1), ALU.mult))
                pre.link(dve.tensor_scalar(r(2).bitcast(U32), r(0).bitcast(U32), 0x7F800000, None, ALU.bitwise_and))
                pre.link(dve.tensor_tensor(r(3), r(0), r(2), ALU.subtract))
                pre.link(dve.scalar_tensor_tensor(r(4), r(2), 2.0, r(0), ALU.mult, ALU.subtract))
                pre.link(dve.tensor_tensor(r(5), r(3), r(4), ALU.is_gt))
                pre.link(dve.scalar_tensor_tensor(r(3), r(5), 1.0, r(2), ALU.add, ALU.mult))
                for part in (wq[0:n, c, :, :].rearrange("p g m -> p (g m)"),
                             wk[0:n, c, :, :].rearrange("p g m -> p (g m)"), wv[0:n, c, :]):
                    last = dve.tensor_scalar(part, part, r(3), None, ALU.mult)
                pre.link(dve.reciprocal(inv_cs[0:n, c:c + 1], r(3)))
            dve.tensor_scalar(qb[:], qb[:], D ** -0.5, None, ALU.mult).then_inc(ready, 2)
            dve.wait_ge(ready, 2)
            chain = Chain(dve, dve_chain, DVE_LINKS, pre.n, spare[:])
            with dve.Fori(0, PAIRS) as it:
                chain.begin(it)
                chain.link(dve_read_pair(dve, L, hres, it))
                for l in L:
                    dve_norm_stats(dve, chain, l, l.h, LN_EPS, l.ln_in)
                for l in L:
                    dve.wait_ge(l.ln_rstd, it + 1)
                    dve_norm_apply(dve, l, l.xn, l.h).then_inc(l.xn_in, 1)
                for l in L:
                    dve.wait_ge(l.q_out, it + 1)
                    dve_queries(dve, l, qb, BANKS_Q, D ** -0.5).then_inc(l.q_in, 1)
                for l in L:
                    dve.wait_ge(l.v_out, it + 1)
                    dve_values(dve, l, vb, 2).then_inc(l.v_in, 1)
                for g in range(NG):
                    for l in L:
                        dve.wait_ge(l.s_out, it * NG + g + 1)
                        dve_group_max(dve, l, g, l.neg).then_inc(l.s_max, 1)
                for l in L:
                    dve.wait_ge(l.e_out, it * NG + 1)
                    dve_copy_group(dve, l, 0, l.e).then_inc(l.e_in, 1)
                    dve.wait_ge(l.eq_in, it * NG + NG)
                    dve.reciprocal(l.den[:], l.den[:]).then_inc(l.den_in, 1)
                for l in L:
                    dve.wait_ge(l.pv_out, it + 1)
                    dve.wait_ge(l.rden_in, it + 1)
                    dve.tensor_tensor(l.ctx[:], l.ps[:, 0:NG, 0:TP], l.rden[:], ALU.mult).then_inc(l.ctx_in, 1)
                for lane, l in enumerate(L):
                    dve.wait_ge(l.proj_out, it + 1)
                    clip = it * len(LANES) + lane
                    dve.tensor_tensor(hres[:, bass.ds(clip, 1), :, :].rearrange("p b t c -> p (b t c)"),
                                      l.h[:].rearrange("p t c -> p (t c)"), l.ps[0:HT, 3, 0:2 * C],
                                      ALU.add).then_inc(l.h_done, 1)
                for l in L:
                    dve.wait_ge(l.h_done, it + 1)
                chain.end()


EXPERTS = 8
SLOTS = 32
L2_EPS = 1e-6


class MixtureLane:

    def __init__(self, a, ps):
        self.ps = ps
        self.h = a.sb("h", [HT, 2, C])
        self.lnst = a.sb("lnst", [HT, 2, 6])
        self.lnmv = a.sb("lnmv", [HT, 2, 2])
        self.lnr = a.sb("lnr", [HT, 2])
        self.xn = a.sb("xn", [HT, 2, C])
        self.xt = a.sb("xt", [P, 2, TP])
        self.sq = a.sb("sq", [HT, 2, C])
        self.nsq = a.sb("nsq", [HT, 2])
        self.nrm = a.sb("nrm", [HT, 2])
        self.cmax = a.sb("cmax", [HT, 2])
        self.csum = a.sb("csum", [HT, 2])
        self.comb = a.sb("comb", [HT, 2, SLOTS])
        self.dmax = a.sb("dmax", [SLOTS, 1])
        self.dsum = a.sb("dsum", [SLOTS, 1])
        self.disp = a.sb("disp", [SLOTS, TP])
        self.combT = a.sb("combT", [SLOTS, TP])
        self.dispT = a.sb("dispT", [HT, 2, SLOTS])
        self.xs = a.sb("xs", [P, 2, SLOTS])
        self.hid = a.sb("hid", [SLOTS, C])
        self.hidT = a.sb("hidT", [P, 2, SLOTS])
        self.ys = a.sb("ys", [SLOTS, C])
        self.ln_in, self.ln_rstd, self.squares_in = a.sems("ln_in", "ln_rstd", "squares_in")
        self.norm_in, self.xn_in, self.xn_t = a.sems("norm_in", "xn_in", "xn_t")
        self.xt_in, self.logits, self.maxima = a.sems("xt_in", "logits", "maxima")
        self.exps, self.weights, self.weights_t = a.sems("exps", "weights", "weights_t")
        self.combT_in, self.dispT_in, self.slots_out = a.sems("combT_in", "dispT_in", "slots_out")
        self.xs_in, self.hid_out, self.hid_in = a.sems("xs_in", "hid_out", "hid_in")
        self.gelu_in, self.own_in, self.own_t = a.sems("gelu_in", "own_in", "own_t")
        self.hidT_in, self.ys_out, self.ys_in = a.sems("hidT_in", "ys_out", "ys_in")
        self.y_out, self.zeroed, self.h_done = a.sems("y_out", "zeroed", "h_done")


def phase_mixture(nc, w, hres):
    DVE_LINKS = 1 + 2 * 6
    with ExitStack() as st:
        A = Alloc(nc, st, "mix_")
        psum = A.psum()
        sp_w = A.sb("slots", [P, 2, SLOTS])
        sq_w = A.sb("slots_sq", [P, 2, SLOTS])
        nrm_w = A.sb("slots_norm", [P, 2, SLOTS // EXPERTS])
        scale = A.sb("scale", [P, 1])
        wd, wu = A.sb("wd", [P, 2, C]), A.sb("wu", [P, 2, C])
        bd, bu, own = (A.sb(n, [SLOTS, C]) for n in ("bd", "bu", "own"))
        ident = A.sb("ident", [P, P])
        spare = A.sb("spare", [1, 1])
        half = A.sb("half", [P, SLOTS + 1])
        loaded, consts, dve_chain, sums_in, roots, slots_in = (
            A.sem(n) for n in ("loaded", "consts", "dve_chain", "sums_in", "roots", "slots_in"))
        L = [MixtureLane(A.of_lane(lane), psum[:, lane * LANE_BANKS:(lane + 1) * LANE_BANKS, :]) for lane in LANES]
        block = st.enter_context(nc.Block())

        @block.sync
        def _(sp):
            load_all(sp, ((sp_w[:], w["m_slots"]), (scale[:], w["m_scale"]), (wd[:], w["m_wd"]),
                          (wu[:], w["m_wu"]), (bd[:], w["m_bd"]), (bu[:], w["m_bu"]), (own[:], w["m_own"]),
                          (ident[:], w["ident"])), loaded)

        @block.gpsimd
        def _(pool):
            pool.memset(half[:, 0:SLOTS], 0.5).then_inc(consts, 1)
            pool.memset(half[:, SLOTS:SLOTS + 1], -0.5).then_inc(consts, 1)
            pool.wait_ge(consts, 2)
            pool.wait_ge(sums_in, 1)
            nrm = nrm_w[:].rearrange("d c p -> d (c p)")
            pool.tensor_tensor(nrm, nrm, half[:, 0:2 * (SLOTS // EXPERTS)], ALU.pow).then_inc(roots, 1)
            with pool.Fori(0, PAIRS) as it:
                for l in L:
                    pool.wait_ge(l.ln_in, it + 1)
                    pool_rstd(pool, l, half[:, SLOTS:SLOTS + 1]).then_inc(l.ln_rstd, 1)
                for l in L:
                    pool.wait_ge(l.squares_in, it + 1)
                    pool.tensor_tensor(l.nrm[:], l.nsq[:], half[0:HT, 0:2], ALU.pow).then_inc(l.norm_in, 1)

        @block.tensor
        def _(pe):
            pe.wait_ge(loaded, 8 * 16)
            pe.wait_ge(slots_in, 1)
            for l in L:
                pe.wait_ge(l.zeroed, 1)
            with pe.Fori(0, PAIRS) as it:
                for l in L:
                    pe.wait_ge(l.xn_in, it + 1)
                    pe.wait_ge(l.h_done, it)
                    pe_transpose_tokens(pe, l, l.xn, ident).then_inc(l.xn_t, 1)
                for l in L:
                    pe.wait_ge(l.xt_in, it * 2 + 2)
                    for t in range(2):
                        for c, n in enumerate(CT):
                            pe.matmul(l.ps[0:HT, 2, t * SLOTS:(t + 1) * SLOTS], l.xt[0:n, c, t * HT:(t + 1) * HT],
                                      sp_w[0:n, c, :], start=(c == 0), stop=(c == 1))
                    for c, n in enumerate(CT):
                        last = pe.matmul(l.ps[0:SLOTS, 3, 0:TP], sp_w[0:n, c, :], l.xt[0:n, c, :],
                                         start=(c == 0), stop=(c == 1))
                    last.then_inc(l.logits, 1)
                for l in L:
                    pe.wait_ge(l.weights, it * 2 + 2)
                    for t in range(2):
                        pe.transpose(l.ps[0:SLOTS, 0, t * HT:(t + 1) * HT], l.comb[:, t, :], ident[0:HT, 0:HT])
                    for t in range(2):
                        last = pe.transpose(l.ps[0:HT, 1, t * SLOTS:(t + 1) * SLOTS], l.disp[:, t * HT:(t + 1) * HT],
                                            ident[0:SLOTS, 0:SLOTS])
                    last.then_inc(l.weights_t, 1)
                for l in L:
                    pe.wait_ge(l.dispT_in, it + 1)
                    for c, n in enumerate(CT):
                        for t, keys in enumerate(TILE_TOK):
                            last = pe.matmul(l.ps[0:n, 2, c * SLOTS:(c + 1) * SLOTS], l.xn[0:keys, t, c * P:c * P + n],
                                             l.dispT[0:keys, t, :], start=(t == 0), stop=(t == 1))
                    last.then_inc(l.slots_out, 1)
                for l in L:
                    pe.wait_ge(l.xs_in, it * 2 + 2)
                    for c, n in enumerate(CT):
                        last = pe.matmul(l.ps[0:SLOTS, 3, 0:C], l.xs[0:n, c, :], wd[0:n, c, :],
                                         start=(c == 0), stop=(c == 1))
                    last.then_inc(l.hid_out, 1)
                for l in L:
                    pe.wait_ge(l.own_in, it + 1)
                    pe.wait_ge(l.combT_in, it + 1)
                    for c, n in enumerate(CT):
                        last = pe.matmul(l.ps[0:n, 0, c * SLOTS:(c + 1) * SLOTS], l.hid[:, c * P:c * P + n],
                                         ident[0:SLOTS, 0:SLOTS], start=True, stop=True)
                    last.then_inc(l.own_t, 1)
                for l in L:
                    pe.wait_ge(l.hidT_in, it * 2 + 2)
                    for c, n in enumerate(CT):
                        last = pe.matmul(l.ps[0:SLOTS, 1, 0:C], l.hidT[0:n, c, :], wu[0:n, c, :],
                                         start=(c == 0), stop=(c == 1))
                    last.then_inc(l.ys_out, 1)
                for l in L:
                    pe.wait_ge(l.ys_in, it + 1)
                    for t in range(2):
                        last = pe.matmul(l.ps[0:HT, 2, t * C:(t + 1) * C], l.combT[:, t * HT:(t + 1) * HT], l.ys[:],
                                         start=True, stop=True)
                    last.then_inc(l.y_out, 1)

        @block.scalar
        def _(act):
            with act.Fori(0, PAIRS) as it:
                for l in L:
                    act.wait_ge(l.xn_t, it + 1)
                    for c, n in enumerate(CT):
                        act.activation(l.xt[0:n, c, :], l.ps[0:n, c, 0:TP], ACT.Copy).then_inc(l.xt_in, 1)
                for l in L:
                    act.wait_ge(l.maxima, it * 2 + 2)
                    for t in range(2):
                        act.activation(l.comb[:, t, :], l.ps[0:HT, 2, t * SLOTS:(t + 1) * SLOTS], ACT.Exp,
                                       bias=l.cmax[:, t:t + 1], accum_out=l.csum[:, t:t + 1]).then_inc(l.exps, 1)
                    act.activation(l.disp[:, 0:TOK], l.ps[0:SLOTS, 3, 0:TOK], ACT.Exp, bias=l.dmax[:, 0:1],
                                   accum_out=l.dsum[:, 0:1]).then_inc(l.exps, 1)
                for l in L:
                    act.wait_ge(l.weights_t, it + 1)
                    act.activation(l.combT[:], l.ps[0:SLOTS, 0, 0:TP], ACT.Copy).then_inc(l.combT_in, 1)
                for l in L:
                    act.wait_ge(l.slots_out, it + 1)
                    for c, n in enumerate(CT):
                        act.activation(l.xs[0:n, c, :], l.ps[0:n, 2, c * SLOTS:(c + 1) * SLOTS], ACT.Copy)\
                           .then_inc(l.xs_in, 1)
                for l in L:
                    act.wait_ge(l.hid_in, it + 1)
                    act.activation(l.hid[:], l.hid[:], ACT.Gelu).then_inc(l.gelu_in, 1)
                for l in L:
                    act.wait_ge(l.own_t, it + 1)
                    for c, n in enumerate(CT):
                        act.activation(l.hidT[0:n, c, :], l.ps[0:n, 0, c * SLOTS:(c + 1) * SLOTS], ACT.Copy)\
                           .then_inc(l.hidT_in, 1)

        @block.vector
        def _(dve):
            for l in L:
                dve.memset(l.disp[:, TOK:TP], 0.0).then_inc(l.zeroed, 1)
            dve.wait_ge(loaded, 8 * 16)
            pre = Chain(dve, dve_chain, 0)
            pre.link(dve.tensor_tensor(sq_w[:], sp_w[:], sp_w[:], ALU.mult))
            dve.tensor_reduce(nrm_w[:], sq_w[:].rearrange("d c (n p) -> d c p n", n=EXPERTS), AX_X, ALU.add)\
               .then_inc(sums_in, 1)
            dve.wait_ge(roots, 1)
            pre.link(dve.tensor_scalar(nrm_w[:], nrm_w[:], L2_EPS, None, ALU.add))
            pre.link(dve.reciprocal(nrm_w[:], nrm_w[:]))
            for n in range(EXPERTS):
                at = slice(n * (SLOTS // EXPERTS), (n + 1) * (SLOTS // EXPERTS))
                last = dve.tensor_tensor(sp_w[:, :, at], sp_w[:, :, at], nrm_w[:], ALU.mult)
            pre.link(last)
            dve.tensor_scalar(sp_w[:], sp_w[:], scale[:, 0:1], None, ALU.mult).then_inc(slots_in, 1)
            chain = Chain(dve, dve_chain, DVE_LINKS, pre.n, spare[:])
            with dve.Fori(0, PAIRS) as it:
                chain.begin(it)
                chain.link(dve_read_pair(dve, L, hres, it))
                for l in L:
                    dve_norm_stats(dve, chain, l, l.h, LN_EPS, l.ln_in)
                for l in L:
                    dve.wait_ge(l.ln_rstd, it + 1)
                    chain.link(dve_norm_apply(dve, l, l.xn, l.h))
                    for t in range(2):
                        last = dve.tensor_tensor_reduce(l.sq[:, t, :], l.xn[:, t, :], l.xn[:, t, :], 1.0, 0.0, ALU.mult,
                                                        ALU.add, l.nsq[:, t:t + 1])
                    last.then_inc(l.squares_in, 1)
                for l in L:
                    dve.wait_ge(l.norm_in, it + 1)
                    chain.link(dve.tensor_scalar(l.nrm[:], l.nrm[:], L2_EPS, None, ALU.add))
                    chain.link(dve.reciprocal(l.nrm[:], l.nrm[:]))
                    for t in range(2):
                        last = dve.tensor_scalar(l.xn[:, t, :], l.xn[:, t, :], l.nrm[:, t:t + 1], None, ALU.mult)
                    last.then_inc(l.xn_in, 1)
                for l in L:
                    dve.wait_ge(l.logits, it + 1)
                    dve.tensor_reduce(l.cmax[:], l.ps[0:HT, 2, 0:2 * SLOTS].rearrange("p (t s) -> p t s", t=2),
                                      AX_X, ALU.max, negate=True).then_inc(l.maxima, 1)
                    dve.tensor_reduce(l.dmax[:], l.ps[0:SLOTS, 3, 0:TOK], AX_X, ALU.max, negate=True)\
                       .then_inc(l.maxima, 1)
                for l in L:
                    dve.wait_ge(l.exps, it * 3 + 3)
                    dve.reciprocal(l.csum[:], l.csum[:])
                    chain.link(dve.reciprocal(l.dsum[:], l.dsum[:]))
                    for t in range(2):
                        last = dve.tensor_scalar(l.comb[:, t, :], l.comb[:, t, :], l.csum[:, t:t + 1], None, ALU.mult)
                    last.then_inc(l.weights, 1)
                    dve.tensor_scalar(l.disp[:, 0:TOK], l.disp[:, 0:TOK], l.dsum[:, 0:1], None, ALU.mult)\
                       .then_inc(l.weights, 1)
                for l in L:
                    dve.wait_ge(l.weights_t, it + 1)
                    dve.tensor_copy(l.dispT[:].rearrange("p t s -> p (t s)"), l.ps[0:HT, 1, 0:2 * SLOTS])\
                       .then_inc(l.dispT_in, 1)
                for l in L:
                    dve.wait_ge(l.hid_out, it + 1)
                    dve.tensor_tensor(l.hid[:], l.ps[0:SLOTS, 3, 0:C], bd[:], ALU.add).then_inc(l.hid_in, 1)
                for l in L:
                    dve.wait_ge(l.gelu_in, it + 1)
                    dve.tensor_tensor(l.hid[:], l.hid[:], own[:], ALU.mult).then_inc(l.own_in, 1)
                for l in L:
                    dve.wait_ge(l.ys_out, it + 1)
                    dve.tensor_tensor(l.ys[:], l.ps[0:SLOTS, 1, 0:C], bu[:], ALU.add).then_inc(l.ys_in, 1)
                for lane, l in enumerate(L):
                    dve.wait_ge(l.y_out, it + 1)
                    clip = it * len(LANES) + lane
                    dve.tensor_tensor(hres[:, bass.ds(clip, 1), :, :].rearrange("p b t c -> p (b t c)"),
                                      l.h[:].rearrange("p t c -> p (t c)"), l.ps[0:HT, 2, 0:2 * C],
                                      ALU.add).then_inc(l.h_done, 1)
                for l in L:
                    dve.wait_ge(l.h_done, it + 1)
                chain.end()


ITERATIONS = 3
HALF_STEPS = 2 * ITERATIONS
OUT_LN_EPS = 1e-12


class SinkhornLane:

    def __init__(self, a, ps):
        self.ps = ps
        self.h = a.sb("h", [HT, 2, C])
        self.lnst = a.sb("lnst", [HT, 2, 6])
        self.lnmv = a.sb("lnmv", [HT, 2, 2])
        self.lnr = a.sb("lnr", [HT, 2])
        self.xn = a.sb("xn", [HT, 2, C])
        self.xt = a.sb("xt", [P, 2, TP])
        self.q = a.sb("q", [P, NG, TP])
        self.kpad = a.sb("kpad", [P, HEADS, TP])
        self.v = a.sb("v", [HT, 2, HEADS, SLOT])
        self.mneg = a.sb("mneg", [HT, NG, 2, P])
        self.kt = a.sb("kt", [HT, NG, HG, 2, TP])
        self.km = a.sb("km", [HT, NG, HG, 2, TP])
        self.row = a.sb("row", [P, NG, TP])
        self.arow = a.sb("arow", [P, NG, TP])
        self.neg = a.sb("neg", [HT, 2, HEADS])
        self.a = a.sb("a", [HT, 2, HEADS])
        self.b = a.sb("b", [HT, 2, HEADS])
        self.ln_in, self.ln_rstd, self.xn_in = a.sems("ln_in", "ln_rstd", "xn_in")
        self.xn_t, self.xt_in, self.q_out = a.sems("xn_t", "xt_in", "q_out")
        self.k_out, self.v_out, self.q_in = a.sems("k_out", "v_out", "q_in")
        self.k_in, self.v_in, self.s_out = a.sems("k_in", "v_in", "s_out")
        self.s_max, self.shift_out, self.q_aug = a.sems("s_max", "shift_out", "q_aug")
        self.zeroed, self.h_done, self.resid_in = a.sems("zeroed", "h_done", "resid_in")
        self.st_out, self.st_max, self.kt_in = a.sems("st_out", "st_max", "kt_in")
        self.b_start, self.km_out, self.km_in = a.sems("b_start", "km_out", "km_in")
        self.sum_out, self.row_in, self.row_t = a.sems("sum_out", "row_in", "row_t")
        self.col_in, self.arow_out, self.arow_in = a.sems("col_in", "arow_out", "arow_in")
        self.v_scaled, self.pv_out, self.ctx_in = a.sems("v_scaled", "pv_out", "ctx_in")
        self.proj_out, self.ln2_in, self.ln2_rstd = a.sems("proj_out", "ln2_in", "ln2_rstd")


def phase_sinkhorn(nc, w, hres):
    DVE_LINKS = 1 + 2 * 8
    with ExitStack() as st:
        A = Alloc(nc, st, "sink_")
        psum = A.psum()
        wq, wk = (A.sb(n, [P, 2, NG, P]) for n in ("wq", "wk"))
        wv = A.sb("wv", [P, 2, C])
        wo = A.sb("wo", [P, NG, C])
        vb = A.sb("vb", [P, 2 * C])
        qb, kb = A.sb("qb", [P, NG]), A.sb("kb", [P, NG])
        rows = A.sb("rows", [P, 1])
        vec = A.sb("vec", [P, 3, 2, C])
        ident = A.sb("ident", [P, P])
        spare = A.sb("spare", [1, 1])
        half = A.sb("half", [P, 1])
        loaded, consts, ready, dve_chain = (A.sem(n) for n in ("loaded", "consts", "ready", "dve_chain"))
        L = [SinkhornLane(A.of_lane(lane), psum[:, lane * LANE_BANKS:(lane + 1) * LANE_BANKS, :]) for lane in LANES]
        block = st.enter_context(nc.Block())

        @block.sync
        def _(sp):
            load_all(sp, ((wq[:], w["s_wq"]), (wk[:], w["s_wk"]), (wv[:], w["s_wv"]), (wo[:], w["s_wo"]),
                          (vb[:], w["s_vb"]), (qb[:], w["s_qb"]), (kb[:], w["s_kb"]), (rows[:], w["slot_rows"]),
                          (ident[:], w["ident"]), (vec[:], w["s_rows"])), loaded)

        @block.gpsimd
        def _(pool):
            pool.memset(half[:], -0.5).then_inc(consts, 1)
            pool.wait_ge(consts, 1)
            with pool.Fori(0, PAIRS) as it:
                for l in L:
                    pool.wait_ge(l.ln_in, it + 1)
                    pool_rstd(pool, l, half).then_inc(l.ln_rstd, 1)
                for l in L:
                    pool.wait_ge(l.ln2_in, it + 1)
                    pool_rstd(pool, l, half).then_inc(l.ln2_rstd, 1)

        @block.tensor
        def _(pe):
            pe.wait_ge(loaded, 10 * 16)
            for l in L:
                pe.wait_ge(l.zeroed, 4)
            with pe.Fori(0, PAIRS) as it:
                for l in L:
                    pe.wait_ge(l.xn_in, it + 1)
                    pe.wait_ge(l.h_done, it)
                    pe_transpose_tokens(pe, l, l.xn, ident).then_inc(l.xn_t, 1)
                for l in L:
                    pe.wait_ge(l.xt_in, it * 2 + 2)
                    pe_project_padded(pe, l, wq, BANKS_Q).then_inc(l.q_out, 1)
                    pe_project_padded(pe, l, wk, BANKS_K).then_inc(l.k_out, 1)
                for l in L:
                    pe.wait_ge(l.q_in, it + 1)
                    pe_project_values(pe, l, wv, 2).then_inc(l.v_out, 1)
                for g in range(NG):
                    for l in L:
                        if g == 0:
                            pe.wait_ge(l.k_in, it + 1)
                            pe.wait_ge(l.v_in, it + 1)
                        else:
                            pe.wait_ge(l.s_max, it * NG + g)
                        pe_scores(pe, l, g, 2).then_inc(l.s_out, 1)
                for l in L:
                    pe.wait_ge(l.s_max, it * NG + NG)
                    pe_shift_rows(pe, l, l.mneg, ident).then_inc(l.shift_out, 1)
                for g in range(NG):
                    for l in L:
                        pe.wait_ge(l.q_aug, it + 1)
                        if g:
                            pe.wait_ge(l.kt_in, it * NG + g)
                        pe_scores_t(pe, l, g).then_inc(l.st_out, 1)
                for g in range(NG):
                    for l in L:
                        pe.wait_ge(l.kt_in, it * NG + NG)
                        if g:
                            pe.wait_ge(l.km_in, it * NG + g)
                        pe_transpose_scores(pe, l, g, l.kt, ident).then_inc(l.km_out, 1)
                for s in range(HALF_STEPS):
                    for l in L:
                        pe.wait_ge(l.km_in, it * NG + NG)
                        if s == 0:
                            pe.wait_ge(l.b_start, it + 1)
                        else:
                            pe.wait_ge(l.col_in, it * HALF_STEPS + s)
                        pe_column_sums(pe, l, *((l.a, l.km) if s % 2 else (l.b, l.kt))).then_inc(l.sum_out, 1)
                    for l in L:
                        pe.wait_ge(l.row_in, it * HALF_STEPS + s + 1)
                        for g in range(NG):
                            for t in range(2):
                                last = pe.transpose(l.ps[0:HT, (3, 0)[t], g * P:(g + 1) * P], l.row[:, g, t * HT:(t + 1) * HT],
                                                    ident[:])
                        last.then_inc(l.row_t, 1)
                        if s == HALF_STEPS - 1:
                            pe_columns_to_rows(pe, l, l.a, ident, BANKS_ROWS).then_inc(l.arow_out, 1)
                for l in L:
                    pe.wait_ge(l.arow_in, it + 1)
                    pe.wait_ge(l.v_scaled, it + 1)
                    pe_weighted_sum(pe, l, l.v, l.kt).then_inc(l.pv_out, 1)
                for l in L:
                    pe.wait_ge(l.ctx_in, it + 1)
                    pe_project_back(pe, l, l.row, wo, 3).then_inc(l.proj_out, 1)

        @block.scalar
        def _(act):
            act.wait_ge(ready, 2)
            for l in L:
                act.wait_ge(l.zeroed, 4)
            with act.Fori(0, PAIRS) as it:
                for l in L:
                    act.wait_ge(l.xn_t, it + 1)
                    for c, n in enumerate(CT):
                        act.activation(l.xt[0:n, c, :], l.ps[0:n, c, 0:TP], ACT.Copy).then_inc(l.xt_in, 1)
                for l in L:
                    act.wait_ge(l.k_out, it + 1)
                    act_keys(act, l, kb, BANKS_K).then_inc(l.k_in, 1)
                for g in range(NG):
                    for l in L:
                        act.wait_ge(l.st_max, it * NG + g + 1)
                        act_group_exp(act, l, g, l.kt, l.neg).then_inc(l.kt_in, 1)
                for l in L:
                    act.activation(l.b[:], l.neg[:], ACT.Exp, scale=-1.0).then_inc(l.b_start, 1)
                for l in L:
                    for g in range(1, NG):
                        act.wait_ge(l.km_out, it * NG + g + 1)
                        act_copy_group(act, l, g, l.km).then_inc(l.km_in, 1)
                for s in range(HALF_STEPS):
                    for l in L:
                        act.wait_ge(l.sum_out, it * HALF_STEPS + s + 1)
                        act.activation(l.row[:], l.ps[:, 0:NG, 0:TP], ACT.Copy).then_inc(l.row_in, 1)
                for l in L:
                    act.wait_ge(l.arow_out, it + 1)
                    act_rows(act, l, l.arow).then_inc(l.arow_in, 1)

        @block.vector
        def _(dve):
            for l in L:
                dve.memset(l.kpad[:], 0.0).then_inc(l.zeroed, 1)
                dve.memset(l.mneg[:], 0.0).then_inc(l.zeroed, 1)
                dve.memset(l.v[:, :, :, D:SLOT], 0.0).then_inc(l.zeroed, 1)
                dve.memset(l.kt[:, :, :, :, TOK:TP], 1.0).then_inc(l.zeroed, 1)
            dve.wait_ge(loaded, 10 * 16)
            pre = Chain(dve, dve_chain, 0)
            dve.tensor_scalar(qb[:], qb[:], D ** -0.5, None, ALU.mult).then_inc(ready, 1)
            dve.tensor_scalar(kb[:], kb[:], rows[:, 0:1], None, ALU.add).then_inc(ready, 1)
            dve.wait_ge(ready, 2)
            chain = Chain(dve, dve_chain, DVE_LINKS, pre.n, spare[:])
            with dve.Fori(0, PAIRS) as it:
                chain.begin(it)
                chain.link(dve_read_pair(dve, L, hres, it))
                for l in L:
                    dve_norm_stats(dve, chain, l, l.h, LN_EPS, l.ln_in)
                for l in L:
                    dve.wait_ge(l.ln_rstd, it + 1)
                    dve_norm_apply(dve, l, l.xn, l.h).then_inc(l.xn_in, 1)
                for l in L:
                    dve.wait_ge(l.xn_t, it + 1)
                    dve.tensor_tensor(l.xn[:], l.xn[:], vec[0:HT, 0, :, :], ALU.add).then_inc(l.resid_in, 1)
                    dve.wait_ge(l.q_out, it + 1)
                    dve_queries(dve, l, qb, BANKS_Q, D ** -0.5).then_inc(l.q_in, 1)
                for l in L:
                    dve.wait_ge(l.v_out, it + 1)
                    dve_values(dve, l, vb, 2).then_inc(l.v_in, 1)
                for g in range(NG):
                    for l in L:
                        dve.wait_ge(l.s_out, it * NG + g + 1)
                        dve_score_max(dve, l, g, l.mneg, ROW_MAX).then_inc(l.s_max, 1)
                for l in L:
                    dve.wait_ge(l.shift_out, it + 1)
                    dve.tensor_tensor(l.q[:], l.q[:], l.ps[:, 0:NG, 0:TP], ALU.add).then_inc(l.q_aug, 1)
                for g in range(NG):
                    for l in L:
                        dve.wait_ge(l.st_out, it * NG + g + 1)
                        dve_group_max(dve, l, g, l.neg).then_inc(l.st_max, 1)
                for l in L:
                    dve.wait_ge(l.km_out, it * NG + 1)
                    dve_copy_group(dve, l, 0, l.km).then_inc(l.km_in, 1)
                for s in range(HALF_STEPS):
                    for l in L:
                        dve.wait_ge(l.row_t, it * HALF_STEPS + s + 1)
                        dst = l.b if s % 2 else l.a
                        for t in range(2):
                            sums = l.ps[0:HT, (3, 0)[t], 0:NG * P].rearrange("p (h r) -> p h r", r=SLOT)[:, :, 0]
                            last = dve.reciprocal(dst[:, t, :], sums)
                        last.then_inc(l.col_in, 1)
                for l in L:
                    dve.wait_ge(l.col_in, (it + 1) * HALF_STEPS)
                    for t in range(2):
                        b = l.b[:, t, :].rearrange("p (h o) -> p h o", o=1).to_broadcast([HT, HEADS, D])
                        last = dve.tensor_tensor(l.v[:, t, :, 0:D], l.v[:, t, :, 0:D], b, ALU.mult)
                    last.then_inc(l.v_scaled, 1)
                for l in L:
                    dve.wait_ge(l.pv_out, it + 1)
                    dve.wait_ge(l.arow_in, it + 1)
                    dve.tensor_tensor(l.row[:], l.ps[:, 0:NG, 0:TP], l.arow[:], ALU.mult).then_inc(l.ctx_in, 1)
                for l in L:
                    dve.wait_ge(l.proj_out, it + 1)
                    xf = l.xn[:].rearrange("p t c -> p (t c)")
                    chain.link(dve.tensor_tensor(xf, xf, l.ps[0:HT, 3, 0:2 * C], ALU.add))
                    dve_norm_stats(dve, chain, l, l.xn, OUT_LN_EPS, l.ln2_in)
                for lane, l in enumerate(L):
                    clip = it * len(LANES) + lane
                    dve.wait_ge(l.ln2_rstd, it + 1)
                    chain.link(dve_norm_apply(dve, l, l.xn, l.xn))
                    chain.link(dve.tensor_tensor(l.xn[:], l.xn[:], vec[0:HT, 1, :, :], ALU.mult))
                    chain.link(dve.tensor_tensor(l.h[:], l.h[:], vec[0:HT, 2, :, :], ALU.add))
                    dve.tensor_tensor(hres[:, bass.ds(clip, 1), :, :].rearrange("p b t c -> p (b t c)"),
                                      l.h[:].rearrange("p t c -> p (t c)"), l.xn[:].rearrange("p t c -> p (t c)"),
                                      ALU.add).then_inc(l.h_done, 1)
                for l in L:
                    dve.wait_ge(l.h_done, it + 1)
                chain.end()


HIDDEN = 768
FT = HIDDEN // P
ROUTED = max(1, int(round(0.15 * TOK)))
POOL_EPS = 1e-6
BANKS_RK = ((2, 0), (2, TP), (3, 0))
G1, B1, G2, B2, BM, BF2, WR = range(7)


class RoutedLane:

    def __init__(self, a, ps):
        self.ps = ps
        self.h = a.sb("h", [HT, 2, C])
        self.lnst = a.sb("lnst", [HT, 2, 6])
        self.lnmv = a.sb("lnmv", [HT, 2, 2])
        self.lnr = a.sb("lnr", [HT, 2])
        self.xt = a.sb("xt", [P, 2, TP])
        self.kpad = a.sb("kpad", [P, HEADS, TP])
        self.v = a.sb("v", [HT, 2, HEADS, SLOT])
        self.hs = a.sb("hs", [HT, 2, C])
        self.nm = a.sb("nm", [HT, 2, C + 1])
        self.zz = a.sb("zz", [HT, 2, C])
        self.z = a.sb("z", [HT, 2])
        self.s = a.sb("s", [HT, 2])
        self.diag = a.sb("diag", [HT, 2, HT])
        self.cmp = a.sb("cmp", [HT, 4, TOK])
        self.cnt = a.sb("cnt", [HT, 4])
        self.rank = a.sb("rank", [HT, 2])
        self.sel = a.sb("sel", [HT, 2, ROUTED])
        self.rest = a.sb("rest", [HT, 2])
        self.pool = a.sb("pool", [HT, C])
        self.rsum = a.sb("rsum", [HT, 1])
        self.mx = a.sb("mx", [HT, 2, C])
        self.xsel = a.sb("xsel", [P, 2, ROUTED])
        self.selT = a.sb("selT", [ROUTED, TP])
        self.q = a.sb("q", [P, NG, ROUTED])
        self.mneg = a.sb("mneg", [ROUTED, NG, P])
        self.e = a.sb("e", [HT, 2, HEADS, ROUTED])
        self.ctx = a.sb("ctx", [P, NG, ROUTED])
        self.rden = a.sb("rden", [P, NG * ROUTED])
        self.asel = a.sb("asel", [ROUTED, C])
        self.h1 = a.sb("h1", [HT, 2, C])
        self.gl = a.sb("gl", [P, FT, TP])
        self.o = a.sb("o", [HT, 2, C])
        self.ln_in, self.ln_rstd, self.z_in = a.sems("ln_in", "ln_rstd", "z_in")
        self.ez_in, self.diag_in, self.xn_in = a.sems("ez_in", "diag_in", "xn_in")
        self.srow_out, self.pool_out, self.xn_t = a.sems("srow_out", "pool_out", "xn_t")
        self.xt_in, self.sel_in, self.mx_in = a.sems("xt_in", "sel_in", "mx_in")
        self.sel_out, self.xsel_in, self.selT_in = a.sems("sel_out", "xsel_in", "selT_in")
        self.q_out, self.k_out, self.v_out = a.sems("q_out", "k_out", "v_out")
        self.q_in, self.k_in, self.v_in = a.sems("q_in", "k_in", "v_in")
        self.s_out, self.s_max, self.shift_out = a.sems("s_out", "s_max", "shift_out")
        self.q_aug, self.st_out, self.e_in = a.sems("q_aug", "st_out", "e_in")
        self.pv_out, self.ctxu_in, self.den_out = a.sems("pv_out", "ctxu_in", "den_out")
        self.ctx_in, self.asel_out, self.asel_in = a.sems("ctx_in", "asel_out", "asel_in")
        self.mx_t, self.mxt_in, self.merged = a.sems("mx_t", "mxt_in", "merged")
        self.n2_in, self.n2_t, self.n2t_in = a.sems("n2_in", "n2_t", "n2t_in")
        self.up_out, self.gl_in, self.down_out = a.sems("up_out", "gl_in", "down_out")
        self.o_in, self.stored, self.zeroed = a.sems("o_in", "stored", "zeroed")


def phase_routed(nc, w, hres, out):
    DVE_LINKS = 1 + 2 * 26
    with ExitStack() as st:
        A = Alloc(nc, st, "rout_")
        psum = A.psum()
        wq, wk = (A.sb(n, [P, 2, NG, P]) for n in ("wq", "wk"))
        wv, wm = A.sb("wv", [P, 2, C]), A.sb("wm", [P, 2, C])
        wo = A.sb("wo", [P, NG, C])
        w1, w2 = A.sb("w1", [P, 2, HIDDEN]), A.sb("w2", [P, FT, C])
        vb = A.sb("vb", [P, 2 * C])
        qb, kb = A.sb("qb", [P, NG]), A.sb("kb", [P, NG])
        b1 = A.sb("b1", [P, FT])
        vec = A.sb("vec", [P, 7, 2, C])
        nbr = A.sb("nbr", [P, 1])
        rows = A.sb("rows", [P, 1])
        ident = A.sb("ident", [P, P])
        spare = A.sb("spare", [1, 1])
        spread = A.sb("spread", [P, P])
        ones = A.sb("ones", [P, P])
        ids = A.sb("ids", [P, ROUTED])
        earlier = A.sb("earlier", [HT, 2, TOK])
        half = A.sb("half", [P, 1])
        loaded, consts, ready, dve_chain = (A.sem(n) for n in ("loaded", "consts", "ready", "dve_chain"))
        L = [RoutedLane(A.of_lane(lane), psum[:, lane * LANE_BANKS:(lane + 1) * LANE_BANKS, :]) for lane in LANES]
        block = st.enter_context(nc.Block())

        @block.sync
        def _(sp):
            load_all(sp, ((wq[:], w["r_wq"]), (wk[:], w["r_wk"]), (wv[:], w["r_wv"]), (wo[:], w["r_wo"]),
                          (vb[:], w["r_vb"]), (qb[:], w["r_qb"]), (kb[:], w["r_kb"]), (rows[:], w["slot_rows"]),
                          (ident[:], w["ident"]), (spread[:], w["spread"]), (wm[:], w["r_wm"]),
                          (w1[:], w["r_w1"]), (w2[:], w["r_w2"]), (b1[:], w["r_b1"]), (vec[:], w["r_rows"]),
                          (nbr[:], w["r_br"]), (ids[:], w["rank_ids"]), (earlier[:], w["earlier"])), loaded)
            with sp.Fori(0, PAIRS) as it:
                for lane, l in enumerate(L):
                    clip = it * len(LANES) + lane
                    sp.wait_ge(l.o_in, it + 1)
                    dst = out[bass.ds(clip, 1), :, :]
                    sp.dma_start(dst[:, 0:HT, :].rearrange("b p c -> p (b c)"), l.o[:, 0, :]).then_inc(l.stored, 16)
                    sp.dma_start(dst[:, HT:TOK, :].rearrange("b p c -> p (b c)"), l.o[0:TILE_TOK[1], 1, :])\
                      .then_inc(l.stored, 16)
            for l in L:
                sp.wait_ge(l.stored, PAIRS * 32)

        @block.gpsimd
        def _(pool):
            pool.memset(half[:], -0.5).then_inc(consts, 1)
            pool.memset(ones[:], 1.0).then_inc(consts, 1)
            pool.wait_ge(consts, 2)
            with pool.Fori(0, PAIRS) as it:
                for k in range(3):
                    for l in L:
                        pool.wait_ge(l.ln_in, it * 3 + k + 1)
                        pool_rstd(pool, l, half).then_inc(l.ln_rstd, 1)

        @block.tensor
        def _(pe):
            pe.wait_ge(loaded, 18 * 16)
            pe.wait_ge(consts, 2)
            for l in L:
                pe.wait_ge(l.zeroed, 5)
            with pe.Fori(0, PAIRS) as it:
                for l in L:
                    pe.wait_ge(l.xn_in, it + 1)
                    pe.wait_ge(l.o_in, it)
                    pe_transpose_tokens(pe, l, l.nm, ident, (2, 3)).then_inc(l.xn_t, 1)
                for l in L:
                    pe.wait_ge(l.diag_in, it + 1)
                    for t in range(2):
                        last = pe.matmul(l.ps[0:HT, 0, t * HT:(t + 1) * HT], ones[0:HT, 0:HT], l.diag[:, t, :],
                                         start=True, stop=True)
                    last.then_inc(l.srow_out, 1)
                    for t, keys in enumerate(TILE_TOK):
                        last = pe.matmul(l.ps[0:HT, 1, 0:C + 1], l.s[0:keys, t:t + 1].to_broadcast([keys, HT]),
                                         l.nm[0:keys, t, :], start=(t == 0), stop=(t == 1))
                    last.then_inc(l.pool_out, 1)
                for l in L:
                    pe.wait_ge(l.xt_in, it * 2 + 2)
                    pe_project_padded(pe, l, wk, BANKS_RK).then_inc(l.k_out, 1)
                for l in L:
                    pe.wait_ge(l.sel_in, it + 1)
                    for c, n in enumerate(CT):
                        for t, keys in enumerate(TILE_TOK):
                            pe.matmul(l.ps[0:n, 0, c * ROUTED:(c + 1) * ROUTED], l.nm[0:keys, t, c * P:c * P + n],
                                      l.sel[0:keys, t, :], start=(t == 0), stop=(t == 1))
                    for t in range(2):
                        last = pe.transpose(l.ps[0:ROUTED, 0, P + t * HT:P + (t + 1) * HT], l.sel[:, t, :],
                                            ident[0:HT, 0:HT])
                    last.then_inc(l.sel_out, 1)
                    pe.wait_ge(l.mx_in, it + 1)
                    pe_project_values(pe, l, wv, 1).then_inc(l.v_out, 1)
                for l in L:
                    pe.wait_ge(l.xsel_in, it * 2 + 2)
                    pe.wait_ge(l.selT_in, it + 1)
                    for g in range(NG):
                        for c, n in enumerate(CT):
                            last = pe.matmul(l.ps[:, 0, g * ROUTED:(g + 1) * ROUTED], wq[0:n, c, g, :],
                                             l.xsel[0:n, c, :], start=(c == 0), stop=(c == 1))
                    last.then_inc(l.q_out, 1)
                for g in range(NG):
                    for l in L:
                        if g == 0:
                            pe.wait_ge(l.q_in, it + 1)
                            pe.wait_ge(l.k_in, it + 1)
                            pe.wait_ge(l.v_in, it + 1)
                        else:
                            pe.wait_ge(l.s_max, it * NG + g)
                        for hq in range(HG):
                            last = pe.matmul(l.ps[0:ROUTED, hq, 0:TP], l.q[:, g, :], l.kpad[:, HG * g + hq, :],
                                             start=True, stop=True)
                        last.then_inc(l.s_out, 1)
                for l in L:
                    pe.wait_ge(l.s_max, it * NG + NG)
                    for g in range(NG):
                        last = pe.matmul(l.ps[:, 0, g * ROUTED:(g + 1) * ROUTED], l.mneg[:, g, :],
                                         ident[0:ROUTED, 0:ROUTED], start=True, stop=True)
                    last.then_inc(l.shift_out, 1)
                for l in L:
                    pe.wait_ge(l.q_aug, it + 1)
                    for t in range(2):
                        for h in range(HEADS):
                            last = pe.matmul(l.ps[0:HT, 1 + t, h * ROUTED:(h + 1) * ROUTED],
                                             l.kpad[:, h, t * HT:(t + 1) * HT], l.q[:, h // HG, :],
                                             start=True, stop=True)
                    last.then_inc(l.st_out, 1)
                for l in L:
                    pe.wait_ge(l.e_in, it + 1)
                    for g in range(NG):
                        for t, keys in enumerate(TILE_TOK):
                            for hq in range(HG):
                                h = HG * g + hq
                                last = pe.matmul(l.ps[SLOT * hq:SLOT * (hq + 1), 3, g * ROUTED:(g + 1) * ROUTED],
                                                 l.v[0:keys, t, h, :], l.e[0:keys, t, h, :], start=(t == 0),
                                                 stop=(t == 1), skip_group_check=True)
                    last.then_inc(l.pv_out, 1)
                for l in L:
                    pe.wait_ge(l.mx_in, it + 1)
                    pe_transpose_tokens(pe, l, l.mx, ident, (1, 2)).then_inc(l.mx_t, 1)
                for l in L:
                    pe.wait_ge(l.ctxu_in, it + 1)
                    pe.matmul(l.ps[:, 0, 0:NG * ROUTED], spread[:], l.ctx[:].rearrange("p g r -> p (g r)"),
                              start=True, stop=True).then_inc(l.den_out, 1)
                for l in L:
                    pe.wait_ge(l.ctx_in, it + 1)
                    for g in range(NG):
                        last = pe.matmul(l.ps[0:ROUTED, 3, 0:C], l.ctx[:, g, :], wo[:, g, :], start=(g == 0),
                                         stop=(g == NG - 1))
                    last.then_inc(l.asel_out, 1)
                for l in L:
                    pe.wait_ge(l.mxt_in, it * 2 + 2)
                    pe.wait_ge(l.asel_in, it + 1)
                    for t in range(2):
                        at = slice(t * HT, (t + 1) * HT)
                        o = l.ps[0:HT, 0, t * C:(t + 1) * C]
                        pe.matmul(o, l.selT[:, at], l.asel[:], start=True, stop=False)
                        for c, n in enumerate(CT):
                            last = pe.matmul(o, l.xt[0:n, c, at], wm[0:n, c, :], start=False, stop=(c == 1))
                    last.then_inc(l.merged, 1)
                for l in L:
                    pe.wait_ge(l.n2_in, it + 1)
                    pe_transpose_tokens(pe, l, l.mx, ident, (1, 2)).then_inc(l.n2_t, 1)
                for l in L:
                    pe.wait_ge(l.n2t_in, it * 2 + 2)
                    for f in range(FT):
                        for c, n in enumerate(CT):
                            last = pe.matmul(l.ps[:, f // 2, (f % 2) * TP:(f % 2 + 1) * TP],
                                             w1[0:n, c, f * P:(f + 1) * P], l.xt[0:n, c, :],
                                             start=(c == 0), stop=(c == 1))
                        if f % 2:
                            last.then_inc(l.up_out, 1)
                for l in L:
                    pe.wait_ge(l.gl_in, it * FT + FT)
                    for t in range(2):
                        for f in range(FT):
                            last = pe.matmul(l.ps[0:HT, 3, t * C:(t + 1) * C], l.gl[:, f, t * HT:(t + 1) * HT],
                                             w2[:, f, :], start=(f == 0), stop=(f == FT - 1))
                    last.then_inc(l.down_out, 1)

        @block.scalar
        def _(act):
            act.wait_ge(loaded, 18 * 16)
            act.wait_ge(ready, 3)
            for l in L:
                act.wait_ge(l.zeroed, 5)
            with act.Fori(0, PAIRS) as it:
                for l in L:
                    act.wait_ge(l.z_in, it + 1)
                    act.activation(l.z[:], l.z[:], ACT.Exp, bias=nbr[0:HT, :], scale=-1.0).then_inc(l.ez_in, 1)
                for l in L:
                    act.wait_ge(l.xn_t, it + 1)
                    for c, n in enumerate(CT):
                        act.activation(l.xt[0:n, c, :], l.ps[0:n, 2 + c, 0:TP], ACT.Copy).then_inc(l.xt_in, 1)
                for l in L:
                    act.wait_ge(l.k_out, it + 1)
                    act_keys(act, l, kb, BANKS_RK).then_inc(l.k_in, 1)
                for l in L:
                    act.wait_ge(l.sel_out, it + 1)
                    for c, n in enumerate(CT):
                        act.activation(l.xsel[0:n, c, :], l.ps[0:n, 0, c * ROUTED:(c + 1) * ROUTED], ACT.Copy)\
                           .then_inc(l.xsel_in, 1)
                    act.activation(l.selT[:], l.ps[0:ROUTED, 0, P:P + TP], ACT.Copy).then_inc(l.selT_in, 1)
                for l in L:
                    act.wait_ge(l.st_out, it + 1)
                    act.activation(l.e[:].rearrange("p t h r -> p t (h r)"), l.ps[0:HT, 1:3, 0:HEADS * ROUTED],
                                   ACT.Exp).then_inc(l.e_in, 1)
                for l in L:
                    act.wait_ge(l.mx_t, it + 1)
                    act.wait_ge(l.v_out, it + 1)
                    for c, n in enumerate(CT):
                        act.activation(l.xt[0:n, c, :], l.ps[0:n, 1 + c, 0:TP], ACT.Copy).then_inc(l.mxt_in, 1)
                for l in L:
                    act.wait_ge(l.asel_out, it + 1)
                    act.activation(l.asel[:], l.ps[0:ROUTED, 3, 0:C], ACT.Copy).then_inc(l.asel_in, 1)
                for l in L:
                    act.wait_ge(l.n2_t, it + 1)
                    for c, n in enumerate(CT):
                        act.activation(l.xt[0:n, c, :], l.ps[0:n, 1 + c, 0:TP], ACT.Copy).then_inc(l.n2t_in, 1)
                for l in L:
                    for f in range(FT):
                        act.wait_ge(l.up_out, it * (FT // 2) + f // 2 + 1)
                        act.activation(l.gl[:, f, :], l.ps[:, f // 2, (f % 2) * TP:(f % 2 + 1) * TP], ACT.Gelu,
                                       bias=b1[:, f:f + 1]).then_inc(l.gl_in, 1)

        @block.vector
        def _(dve):
            for l in L:
                dve.memset(l.kpad[:], 0.0).then_inc(l.zeroed, 1)
                dve.memset(l.mneg[:], 0.0).then_inc(l.zeroed, 1)
                dve.memset(l.v[:, :, :, D + 1:SLOT], 0.0).then_inc(l.zeroed, 1)
                dve.memset(l.v[:, :, :, V_ONE], 1.0).then_inc(l.zeroed, 1)
                dve.memset(l.nm[:, :, C:C + 1], 1.0).then_inc(l.zeroed, 1)
            dve.wait_ge(loaded, 18 * 16)
            dve.tensor_scalar(qb[:], qb[:], D ** -0.5, None, ALU.mult).then_inc(ready, 1)
            dve.tensor_scalar(kb[:], kb[:], rows[:, 0:1], None, ALU.add).then_inc(ready, 1)
            dve.tensor_scalar(nbr[:], nbr[:], -1.0, None, ALU.mult).then_inc(ready, 1)
            dve.wait_ge(ready, 3)
            chain = Chain(dve, dve_chain, DVE_LINKS, 0, spare[:])
            v_ = lambda k: vec[0:HT, k, :, :]
            with dve.Fori(0, PAIRS) as it:
                chain.begin(it)
                chain.link(dve_read_pair(dve, L, hres, it))
                for l in L:
                    dve_norm_stats(dve, chain, l, l.h, LN_EPS, l.ln_in)
                for l in L:
                    dve.wait_ge(l.ln_rstd, it * 3 + 1)
                    chain.link(dve_norm_apply(dve, l, l.hs, l.h))
                    dve_norm_stats(dve, chain, l, l.hs, LN_EPS, l.ln_in)
                for l in L:
                    dve.wait_ge(l.ln_rstd, it * 3 + 2)
                    nm = l.nm[:, :, 0:C]
                    chain.link(dve_norm_apply(dve, l, nm, l.hs))
                    chain.link(dve.tensor_tensor(nm, nm, v_(G1), ALU.mult))
                    dve.tensor_tensor(nm, nm, v_(B1), ALU.add).then_inc(l.xn_in, 1)
                    dve.wait_ge(l.xn_in, it + 1)
                    chain.link(dve.tensor_tensor(l.zz[:], nm, v_(WR), ALU.mult))
                    dve.tensor_reduce(l.z[:], l.zz[:], AX_X, ALU.add).then_inc(l.z_in, 1)
                for l in L:
                    dve.wait_ge(l.ez_in, it + 1)
                    chain.link(dve.tensor_scalar(l.s[:], l.z[:], 1.0, None, ALU.add))
                    chain.link(dve.reciprocal(l.s[:], l.s[:]))
                    for t in range(2):
                        last = dve.tensor_scalar(l.diag[:, t, :], ident[0:HT, 0:HT], l.s[:, t:t + 1], None, ALU.mult)
                    last.then_inc(l.diag_in, 1)
                for l in L:
                    dve.wait_ge(l.srow_out, it + 1)
                    srow = l.ps[0:HT, 0, 0:TOK]
                    for t in range(2):
                        dve.tensor_scalar(l.cmp[:, t, :], srow, l.s[:, t:t + 1], None, ALU.is_lt)
                        last = dve.scalar_tensor_tensor(l.cmp[:, 2 + t, :], srow, l.s[:, t:t + 1], earlier[:, t, :],
                                                        ALU.is_equal, ALU.mult)
                    chain.link(last)
                    chain.link(dve.tensor_reduce(l.cnt[:], l.cmp[:], AX_X, ALU.add))
                    chain.link(dve.tensor_tensor(l.rank[:], l.cnt[:, 0:2], l.cnt[:, 2:4], ALU.add))
                    dve.tensor_scalar(l.rest[:], l.rank[:], float(ROUTED), None, ALU.is_ge)
                    for t in range(2):
                        last = dve.tensor_scalar(l.sel[:, t, :], ids[0:HT, :], l.rank[:, t:t + 1], None, ALU.is_equal)
                    last.then_inc(l.sel_in, 1)
                    dve.wait_ge(l.sel_in, it + 1)
                    dve.wait_ge(l.pool_out, it + 1)
                    chain.link(dve.tensor_scalar(l.rsum[:], l.ps[0:HT, 1, C:C + 1], POOL_EPS, None, ALU.add))
                    chain.link(dve.reciprocal(l.rsum[:], l.rsum[:]))
                    chain.link(dve.tensor_scalar(l.pool[:], l.ps[0:HT, 1, 0:C], l.rsum[:, 0:1], None, ALU.mult))
                    for t in range(2):
                        last = dve.scalar_tensor_tensor(l.mx[:, t, :], l.pool[:], l.s[:, t:t + 1], l.nm[:, t, 0:C],
                                                        ALU.mult, ALU.add)
                    chain.link(last)
                    for t in range(2):
                        last = dve.tensor_scalar(l.mx[:, t, :], l.mx[:, t, :], l.rest[:, t:t + 1], None, ALU.mult)
                    last.then_inc(l.mx_in, 1)
                    for t in range(2):
                        last = dve.scalar_tensor_tensor(l.hs[:, t, :], vec[0:HT, BM, t, :], l.rest[:, t:t + 1],
                                                        l.hs[:, t, :], ALU.mult, ALU.add)
                    chain.link(last)
                for l in L:
                    dve.wait_ge(l.v_out, it + 1)
                    dve_values(dve, l, vb, 1).then_inc(l.v_in, 1)
                    dve.wait_ge(l.q_out, it + 1)
                    for g in range(NG):
                        last = dve.tensor_scalar(l.q[:, g, :], l.ps[:, 0, g * ROUTED:(g + 1) * ROUTED], D ** -0.5,
                                                 qb[:, g:g + 1], ALU.mult, ALU.add)
                    last.then_inc(l.q_in, 1)
                for g in range(NG):
                    for l in L:
                        dve.wait_ge(l.s_out, it * NG + g + 1)
                        o = l.mneg[:, g, :].rearrange("p (q s) -> p q s", s=SLOT)[:, :, ROW_MAX]
                        dve.tensor_reduce(o, l.ps[0:ROUTED, :, 0:TOK], AX_X, ALU.max, negate=True).then_inc(l.s_max, 1)
                for l in L:
                    dve.wait_ge(l.shift_out, it + 1)
                    qf = l.q[:].rearrange("p g r -> p (g r)")
                    dve.tensor_tensor(qf, qf, l.ps[:, 0, 0:NG * ROUTED], ALU.add).then_inc(l.q_aug, 1)
                for l in L:
                    dve.wait_ge(l.pv_out, it + 1)
                    cf = l.ctx[:].rearrange("p g r -> p (g r)")
                    dve.tensor_copy(cf, l.ps[:, 3, 0:NG * ROUTED]).then_inc(l.ctxu_in, 1)
                for l in L:
                    dve.wait_ge(l.den_out, it + 1)
                    cf = l.ctx[:].rearrange("p g r -> p (g r)")
                    chain.link(dve.reciprocal(l.rden[:], l.ps[:, 0, 0:NG * ROUTED]))
                    dve.tensor_tensor(cf, cf, l.rden[:], ALU.mult).then_inc(l.ctx_in, 1)
                for l in L:
                    dve.wait_ge(l.merged, it + 1)
                    chain.link(dve.tensor_tensor(l.h1[:].rearrange("p t c -> p (t c)"),
                                                 l.hs[:].rearrange("p t c -> p (t c)"), l.ps[0:HT, 0, 0:2 * C],
                                                 ALU.add))
                    dve_norm_stats(dve, chain, l, l.h1, LN_EPS, l.ln_in)
                for l in L:
                    dve.wait_ge(l.ln_rstd, it * 3 + 3)
                    chain.link(dve_norm_apply(dve, l, l.mx, l.h1))
                    chain.link(dve.tensor_tensor(l.mx[:], l.mx[:], v_(G2), ALU.mult))
                    dve.tensor_tensor(l.mx[:], l.mx[:], v_(B2), ALU.add).then_inc(l.n2_in, 1)
                    chain.link(dve.tensor_tensor(l.h1[:], l.h1[:], v_(BF2), ALU.add))
                    chain.link(dve.tensor_tensor(l.h1[:], l.h1[:], l.h[:], ALU.add))
                for l in L:
                    dve.wait_ge(l.down_out, it + 1)
                    dve.wait_ge(l.stored, it * 32)
                    dve.tensor_tensor(l.o[:].rearrange("p t c -> p (t c)"), l.h1[:].rearrange("p t c -> p (t c)"),
                                      l.ps[0:HT, 3, 0:2 * C], ALU.add).then_inc(l.o_in, 1)
                chain.end()


def more_layouts(a, f):
    import numpy as np

    def tiles(m):
        out = np.zeros((P, 2) + m.shape[1:], np.float32)
        out[:, 0], out[:CT[1], 1] = m[:P], m[P:]
        return out

    def slots(m):
        out = np.zeros(m.shape[:-1] + (NG, HG, SLOT), np.float32)
        out[..., :D] = m.reshape(m.shape[:-1] + (NG, HG, D))
        return out.reshape(m.shape[:-1] + (NG, P))

    def back(m, bias):
        out = slots(m.T)
        if bias is not None:
            out[:, 0, V_ONE] = bias
        return out.transpose(2, 1, 0)

    rows = np.zeros((HG, SLOT), np.float32)
    rows[:, ROW_MAX] = 1
    a["slot_rows"] = rows.reshape(P, 1)
    spread = np.zeros((HG, SLOT, HG, SLOT), np.float32)
    for q in range(HG):
        spread[q, V_ONE, q, :] = 1
    a["spread"] = spread.reshape(P, P)
    qkv, bias = f["L0_attn_qkv_weight"].T, f["L0_attn_qkv_bias"]
    a["a_wq"], a["a_wk"] = tiles(slots(qkv[:, 0:C])), tiles(slots(qkv[:, C:2 * C]))
    a["a_wv"] = tiles(qkv[:, 2 * C:])
    a["a_qb"], a["a_kb"] = slots(bias[0:C]).T, slots(bias[C:2 * C]).T
    a["a_vb"] = np.tile(bias[2 * C:], (P, 2))
    a["a_wo"] = back(f["L0_attn_proj_weight"].T, f["L0_attn_proj_bias"])
    a["m_slots"] = tiles(f["L0_ffn_slot_params"].reshape(C, SLOTS))
    a["m_scale"] = np.tile(f["L0_ffn_scale"].reshape(1, 1), (P, 1))
    a["m_wd"] = tiles(f["L0_ffn_W_down"].transpose(1, 0, 2).reshape(C, C))
    a["m_wu"] = tiles(f["L0_ffn_W_up"].reshape(C, C))
    a["m_bd"] = np.tile(f["L0_ffn_b_down"].reshape(1, C), (SLOTS, 1))
    a["m_bu"] = np.repeat(f["L0_ffn_b_up"], SLOTS // EXPERTS, 0)
    a["m_own"] = np.kron(np.eye(EXPERTS, dtype=np.float32),
                         np.ones((SLOTS // EXPERTS, C // EXPERTS), np.float32))
    p = "L1_attn_"
    a["s_wq"], a["s_wk"] = tiles(slots(f[p + "Wq"])), tiles(slots(f[p + "Wk"]))
    a["s_wv"] = tiles(f[p + "Wv"])
    a["s_qb"], a["s_kb"] = slots(f[p + "bq"]).T, slots(f[p + "bk"]).T
    a["s_vb"] = np.tile(f[p + "bv"], (P, 2))
    a["s_wo"] = back(f[p + "Wo"], None)
    a["s_rows"] = np.stack([np.tile(f[p + n], (P, 2)).reshape(P, 2, C) for n in ("bo", "ln_g", "ln_b")], 1)
    p = "L1_ffn_"
    a["r_wq"], a["r_wk"] = tiles(slots(f[p + "Wq"])), tiles(slots(f[p + "Wk"]))
    a["r_wv"], a["r_wm"], a["r_w1"] = tiles(f[p + "Wv"]), tiles(f[p + "Wm"]), tiles(f[p + "W1"])
    a["r_w2"] = f[p + "W2"].reshape(HIDDEN // P, P, C).transpose(1, 0, 2)
    a["r_qb"], a["r_kb"] = slots(f[p + "bq"]).T, slots(f[p + "bk"]).T
    a["r_vb"] = np.tile(f[p + "bv"], (P, 2))
    a["r_wo"] = back(f[p + "Wo"], f[p + "bo"])
    a["r_b1"] = f[p + "bf1"].reshape(HIDDEN // P, P).T
    a["r_rows"] = np.stack([np.tile(f[p + n], (P, 2)).reshape(P, 2, C)
                            for n in ("g1", "b1", "g2", "b2", "bm", "bf2", "Wr")], 1)
    a["r_br"] = np.tile(f[p + "br"].reshape(1, 1), (P, 1))
    a["rank_ids"] = np.tile(np.arange(ROUTED, dtype=np.float32), (P, 1))
    i, j = np.arange(TP).reshape(2, HT), np.arange(TOK)
    a["earlier"] = (j[None, None, :] < i[:, :, None]).astype(np.float32).transpose(1, 0, 2)


def audio_tower(nc, w, out):
    with ExitStack() as st:
        hres = st.enter_context(nc.sbuf_tensor("hres", [HT, CLIPS, 2, C], F32))
        gmax = st.enter_context(nc.sbuf_tensor("gmax", [P, 2], F32))
        phase_tokenizer(nc, w, hres, gmax)
        phase_attention(nc, w, hres, gmax)
        phase_mixture(nc, w, hres)
        phase_sinkhorn(nc, w, hres)
        phase_routed(nc, w, hres, out)


def layouts(inputs):
    import numpy as np

    f = {k: np.asarray(v) for k, v in inputs.items()}
    a = {"x": f["x"]}
    w0 = np.zeros((COPIES, WTAPS, WIN, CH), np.float32)
    for v in range(WIN):
        w0[:, S0 * v:S0 * v + K0, v, :] = f["L0_tok_cw0"][:, 0, :].T
    a["w0"] = w0.reshape(WK, WIN * CH)
    masks = np.zeros((COPIES, WTAPS, 3), np.float32)
    for c, part in enumerate(W_PART):
        masks[c, :, part] = 1.0
    a["w0_masks"] = masks.reshape(WK, 3)
    cw = [f[f"L0_tok_cw{l}"].transpose(1, 2, 0) for l in range(1, 6)]
    a["cw"] = np.ascontiguousarray(np.concatenate(cw, axis=1))
    a["conv_vecs"] = np.stack([np.stack([f[f"L0_tok_{n}{l}"] for n in ("cb", "gw", "gb")], 1)
                               for l in range(6)], 1)
    a["pw"] = np.ascontiguousarray(f["L0_tok_pw"].T)
    a["pb"] = np.tile(f["L0_tok_pb"], (P, 2))
    a["gavg"] = np.kron(np.eye(CH // GROUP), np.full((GROUP, GROUP), 1 / GROUP)).astype(np.float32)
    a["ident"] = np.eye(P, dtype=np.float32)
    more_layouts(a, f)
    return a


def kernel(**inputs):
    import numpy as _np
    import concourse.bacc as _bacc
    from concourse import mybir as _mybir
    from concourse.bass_utils import run_bass_kernel_spmd as _run

    nc = _bacc.Bacc("TRN2", target_bir_lowering=False, num_devices=1)
    arrays, w = {}, {}
    for name, a in layouts(inputs).items():
        a = _np.ascontiguousarray(a)
        arrays[f"in_{name}"] = a
        w[name] = nc.dram_tensor(f"in_{name}", a.shape, _mybir.dt.from_np(a.dtype), kind="ExternalInput").ap()
    out = nc.dram_tensor("out_h", (CLIPS, TOK, C), F32, kind="ExternalOutput").ap()
    audio_tower(nc, w, out)
    r = _run(nc, [arrays], core_ids=[0])
    return r.results[0]["out_h"]
```

```python
from contextlib import ExitStack

import concourse.bass as bass
from concourse import mybir

ALU = mybir.AluOpType
ACT = mybir.ActivationFunctionType
F32 = mybir.dt.float32
BF16 = mybir.dt.bfloat16
U32 = mybir.dt.uint32
AX_X = mybir.AxisListType.X

CLIPS = 16
SAMPLES = 40000
LANES = (0, 1)
PAIRS = CLIPS // len(LANES)
P = 128
BANK = 512
LANE_BANKS = 4

CH = 128
GROUP = 4
GN_EPS = 1e-5
K0, S0 = 10, 5
LEN0 = (SAMPLES - K0) // S0 + 1
WINDOWS_APART = 3
NORM_APART = 2
CONV0_STAGES = 3
TOKENIZER_LAG = 17
CHUNK_APART = (1, 1, 1, 1, 1, 1)
CONVS = [(3, 2), (3, 2), (3, 2), (3, 2), (2, 2)]
LENS = [LEN0]
for _k, _s in CONVS:
    LENS.append((LENS[-1] - _k) // _s + 1)
TOK = LENS[-1]
HT = 125
TP = 2 * HT
TILE_TOK = (HT, TOK - HT)
ROWS0 = 64
RUN0 = ROWS0 * S0
WIN = 3
WROWS = WIN + 1
WTAPS = WROWS * S0
COPIES = 6
WK = COPIES * WTAPS
WT = HT + 1
WGROUPS = ROWS0 // WIN + 1
XW = (WGROUPS - 1) * WIN * S0 + WTAPS
X_PART = (0, 0, 0, 1, 1, 2)
W_PART = (0, 1, 2, 0, 1, 0)

C = 192
CT = (128, 64)
HEADS = 12
D = C // HEADS
SLOT = 32
HG = P // SLOT
NG = HEADS // HG
LN_EPS = 1e-5


def blocks_of(n, size=500):
    return [(a, min(size, n - a)) for a in range(0, n, size)]


class Chain:

    def __init__(self, eng, sem, per, before=0, spare=None):
        self.eng, self.sem, self.per, self.before, self.n = eng, sem, per, before, 0
        self.turn, self.spare = 0, spare

    def begin(self, turn):
        self.turn, self.n = turn, 0

    def link(self, ins):
        self.n += 1
        ins.then_inc(self.sem, 1)
        self.eng.wait_ge(self.sem, self.turn * self.per + self.before + self.n)

    def link_before_aggregate(self, ins):
        self.link(ins)
        self.eng.memset(self.spare, 0.0)

    def end(self):
        assert self.n == self.per, self.n


def lanes_apart(eng, lanes, stages, count, lag):
    first, second = lanes[:len(lanes) // 2], lanes[len(lanes) // 2:]
    turns = CLIPS // len(lanes)

    def run(group, i, it):
        for l in group:
            stages(i, it, l)

    for i in range(count):
        run(first, i, 0)
        if i >= lag:
            run(second, i - lag, 0)
    turn_2 = eng.alloc_register()
    with eng.Fori(1, turns) as it:
        eng.reg_mov(turn_2, it)
        it_2 = eng.snap(turn_2, min_val=1, max_val=turns - 1)
        for i in range(count):
            run(first, i, it)
            run(second, (i - lag) % count, it_2 if i >= lag else it_2 - 1)
    eng.free_register(turn_2)
    for i in range(count - lag, count):
        run(second, i, turns - 1)


def lanes_ahead(eng, lanes, stages, count, ahead, at):
    turns = CLIPS // len(lanes)

    def run(i, it):
        for l in lanes:
            stages(i, it, l)

    def turn(it, following):
        for i in range(ahead, count):
            if i == at and following is not None:
                for j in range(ahead):
                    run(j, following)
            run(i, it)

    for j in range(ahead):
        run(j, 0)
    with eng.Fori(0, turns - 1) as it:
        turn(it, it + 1)
    turn(turns - 1, None)


class Alloc:

    def __init__(self, nc, stack, tag, all_sems=None):
        self.nc, self.stack, self.tag = nc, stack, tag
        self.all_sems = all_sems
        if all_sems is None:
            self.all_sems = []
            stack.callback(self.clear)

    def clear(self):
        self.nc.clear_and_free_semaphores(self.all_sems)
        self.nc.all_engine_barrier()

    def sb(self, name, shape, dt=F32):
        return self.stack.enter_context(self.nc.sbuf_tensor(self.tag + name, shape, dt))

    def psum(self):
        return self.stack.enter_context(self.nc.psum_tensor(self.tag + "psum", [P, 8, BANK], F32))

    def sem(self, name):
        self.all_sems.append(self.nc.alloc_semaphore(name=self.tag + name))
        return self.all_sems[-1]

    def sems(self, *names):
        return [self.sem(n) for n in names]

    def of_lane(self, lane):
        return Alloc(self.nc, self.stack, f"{self.tag}{lane}_", self.all_sems)


class TokenizerLane:

    def __init__(self, a, ps):
        self.ps = ps
        sizes = [ROWS0 * HT] + LENS[1:-1] + [TP]
        self.h = [a.sb(f"h{i}", [CH, n]) for i, n in enumerate(sizes)]
        self.x = a.sb("x", [HT, XW])
        self.rest = a.sb("rest", [HT, XW])
        self.part = a.sb("part", [HT, 3, XW], BF16)
        self.win = a.sb("win", [HT, WGROUPS, WK], BF16)
        self.winT = a.sb("winT", [WK, WGROUPS, HT], BF16)
        self.stats = a.sb("stats", [CH, 18, 6])
        self.mv = a.sb("mv", [CH, 2])
        self.dev = a.sb("dev", [CH, 2])
        self.var = a.sb("var", [CH, 1])
        self.rstd = a.sb("rstd", [CH, 1])
        self.aff = a.sb("aff", [CH, 3])
        self.lnst = a.sb("lnst", [HT, 2, 6])
        self.lnmv = a.sb("lnmv", [HT, 2, 2])
        self.lnr = a.sb("lnr", [HT, 2])
        self.hx = a.sb("hx", [HT, 2, C])
        self.xn = a.sb("xn", [HT, 2, C])
        self.cm = a.sb("cm", [P, 2])
        self.spare = a.sb("spare", [1, 1])
        self.zeroed, self.x_in, self.x_split = a.sems("zeroed", "x_in", "x_split")
        self.windows, self.window_t, self.conv = a.sems("windows", "window_t", "conv")
        self.seen, self.evac, self.chain = a.sems("seen", "evac", "chain")
        self.stats_in, self.gmean, self.dev_in = a.sems("stats_in", "gmean", "dev_in")
        self.gvar, self.var_in, self.rsqrt = a.sems("gvar", "var_in", "rsqrt")
        self.normed, self.gelu, self.proj = a.sems("normed", "gelu", "proj")
        self.ln_in, self.ln_rstd, self.xn_in = a.sems("ln_in", "ln_rstd", "xn_in")
        self.xn_t, self.cm_done = a.sems("xn_t", "cm_done")


def phase_tokenizer(nc, w, hres, gmax):
    chunks = []
    for layer, n in enumerate(LENS[1:], 1):
        chunks += [(layer, a, m) for a, m in blocks_of(n)]
    first_chunk = {l: min(i for i, c in enumerate(chunks) if c[0] == l) for l in range(1, 6)}
    n_chunks = {l: len(blocks_of(LENS[l])) for l in range(1, 6)}
    pieces = {}
    for l in range(5):
        ends = [min(2 * (a + m - 1) + CONVS[l][0], LENS[l]) for a, m in blocks_of(LENS[l + 1])]
        ends[-1] = LENS[l]
        pieces[l] = list(zip([0] + ends[:-1], ends))
    pieces[5] = [(0, TOK)]
    piece_at, n_pieces = {}, 0
    for l in range(6):
        piece_at[l] = n_pieces
        n_pieces += len(pieces[l])
    conv0 = []
    for v in range(WIN):
        groups = WGROUPS if v == 0 else WGROUPS - 1
        conv0 += [(v, g, min(4, groups - g)) for g in range(0, groups, 4)]
    window_banks = [(0, 8), (8, 8), (16, WGROUPS - 16)]
    n_evac = len(window_banks) + len(conv0) + len(chunks)
    at_conv0 = len(window_banks)
    n_conv = len(conv0) + len(chunks)
    n_stats = {l: len(blocks_of(LENS[l])) for l in range(6)}
    n_stats[0] = len(conv0)
    DVE_LINKS = 4 + 5 * 6 - 6 + 4
    count = 0

    def number(n=1):
        nonlocal count
        count += n
        return count - n

    SPLIT, WINDOWS = number(3), number(WINDOWS_APART)
    CONV, STATS, GROUPS, AFFINE = {}, {}, {}, {}
    CONV[0] = number(CONV0_STAGES)
    for l in range(6):
        if l:
            CONV[l] = number(n_chunks[l] * CHUNK_APART[l])
        STATS[l], GROUPS[l], AFFINE[l] = number(), number(2), number(NORM_APART)
    PROJECT, NORM, NORMED, TRANSPOSE, MAXIMA = (number() for _ in range(5))

    def chunk_at(i, layer):
        c, off = divmod(i - CONV[layer], CHUNK_APART[layer])
        return c if off == 0 and 0 <= c < n_chunks[layer] else None

    per_stage = -(-len(conv0) // CONV0_STAGES)
    conv0_of = lambda i: [(k, conv0[k]) for k in range(len(conv0)) if k // per_stage == i - CONV[0]]

    with ExitStack() as st:
        A = Alloc(nc, st, "tok_")
        psum = A.psum()
        w0_all = A.sb("w0_all", [WK, WIN * CH])
        w0_rest = A.sb("w0_rest", [WK, WIN * CH])
        w0_part = A.sb("w0_part", [WK, 3, WIN * CH], BF16)
        w0 = A.sb("w0", [WK, WIN * CH], BF16)
        cw = A.sb("cw", [CH, 14, CH])
        vecs = A.sb("vecs", [CH, 6, 3])
        pw = A.sb("pw", [CH, C])
        pb = A.sb("pb", [P, 2 * C])
        masks = A.sb("masks", [WK, 3])
        gavg = A.sb("gavg", [CH, CH])
        ident = A.sb("ident", [P, P])
        identb = A.sb("identb", [P, P], BF16)
        half = A.sb("half", [P, 1])
        spare = A.sb("spare", [1, 1])
        loaded, consts, parts, dve_chain = (A.sem(n) for n in ("loaded", "consts", "parts", "dve_chain"))
        L = [TokenizerLane(A.of_lane(lane), psum[:, lane * LANE_BANKS:(lane + 1) * LANE_BANKS, :]) for lane in LANES]
        for lane, l in enumerate(L):
            l.lane = lane
        block = st.enter_context(nc.Block())

        @block.sync
        def _(sp):
            for dst, src in ((w0_all[:], w["w0"]), (masks[:], w["w0_masks"]), (cw[:], w["cw"]),
                             (vecs[:], w["conv_vecs"]), (pw[:], w["pw"]), (pb[:], w["pb"]),
                             (gavg[:], w["gavg"]), (ident[:], w["ident"])):
                sp.dma_start(dst, src).then_inc(loaded, 16)
            for l in L:
                sp.wait_ge(l.zeroed, 2)
            with sp.Fori(0, PAIRS) as it:
                for l in L:
                    sp.wait_ge(l.x_split, it)
                    clip = it * len(LANES) + l.lane
                    src = w["x"][bass.ds(clip, 1), 0:SAMPLES]
                    body = bass.AP(src.tensor, src.offset, [[RUN0, HT - 1], [1, RUN0 + S0]])
                    tail = bass.AP(src.tensor, src.offset + RUN0 * (HT - 1), [[RUN0, 1], [1, RUN0]])
                    sp.dma_start(l.x[0:HT - 1, 0:RUN0 + S0], body).then_inc(l.x_in, 16)
                    sp.dma_start(l.x[HT - 1:HT, 0:RUN0], tail).then_inc(l.x_in, 16)

        @block.gpsimd
        def _(pool):
            pool.memset(half[:], -0.5).then_inc(consts, 1)
            pool.wait_ge(consts, 1)

            def stages(i, it, l):
                for layer in range(6):
                    if i == AFFINE[layer]:
                        pool.wait_ge(l.var_in, it * 6 + layer + 1)
                        pool.tensor_tensor(l.rstd[:], l.var[:], half[0:CH, :], ALU.pow).then_inc(l.rsqrt, 1)
                if i == NORMED:
                    pool.wait_ge(l.ln_in, it + 1)
                    pool.tensor_tensor(l.lnr[:], l.lnmv[:, :, 1], half[0:HT, :].to_broadcast([HT, 2]),
                                       ALU.pow).then_inc(l.ln_rstd, 1)

            lanes_apart(pool, L, stages, count, TOKENIZER_LAG)

        @block.scalar
        def _(act):
            act.wait_ge(loaded, 8 * 16)

            def gelu(it, l, layer, piece):
                if piece < len(pieces[layer]):
                    a, b = pieces[layer][piece]
                    act.activation(l.h[layer][:, a:b], l.h[layer][:, a:b], ACT.Gelu_apprx_tanh,
                                   bias=l.aff[:, 1:2], scale=l.aff[:, 0:1]).then_inc(l.gelu, 1)

            def stages(i, it, l):
                if i == WINDOWS:
                    for b, (g, n) in enumerate(window_banks):
                        act.wait_ge(l.window_t, it * 3 + b + 1)
                        src = l.ps[0:WK, b, :].bitcast(BF16)[:, 0:n * WT].rearrange("k (g t) -> k g t", t=WT)
                        act.activation(l.winT[:, g:g + n, :], src[:, :, 0:HT], ACT.Copy).then_inc(l.evac, 1)
                for k, (v, g, n) in conv0_of(i):
                    act.wait_ge(l.seen, it * len(conv0) + k + 1)
                    dst = l.h[0][:].rearrange("c (p r) -> c r p", r=ROWS0)[
                        :, WIN * g + v:WIN * (g + n - 1) + v + 1:WIN, :]
                    act.activation(dst, l.ps[:, k % 4, 0:n * HT].rearrange("c (g p) -> c g p", p=HT),
                                   ACT.Identity, bias=vecs[:, 0, 0:1]).then_inc(l.evac, 1)
                for layer in range(6):
                    if i == AFFINE[layer]:
                        act.wait_ge(l.normed, it * 6 + layer + 1)
                        gelu(it, l, layer, 0)
                for layer in range(1, 6):
                    c = chunk_at(i, layer)
                    if c is not None:
                        gelu(it, l, layer - 1, c + 1)
                        k = first_chunk[layer] + c
                        _, a, m = chunks[k]
                        act.wait_ge(l.conv, it * n_conv + len(conv0) + k + 1)
                        act.activation(l.h[layer][:, a:a + m], l.ps[:, (len(conv0) + k) % 4, 0:m],
                                       ACT.Identity, bias=vecs[:, layer, 0:1]).then_inc(l.evac, 1)

            lanes_apart(act, L, stages, count, TOKENIZER_LAG)

        @block.tensor
        def _(pe):
            pe.wait_ge(loaded, 8 * 16)
            pe.wait_ge(parts, 2)

            def stages(i, it, l):
                if i == WINDOWS:
                    pe.wait_ge(l.windows, it + 1)
                    pe.wait_ge(l.cm_done, it)
                    for b, (g0, n) in enumerate(window_banks):
                        bank = l.ps[0:WK, b, :].bitcast(BF16)
                        for g in range(n):
                            last = pe.transpose(bank[:, g * WT:g * WT + HT], l.win[:, g0 + g, :],
                                                identb[0:HT, 0:HT])
                        last.then_inc(l.window_t, 1)
                for k, (v, g, n) in conv0_of(i):
                    pe.wait_ge(l.evac, it * n_evac + (at_conv0 if k < 4 else at_conv0 + k - 3))
                    pe.matmul(l.ps[:, k % 4, 0:n * HT], w0[:, v * CH:(v + 1) * CH],
                              l.winT[:, g:g + n, :].rearrange("k g t -> k (g t)"),
                              start=True, stop=True).then_inc(l.conv, 1)
                for layer in range(6):
                    if i == GROUPS[layer]:
                        if layer == 0:
                            pe.wait_ge(l.evac, it * n_evac + at_conv0 + len(conv0))
                        pe.wait_ge(l.stats_in, it * 6 + layer + 1)
                        pe.matmul(l.ps[:, 0, 0:1], gavg[:], l.mv[:, 0:1], start=True, stop=True).then_inc(l.gmean, 1)
                    if i == GROUPS[layer] + 1:
                        pe.wait_ge(l.dev_in, it * 6 + layer + 1)
                        pe.matmul(l.ps[:, 1, 0:1], gavg[:], l.dev[:, 1:2], start=True, stop=True).then_inc(l.gvar, 1)
                for layer in range(1, 6):
                    taps, stride = CONVS[layer - 1]
                    c = chunk_at(i, layer)
                    if c is not None:
                        k = first_chunk[layer] + c
                        _, a, m = chunks[k]
                        j = len(conv0) + k
                        pe.wait_ge(l.evac, it * n_evac + at_conv0 + j - 3)
                        pe.wait_ge(l.gelu, it * n_pieces + piece_at[layer - 1] + c + 1)
                        for t in range(taps):
                            first = stride * a + t
                            rhs = l.h[layer - 1][:, first:first + stride * (m - 1) + 1:stride]
                            last = pe.matmul(l.ps[:, j % 4, 0:m], cw[:, 3 * (layer - 1) + t, :], rhs,
                                             start=(t == 0), stop=(t == taps - 1))
                        last.then_inc(l.conv, 1)
                if i == PROJECT:
                    pe.wait_ge(l.gelu, it * n_pieces + n_pieces)
                    for t in range(2):
                        last = pe.matmul(l.ps[0:HT, 2, t * C:(t + 1) * C], l.h[5][:, t * HT:(t + 1) * HT],
                                         pw[:], start=True, stop=True)
                    last.then_inc(l.proj, 1)
                if i == TRANSPOSE:
                    pe.wait_ge(l.xn_in, it + 1)
                    for t in range(2):
                        for c, rows in enumerate(CT):
                            at = c * TP + t * HT
                            last = pe.transpose(l.ps[0:rows, 3, at:at + HT], l.xn[:, t, c * P:c * P + rows],
                                                ident[0:HT, 0:HT])
                    last.then_inc(l.xn_t, 1)

            lanes_apart(pe, L, stages, count, TOKENIZER_LAG)

        @block.vector
        def _(dve):
            dve.memset(gmax[:], 0.0)
            for l in L:
                dve.memset(l.x[:, RUN0:XW], 0.0).then_inc(l.zeroed, 1)
                dve.memset(l.h[5][:, TOK:TP], 0.0).then_inc(l.zeroed, 1)
            dve.wait_ge(loaded, 8 * 16)
            pre = Chain(dve, dve_chain, 0)
            pre.link(dve.tensor_copy(w0_part[:, 0, :], w0_all[:]))
            pre.link(dve.tensor_tensor(w0_rest[:], w0_all[:], w0_part[:, 0, :], ALU.subtract))
            pre.link(dve.tensor_copy(w0_part[:, 1, :], w0_rest[:]))
            pre.link(dve.tensor_tensor(w0_all[:], w0_rest[:], w0_part[:, 1, :], ALU.subtract))
            pre.link(dve.tensor_copy(w0_part[:, 2, :], w0_all[:]))
            pre.link(dve.tensor_scalar(w0[:], w0_part[:, 0, :], masks[:, 0:1], None, ALU.mult))
            pre.link(dve.scalar_tensor_tensor(w0[:], w0_part[:, 1, :], masks[:, 1:2], w0[:], ALU.mult, ALU.add))
            dve.scalar_tensor_tensor(w0[:], w0_part[:, 2, :], masks[:, 2:3], w0[:], ALU.mult, ALU.add)\
               .then_inc(parts, 1)
            dve.tensor_copy(identb[:], ident[:]).then_inc(parts, 1)
            for l in L:
                l.links = Chain(dve, l.chain, DVE_LINKS, spare=l.spare[:])

            def split_samples(it, l):
                dve.wait_ge(l.x_in, it * 32 + 32)
                dve.wait_ge(l.window_t, it * 3)
                l.links.link(dve.tensor_copy(l.part[:, 0, :], l.x[:]))
                l.links.link(dve.tensor_tensor(l.rest[:], l.x[:], l.part[:, 0, :], ALU.subtract))
                l.links.link(dve.tensor_copy(l.part[:, 1, :], l.rest[:]))
                l.links.link(dve.tensor_tensor(l.rest[:], l.rest[:], l.part[:, 1, :], ALU.subtract))
                dve.tensor_copy(l.part[:, 2, :], l.rest[:]).then_inc(l.x_split, 1)
                dve.wait_ge(l.x_split, it + 1)
                for c, part in enumerate(X_PART):
                    src = l.part[:, part, :]
                    src = bass.AP(src.tensor, src.offset, [list(src.ap[0]), [WIN * S0, WGROUPS], [1, WTAPS]])
                    last = dve.tensor_copy(l.win[:, :, c * WTAPS:(c + 1) * WTAPS], src)
                last.then_inc(l.windows, 1)

            def stages(i, it, l):
                l.links.turn = it
                if i == SPLIT:
                    l.links.begin(it)
                    split_samples(it, l)
                for k, (v, g, n) in conv0_of(i):
                    dve.wait_ge(l.conv, it * n_conv + k + 1)
                    real = n * HT - (WIN * (g + n - 1) + v == ROWS0 - 1)
                    l.last = dve.bn_stats(l.stats[:, k, :], l.ps[:, k % 4, 0:real]).then_inc(l.seen, 1)
                for layer in range(1, 6):
                    c = chunk_at(i, layer)
                    if c is not None:
                        _, a, m = chunks[first_chunk[layer] + c]
                        dve.wait_ge(l.evac, it * n_evac + at_conv0 + len(conv0) + first_chunk[layer] + c + 1)
                        l.last = dve.bn_stats(l.stats[:, c, :], l.h[layer][:, a:a + m])
                        if c == n_chunks[layer] - 1:
                            l.links.link_before_aggregate(l.last)
                            dve.bn_aggr(l.mv[:], l.stats[:, 0:n_stats[layer], :]).then_inc(l.stats_in, 1)
                if i == STATS[0]:
                    dve.wait_ge(l.seen, (it + 1) * len(conv0))
                    dve.memset(l.spare[:], 0.0)
                    l.links.link(dve.bn_aggr(l.mv[:], l.stats[:, 0:n_stats[0], :]))
                    dve.tensor_tensor(l.mv[:, 0:1], l.mv[:, 0:1], vecs[:, 0, 0:1], ALU.add).then_inc(l.stats_in, 1)
                for layer in range(6):
                    if i == GROUPS[layer]:
                        dve.wait_ge(l.gmean, it * 6 + layer + 1)
                        dve.wait_ge(l.stats_in, it * 6 + layer + 1)
                        l.links.link(dve.tensor_tensor(l.dev[:, 0:1], l.mv[:, 0:1], l.ps[:, 0, 0:1], ALU.subtract))
                        dve.scalar_tensor_tensor(l.dev[:, 1:2], l.dev[:, 0:1], l.dev[:, 0:1], l.mv[:, 1:2],
                                                 ALU.mult, ALU.add).then_inc(l.dev_in, 1)
                    if i == GROUPS[layer] + 1:
                        dve.wait_ge(l.gvar, it * 6 + layer + 1)
                        dve.tensor_scalar(l.var[:], l.ps[:, 1, 0:1], GN_EPS, None, ALU.add).then_inc(l.var_in, 1)
                        l.links.link(dve.tensor_scalar(l.aff[:, 2:3], l.ps[:, 0, 0:1], -1.0, None, ALU.mult))
                    if i == AFFINE[layer]:
                        dve.wait_ge(l.rsqrt, it * 6 + layer + 1)
                        l.links.link(dve.tensor_tensor(l.aff[:, 0:1], l.rstd[:], vecs[:, layer, 1:2], ALU.mult))
                        dve.scalar_tensor_tensor(l.aff[:, 1:2], l.aff[:, 0:1], l.aff[:, 2:3], vecs[:, layer, 2:3],
                                                 ALU.mult, ALU.add).then_inc(l.normed, 1)
                if i == NORM:
                    dve.wait_ge(l.proj, it + 1)
                    clip = it * len(LANES) + l.lane
                    dve.tensor_tensor(hres[:, bass.ds(clip, 1), :, :].rearrange("p b t c -> p (b t c)"),
                                      l.ps[0:HT, 2, 0:2 * C], pb[0:HT, :], ALU.add)
                    l.links.link(dve.tensor_tensor(l.hx[:].rearrange("p t c -> p (t c)"),
                                                       l.ps[0:HT, 2, 0:2 * C], pb[0:HT, :], ALU.add))
                    for t in range(2):
                        last = dve.bn_stats(l.lnst[:, t, :], l.hx[:, t, :])
                    l.links.link_before_aggregate(last)
                    for t in range(2):
                        last = dve.bn_aggr(l.lnmv[:, t, :], l.lnst[:, t, :])
                    l.links.link(last)
                    dve.tensor_scalar(l.lnmv[:, :, 1], l.lnmv[:, :, 1], LN_EPS, None, ALU.add).then_inc(l.ln_in, 1)
                if i == NORMED:
                    dve.wait_ge(l.ln_rstd, it + 1)
                    for t in range(2):
                        last = dve.tensor_scalar(l.xn[:, t, :], l.hx[:, t, :], l.lnmv[:, t, 0:1], l.lnr[:, t:t + 1],
                                                 ALU.subtract, ALU.mult)
                    last.then_inc(l.xn_in, 1)
                if i == MAXIMA:
                    dve.wait_ge(l.xn_t, it + 1)
                    for c, rows in enumerate(CT):
                        last = dve.tensor_reduce(l.cm[0:rows, c:c + 1], l.ps[0:rows, 3, c * TP:c * TP + TOK],
                                                 AX_X, ALU.max, apply_absolute_value=True)
                    l.links.link(last)
                    for c, rows in enumerate(CT):
                        last = dve.tensor_tensor(gmax[0:rows, c:c + 1], gmax[0:rows, c:c + 1],
                                                 l.cm[0:rows, c:c + 1], ALU.max)
                    last.then_inc(l.cm_done, 1)
                    l.links.end()

            lanes_apart(dve, L, stages, count, TOKENIZER_LAG)


V_ONE = D


def pe_transpose_tokens(pe, l, src, ident, banks=(0, 1)):
    for t in range(2):
        for c, rows in enumerate(CT):
            last = pe.transpose(l.ps[0:rows, banks[c], t * HT:(t + 1) * HT], src[:, t, c * P:c * P + rows],
                                ident[0:HT, 0:HT])
    return last


def pe_project_padded(pe, l, wt, out_banks):
    for g in range(NG):
        for c, rows in enumerate(CT):
            b, at = out_banks[g]
            last = pe.matmul(l.ps[:, b, at:at + TP], wt[0:rows, c, g, :], l.xt[0:rows, c, :],
                             start=(c == 0), stop=(c == 1))
    return last


def pe_project_values(pe, l, wt, bank):
    for t in range(2):
        for c, rows in enumerate(CT):
            last = pe.matmul(l.ps[0:HT, bank, t * C:(t + 1) * C], l.xt[0:rows, c, t * HT:(t + 1) * HT],
                             wt[0:rows, c, :], start=(c == 0), stop=(c == 1))
    return last


UNIT = 2
UNITS = HEADS // UNIT


def heads_of(u):
    return [(h // HG, h % HG, h) for h in range(UNIT * u, UNIT * (u + 1))]


def unit_banks(l, u):
    hq = heads_of(u)[0][1]
    return l.ps[0:HT, hq:hq + UNIT, 0:2 * TP]


def unit_of(dst, u):
    g, hq, _ = heads_of(u)[0]
    return dst[:, g, hq:hq + UNIT, :, :].rearrange("p q t i -> p q (t i)")


def pe_scores(pe, l, u):
    for g, hq, h in heads_of(u):
        for t in range(2):
            last = pe.matmul(l.ps[0:HT, hq, t * TP:(t + 1) * TP], l.q[:, g, t * HT:(t + 1) * HT],
                             l.kpad[:, h, :], start=True, stop=True)
    return last


def pe_transpose_scores(pe, l, u, src, ident):
    for g, hq, h in heads_of(u):
        for t in range(2):
            for v in range(2):
                last = pe.transpose(l.ps[0:HT, hq, v * TP + t * HT:v * TP + (t + 1) * HT],
                                    src[:, g, hq, t, v * HT:(v + 1) * HT], ident[0:HT, 0:HT])
    return last


def pe_column_sums(pe, l, col, k):
    for g in range(NG):
        for t, n in enumerate(TILE_TOK):
            for hq in range(HG):
                h = HG * g + hq
                last = pe.matmul(l.ps[SLOT * hq:SLOT * (hq + 1), g, 0:TP],
                                 col[0:n, t, h:h + 1].to_broadcast([n, SLOT]), k[0:n, g, hq, t, :],
                                 start=(t == 0), stop=(t == 1), skip_group_check=True)
    return last


def pe_columns_to_rows(pe, l, col, ident, banks):
    for g in range(NG):
        b, at = banks[g]
        for t in range(2):
            for hq in range(HG):
                h = HG * g + hq
                last = pe.matmul(l.ps[SLOT * hq:SLOT * (hq + 1), b, at + t * HT:at + (t + 1) * HT],
                                 col[:, t, h:h + 1].to_broadcast([HT, SLOT]), ident[0:HT, 0:HT],
                                 start=True, stop=True, skip_group_check=True)
    return last


def act_unit_exp(act, l, u, dst, shift, shifts_in, before, sums=None):
    for g, hq, h in heads_of(u):
        act.wait_ge(shifts_in, before + h + 1)
        for t in range(2):
            acc = {} if sums is None else {"accum_out": sums[:, t, h:h + 1]}
            last = act.activation(dst[:, g, hq, t, 0:TOK], l.ps[0:HT, hq, t * TP:t * TP + TOK], ACT.Exp,
                                  bias=shift[:, t, h:h + 1], **acc)
    return last


def dve_unit_max(dve, l, u, dst, done):
    for g, hq, h in heads_of(u):
        src = l.ps[0:HT, hq, 0:2 * TP].rearrange("p (t j) -> p t j", t=2)[:, :, 0:TOK]
        dve.tensor_reduce(dst[:, :, h], src, AX_X, ALU.max, negate=True).then_inc(done, 1)


def dve_copy_unit(dve, l, u, dst):
    return dve.tensor_copy(unit_of(dst, u), unit_banks(l, u))


def act_copy_unit(act, l, u, dst):
    return act.activation(unit_of(dst, u), unit_banks(l, u), ACT.Copy)


BANKS_ROWS = ((1, 0), (1, TP), (2, 0))


def act_rows(act, l, dst):
    act.activation(dst[:, 0:2, :], l.ps[:, 1, 0:2 * TP].rearrange("p (g i) -> p g i", g=2), ACT.Copy)
    return act.activation(dst[:, 2, :], l.ps[:, 2, 0:TP], ACT.Copy)


def pe_weighted_sum(pe, l, vals, e, width=TP):
    for g in range(NG):
        for t, keys in enumerate(TILE_TOK):
            for hq in range(HG):
                last = pe.matmul(l.ps[SLOT * hq:SLOT * (hq + 1), g, 0:width], vals[0:keys, t, HG * g + hq, :],
                                 e[0:keys, g, hq, t, :], start=(t == 0), stop=(t == 1), skip_group_check=True)
    return last


def pe_project_back(pe, l, ctx, wt, bank):
    for t in range(2):
        for g in range(NG):
            last = pe.matmul(l.ps[0:HT, bank, t * C:(t + 1) * C], ctx[:, g, t * HT:(t + 1) * HT], wt[:, g, :],
                             start=(g == 0), stop=(g == NG - 1))
    return last


def dve_read(dve, l, hres, clip):
    return dve.tensor_scalar(l.h[:].rearrange("p t c -> p (t c)"),
                             hres[:, bass.ds(clip, 1), :, :].rearrange("p b t c -> p (b t c)"), 1.0, None, ALU.mult)


def dve_norm_stats(dve, chain, l, src, eps, sem):
    for t in range(2):
        last = dve.bn_stats(l.lnst[:, t, :], src[:, t, :])
    chain.link_before_aggregate(last)
    for t in range(2):
        last = dve.bn_aggr(l.lnmv[:, t, :], l.lnst[:, t, :])
    chain.link(last)
    dve.tensor_scalar(l.lnmv[:, :, 1], l.lnmv[:, :, 1], eps, None, ALU.add).then_inc(sem, 1)


def dve_norm_apply(dve, l, dst, src):
    for t in range(2):
        last = dve.tensor_scalar(dst[:, t, :], src[:, t, :], l.lnmv[:, t, 0:1], l.lnr[:, t:t + 1],
                                 ALU.subtract, ALU.mult)
    return last


def pool_rstd(pool, l, half):
    return pool.tensor_tensor(l.lnr[:], l.lnmv[:, :, 1], half[0:HT, 0:1].to_broadcast([HT, 2]), ALU.pow)


def act_keys(act, l, bias, banks):
    for g in range(NG):
        b, at = banks[g]
        for hq in range(HG):
            rows = slice(SLOT * hq, SLOT * (hq + 1))
            last = act.activation(l.kpad[rows, HG * g + hq, :], l.ps[rows, b, at:at + TP], ACT.Identity,
                                  bias=bias[rows, g:g + 1])
    return last


def dve_queries(dve, l, bias, banks, scale):
    for g in range(NG):
        b, at = banks[g]
        last = dve.tensor_scalar(l.q[:, g, :], l.ps[:, b, at:at + TP], scale, bias[:, g:g + 1], ALU.mult, ALU.add)
    return last


def dve_values(dve, l, bias, bank):
    return dve.tensor_tensor(l.v[:, :, :, 0:D],
                             l.ps[0:HT, bank, 0:2 * C].rearrange("p (t h d) -> p t h d", t=2, d=D),
                             bias[0:HT, :].rearrange("p (t h d) -> p t h d", t=2, d=D), ALU.add)


def load_all(sp, pairs, sem):
    for dst, src in pairs:
        sp.dma_start(dst, src).then_inc(sem, 16)


BANKS_Q = ((2, 0), (2, TP), (3, 0))
BANKS_K = ((0, 0), (0, TP), (1, 0))
ALPHA = 0.35
ATTENTION_LAG = 5


class AttentionLane:

    def __init__(self, a, ps):
        self.ps = ps
        self.h = a.sb("h", [HT, 2, C])
        self.lnst = a.sb("lnst", [HT, 2, 6])
        self.lnmv = a.sb("lnmv", [HT, 2, 2])
        self.lnr = a.sb("lnr", [HT, 2])
        self.xn = a.sb("xn", [HT, 2, C])
        self.xt = a.sb("xt", [P, 2, TP])
        self.q = a.sb("q", [P, NG, TP])
        self.kpad = a.sb("kpad", [P, HEADS, TP])
        self.v = a.sb("v", [HT, 2, HEADS, SLOT])
        self.neg = a.sb("neg", [HT, 2, HEADS])
        self.den = a.sb("den", [HT, 2, HEADS])
        self.eq = a.sb("eq", [HT, NG, HG, 2, TP])
        self.e = a.sb("e", [HT, NG, HG, 2, TP])
        self.ctx = a.sb("ctx", [P, NG, TP])
        self.rden = a.sb("rden", [P, NG, TP])
        self.spare = a.sb("spare", [1, 1])
        self.ln_in, self.ln_rstd, self.xn_in = a.sems("ln_in", "ln_rstd", "xn_in")
        self.xn_t, self.xt_in, self.q_out = a.sems("xn_t", "xt_in", "q_out")
        self.k_out, self.v_out, self.q_in = a.sems("k_out", "v_out", "q_in")
        self.k_in, self.v_in, self.s_out = a.sems("k_in", "v_in", "s_out")
        self.s_max, self.eq_in, self.e_out = a.sems("s_max", "eq_in", "e_out")
        self.e_in_even, self.e_in_odd, self.den_in = a.sems("e_in_even", "e_in_odd", "den_in")
        self.den_out, self.rden_in, self.pv_out = a.sems("den_out", "rden_in", "pv_out")
        self.ctx_in, self.proj_out, self.zeroed = a.sems("ctx_in", "proj_out", "zeroed")
        self.chain, self.h_done = a.sems("chain", "h_done")


def phase_attention(nc, w, hres, gmax):
    DVE_LINKS = 3
    READ, NORMED, TRANSPOSE, PROJECT, VALUES = range(5)
    SCORES = VALUES + 1
    TURNED = SCORES + UNITS
    ROWS = TURNED + UNITS
    WEIGHTED, BACK = ROWS + 1, ROWS + 2
    count = BACK + 1
    with ExitStack() as st:
        A = Alloc(nc, st, "att_")
        psum = A.psum()
        wq, wk = (A.sb(n, [P, 2, NG, P]) for n in ("wq", "wk"))
        wv = A.sb("wv", [P, 2, C])
        wo = A.sb("wo", [P, NG, C])
        vb = A.sb("vb", [P, 2 * C])
        qb, kb = A.sb("qb", [P, NG]), A.sb("kb", [P, NG])
        ident = A.sb("ident", [P, P])
        half = A.sb("half", [P, 1])
        expo = A.sb("expo", [P, 2])
        wmax = A.sb("wmax", [P, 2, 3])
        cs = A.sb("cs", [P, 2, 6])
        inv_cs = A.sb("inv_cs", [P, 2])
        loaded, consts, ready, dve_chain, wmax_in, ratio_in = (
            A.sem(n) for n in ("loaded", "consts", "ready", "dve_chain", "wmax_in", "ratio_in"))
        L = [AttentionLane(A.of_lane(lane), psum[:, lane * LANE_BANKS:(lane + 1) * LANE_BANKS, :]) for lane in LANES]
        for lane, l in enumerate(L):
            l.lane = lane
        block = st.enter_context(nc.Block())

        @block.sync
        def _(sp):
            load_all(sp, ((wq[:], w["a_wq"]), (wk[:], w["a_wk"]), (wv[:], w["a_wv"]), (wo[:], w["a_wo"]),
                          (vb[:], w["a_vb"]), (qb[:], w["a_qb"]), (kb[:], w["a_kb"]),
                          (ident[:], w["ident"])), loaded)

        @block.gpsimd
        def _(pool):
            pool.memset(half[:], -0.5).then_inc(consts, 1)
            pool.memset(expo[:, 0:1], ALPHA).then_inc(consts, 1)
            pool.memset(expo[:, 1:2], 1.0 - ALPHA).then_inc(consts, 1)
            pool.wait_ge(consts, 3)
            pool.wait_ge(wmax_in, 2)
            for c, n in enumerate(CT):
                pool.tensor_tensor(cs[0:n, c, 0:1], gmax[0:n, c:c + 1], expo[0:n, 0:1], ALU.pow).then_inc(ratio_in, 1)
                pool.tensor_tensor(cs[0:n, c, 1:2], wmax[0:n, c, 2:3], expo[0:n, 1:2], ALU.pow).then_inc(ratio_in, 1)

            def stages(i, it, l):
                if i == READ:
                    pool.wait_ge(l.ln_in, it + 1)
                    pool_rstd(pool, l, half).then_inc(l.ln_rstd, 1)

            lanes_apart(pool, L, stages, count, ATTENTION_LAG)

        @block.tensor
        def _(pe):
            pe.wait_ge(loaded, 8 * 16)
            pe.wait_ge(ready, 2)
            for l in L:
                pe.wait_ge(l.zeroed, 4)

            def stages(i, it, l):
                if i == TRANSPOSE:
                    pe.wait_ge(l.xn_in, it + 1)
                    pe.wait_ge(l.h_done, it)
                    pe_transpose_tokens(pe, l, l.xn, ident).then_inc(l.xn_t, 1)
                if i == PROJECT:
                    pe.wait_ge(l.xt_in, it * 2 + 2)
                    pe_project_padded(pe, l, wq, BANKS_Q).then_inc(l.q_out, 1)
                    pe_project_padded(pe, l, wk, BANKS_K).then_inc(l.k_out, 1)
                if i == VALUES:
                    pe.wait_ge(l.q_in, it + 1)
                    pe_project_values(pe, l, wv, 2).then_inc(l.v_out, 1)
                u = i - SCORES
                if 0 <= u < UNITS:
                    if u == 0:
                        pe.wait_ge(l.k_in, it + 1)
                        pe.wait_ge(l.v_in, it + 1)
                    elif u > 1:
                        pe.wait_ge(l.eq_in, it * UNITS + u - 1)
                    pe_scores(pe, l, u).then_inc(l.s_out, 1)
                u = i - TURNED
                if 0 <= u < UNITS:
                    pe.wait_ge(l.eq_in, it * UNITS + UNITS)
                    if u > 1:
                        pe.wait_ge(l.e_in_odd if u % 2 else l.e_in_even, it * (UNITS // 2) + u // 2)
                    pe_transpose_scores(pe, l, u, l.eq, ident).then_inc(l.e_out, 1)
                if i == ROWS:
                    pe.wait_ge(l.den_in, it + 1)
                    for half in (l.e_in_even, l.e_in_odd):
                        pe.wait_ge(half, (it + 1) * (UNITS // 2))
                    pe_columns_to_rows(pe, l, l.den, ident, BANKS_ROWS).then_inc(l.den_out, 1)
                if i == WEIGHTED:
                    pe.wait_ge(l.rden_in, it + 1)
                    pe_weighted_sum(pe, l, l.v, l.e).then_inc(l.pv_out, 1)
                if i == BACK:
                    pe.wait_ge(l.ctx_in, it + 1)
                    pe_project_back(pe, l, l.ctx, wo, 3).then_inc(l.proj_out, 1)

            lanes_apart(pe, L, stages, count, ATTENTION_LAG)

        @block.scalar
        def _(act):
            act.wait_ge(ready, 2)
            for l in L:
                act.wait_ge(l.zeroed, 4)

            def stages(i, it, l):
                if i == TRANSPOSE:
                    act.wait_ge(l.xn_t, it + 1)
                    for c, n in enumerate(CT):
                        act.activation(l.xt[0:n, c, :], l.ps[0:n, c, 0:TP], ACT.Copy, scale=inv_cs[0:n, c:c + 1])\
                           .then_inc(l.xt_in, 1)
                if i == PROJECT:
                    act.wait_ge(l.k_out, it + 1)
                    act_keys(act, l, kb, BANKS_K).then_inc(l.k_in, 1)
                u = i - SCORES
                if 0 <= u < UNITS:
                    act_unit_exp(act, l, u, l.eq, l.neg, l.s_max, it * HEADS, l.den).then_inc(l.eq_in, 1)
                u = i - TURNED
                if 0 <= u < UNITS:
                    if u % 2:
                        act.wait_ge(l.e_out, it * UNITS + u + 1)
                        act_copy_unit(act, l, u, l.e).then_inc(l.e_in_odd, 1)
                if i == ROWS:
                    act.wait_ge(l.den_out, it + 1)
                    act_rows(act, l, l.rden).then_inc(l.rden_in, 1)

            lanes_apart(act, L, stages, count, ATTENTION_LAG)

        @block.vector
        def _(dve):
            for l in L:
                dve.memset(l.kpad[:], 0.0).then_inc(l.zeroed, 1)
                dve.memset(l.eq[:, :, :, :, TOK:TP], 1.0).then_inc(l.zeroed, 1)
                dve.memset(l.v[:, :, :, D + 1:SLOT], 0.0).then_inc(l.zeroed, 1)
                dve.memset(l.v[:, :, :, V_ONE], 1.0).then_inc(l.zeroed, 1)
            dve.wait_ge(loaded, 8 * 16)
            pre = Chain(dve, dve_chain, 0)
            for c, n in enumerate(CT):
                for j, part in enumerate((wq[0:n, c, :, :].rearrange("p g m -> p (g m)"),
                                          wk[0:n, c, :, :].rearrange("p g m -> p (g m)"), wv[0:n, c, :])):
                    last = dve.tensor_reduce(wmax[0:n, c, j:j + 1], part, AX_X, ALU.max, apply_absolute_value=True)
                pre.link(last)
                pre.link(dve.tensor_tensor(wmax[0:n, c, 0:1], wmax[0:n, c, 0:1], wmax[0:n, c, 1:2], ALU.max))
                dve.tensor_tensor(wmax[0:n, c, 2:3], wmax[0:n, c, 2:3], wmax[0:n, c, 0:1], ALU.max).then_inc(wmax_in, 1)
            dve.wait_ge(ratio_in, 4)
            for c, n in enumerate(CT):
                r = lambda j: cs[0:n, c, j:j + 1]
                pre.link(dve.reciprocal(r(1), r(1)))
                pre.link(dve.tensor_tensor(r(0), r(0), r(1), ALU.mult))
                pre.link(dve.tensor_scalar(r(2).bitcast(U32), r(0).bitcast(U32), 0x7F800000, None, ALU.bitwise_and))
                pre.link(dve.tensor_tensor(r(3), r(0), r(2), ALU.subtract))
                pre.link(dve.scalar_tensor_tensor(r(4), r(2), 2.0, r(0), ALU.mult, ALU.subtract))
                pre.link(dve.tensor_tensor(r(5), r(3), r(4), ALU.is_gt))
                pre.link(dve.scalar_tensor_tensor(r(3), r(5), 1.0, r(2), ALU.add, ALU.mult))
                for part in (wq[0:n, c, :, :].rearrange("p g m -> p (g m)"),
                             wk[0:n, c, :, :].rearrange("p g m -> p (g m)"), wv[0:n, c, :]):
                    last = dve.tensor_scalar(part, part, r(3), None, ALU.mult)
                pre.link(dve.reciprocal(inv_cs[0:n, c:c + 1], r(3)))
            dve.tensor_scalar(qb[:], qb[:], D ** -0.5, None, ALU.mult).then_inc(ready, 2)
            dve.wait_ge(ready, 2)
            for l in L:
                l.links = Chain(dve, l.chain, DVE_LINKS, spare=l.spare[:])

            def stages(i, it, l):
                l.links.turn = it
                if i == READ:
                    l.links.begin(it)
                    l.links.link(dve_read(dve, l, hres, it * len(LANES) + l.lane))
                    dve_norm_stats(dve, l.links, l, l.h, LN_EPS, l.ln_in)
                if i == NORMED:
                    dve.wait_ge(l.ln_rstd, it + 1)
                    dve_norm_apply(dve, l, l.xn, l.h).then_inc(l.xn_in, 1)
                if i == PROJECT:
                    dve.wait_ge(l.q_out, it + 1)
                    dve_queries(dve, l, qb, BANKS_Q, D ** -0.5).then_inc(l.q_in, 1)
                if i == VALUES:
                    dve.wait_ge(l.v_out, it + 1)
                    dve_values(dve, l, vb, 2).then_inc(l.v_in, 1)
                u = i - SCORES
                if 0 <= u < UNITS:
                    dve.wait_ge(l.s_out, it * UNITS + u + 1)
                    dve_unit_max(dve, l, u, l.neg, l.s_max)
                u = i - TURNED
                if 0 <= u < UNITS and u % 2 == 0:
                    dve.wait_ge(l.e_out, it * UNITS + u + 1)
                    dve_copy_unit(dve, l, u, l.e).then_inc(l.e_in_even, 1)
                if u == 0:
                    dve.wait_ge(l.eq_in, it * UNITS + UNITS)
                    dve.reciprocal(l.den[:], l.den[:]).then_inc(l.den_in, 1)
                if i == WEIGHTED:
                    dve.wait_ge(l.pv_out, it + 1)
                    dve.wait_ge(l.rden_in, it + 1)
                    dve.tensor_tensor(l.ctx[:], l.ps[:, 0:NG, 0:TP], l.rden[:], ALU.mult).then_inc(l.ctx_in, 1)
                if i == BACK:
                    dve.wait_ge(l.proj_out, it + 1)
                    clip = it * len(LANES) + l.lane
                    dve.tensor_tensor(hres[:, bass.ds(clip, 1), :, :].rearrange("p b t c -> p (b t c)"),
                                      l.h[:].rearrange("p t c -> p (t c)"), l.ps[0:HT, 3, 0:2 * C],
                                      ALU.add).then_inc(l.h_done, 1)
                    dve.wait_ge(l.h_done, it + 1)
                    l.links.end()

            lanes_apart(dve, L, stages, count, ATTENTION_LAG)




EXPERTS = 8
SLOTS = 32
L2_EPS = 1e-6
MIXTURE_LAG = 6
MIXTURE_LANES = 4


class MixtureLane:

    def __init__(self, a, ps):
        self.ps = ps
        self.h = a.sb("h", [HT, 2, C])
        self.lnst = a.sb("lnst", [HT, 2, 6])
        self.lnmv = a.sb("lnmv", [HT, 2, 2])
        self.lnr = a.sb("lnr", [HT, 2])
        self.xn = a.sb("xn", [HT, 2, C])
        self.xt = a.sb("xt", [P, 2, TP])
        self.sq = a.sb("sq", [HT, 2, C])
        self.nsq = a.sb("nsq", [HT, 2])
        self.nrm = a.sb("nrm", [HT, 2])
        self.cmax = a.sb("cmax", [HT, 2])
        self.csum = a.sb("csum", [HT, 2])
        self.comb = a.sb("comb", [HT, 2, SLOTS])
        self.dmax = a.sb("dmax", [SLOTS, 1])
        self.dsum = a.sb("dsum", [SLOTS, 1])
        self.disp = a.sb("disp", [SLOTS, TP])
        self.combT = a.sb("combT", [SLOTS, TP])
        self.dispT = a.sb("dispT", [HT, 2, SLOTS])
        self.xs = a.sb("xs", [P, 2, SLOTS])
        self.spare = a.sb("spare", [1, 1])
        self.hid = a.sb("hid", [SLOTS, C])
        self.hidT = a.sb("hidT", [P, 2, SLOTS])
        self.ys = a.sb("ys", [SLOTS, C])
        self.ln_in, self.ln_rstd, self.squares_in = a.sems("ln_in", "ln_rstd", "squares_in")
        self.norm_in, self.xn_in, self.xn_t = a.sems("norm_in", "xn_in", "xn_t")
        self.xt_in, self.logits, self.maxima = a.sems("xt_in", "logits", "maxima")
        self.exps, self.weights, self.weights_t = a.sems("exps", "weights", "weights_t")
        self.combT_in, self.dispT_in, self.slots_out = a.sems("combT_in", "dispT_in", "slots_out")
        self.xs_in, self.hid_out, self.hid_in = a.sems("xs_in", "hid_out", "hid_in")
        self.gelu_in, self.own_in, self.own_t = a.sems("gelu_in", "own_in", "own_t")
        self.hidT_in, self.ys_out, self.ys_in = a.sems("hidT_in", "ys_out", "ys_in")
        self.y_out, self.zeroed, self.chain = a.sems("y_out", "zeroed", "chain")
        self.h_done = a.sem("h_done")


def phase_mixture(nc, w, hres):
    DVE_LINKS = 7
    (READ, NORMED, SCALED, TRANSPOSE, LOGITS, WEIGHTS, TURNED, SLOT_INPUTS, HIDDEN_UNITS, OWN, BACK, ADD) = range(12)
    count = ADD + 1
    with ExitStack() as st:
        A = Alloc(nc, st, "mix_")
        psum = A.psum()
        sp_w = A.sb("slots", [P, 2, SLOTS])
        sq_w = A.sb("slots_sq", [P, 2, SLOTS])
        nrm_w = A.sb("slots_norm", [P, 2, SLOTS // EXPERTS])
        scale = A.sb("scale", [P, 1])
        wd, wu = A.sb("wd", [P, 2, C]), A.sb("wu", [P, 2, C])
        bd, bu, own = (A.sb(n, [SLOTS, C]) for n in ("bd", "bu", "own"))
        ident = A.sb("ident", [P, P])
        half = A.sb("half", [P, SLOTS + 1])
        loaded, consts, dve_chain, sums_in, roots, slots_in = (
            A.sem(n) for n in ("loaded", "consts", "dve_chain", "sums_in", "roots", "slots_in"))
        L = [MixtureLane(A.of_lane(lane), psum[:, 2 * lane:2 * lane + 2, :]) for lane in range(MIXTURE_LANES)]
        for lane, l in enumerate(L):
            l.lane = lane
        block = st.enter_context(nc.Block())

        @block.sync
        def _(sp):
            load_all(sp, ((sp_w[:], w["m_slots"]), (scale[:], w["m_scale"]), (wd[:], w["m_wd"]),
                          (wu[:], w["m_wu"]), (bd[:], w["m_bd"]), (bu[:], w["m_bu"]), (own[:], w["m_own"]),
                          (ident[:], w["ident"])), loaded)

        @block.gpsimd
        def _(pool):
            pool.memset(half[:, 0:SLOTS], 0.5).then_inc(consts, 1)
            pool.memset(half[:, SLOTS:SLOTS + 1], -0.5).then_inc(consts, 1)
            pool.wait_ge(consts, 2)
            pool.wait_ge(sums_in, 1)
            nrm = nrm_w[:].rearrange("d c p -> d (c p)")
            pool.tensor_tensor(nrm, nrm, half[:, 0:2 * (SLOTS // EXPERTS)], ALU.pow).then_inc(roots, 1)

            def stages(i, it, l):
                if i == READ:
                    pool.wait_ge(l.ln_in, it + 1)
                    pool_rstd(pool, l, half[:, SLOTS:SLOTS + 1]).then_inc(l.ln_rstd, 1)
                if i == NORMED:
                    pool.wait_ge(l.squares_in, it + 1)
                    pool.tensor_tensor(l.nrm[:], l.nsq[:], half[0:HT, 0:2], ALU.pow).then_inc(l.norm_in, 1)

            lanes_apart(pool, L, stages, count, MIXTURE_LAG)

        @block.tensor
        def _(pe):
            pe.wait_ge(loaded, 8 * 16)
            pe.wait_ge(slots_in, 1)
            for l in L:
                pe.wait_ge(l.zeroed, 1)

            def stages(i, it, l):
                if i == TRANSPOSE:
                    pe.wait_ge(l.xn_in, it + 1)
                    pe.wait_ge(l.h_done, it)
                    pe_transpose_tokens(pe, l, l.xn, ident).then_inc(l.xn_t, 1)
                if i == LOGITS:
                    pe.wait_ge(l.xt_in, it * 2 + 2)
                    for t in range(2):
                        for c, n in enumerate(CT):
                            pe.matmul(l.ps[0:HT, 0, t * SLOTS:(t + 1) * SLOTS], l.xt[0:n, c, t * HT:(t + 1) * HT],
                                      sp_w[0:n, c, :], start=(c == 0), stop=(c == 1))
                    for c, n in enumerate(CT):
                        last = pe.matmul(l.ps[0:SLOTS, 1, 0:TP], sp_w[0:n, c, :], l.xt[0:n, c, :],
                                         start=(c == 0), stop=(c == 1))
                    last.then_inc(l.logits, 1)
                if i == TURNED:
                    pe.wait_ge(l.weights, it * 2 + 2)
                    for t in range(2):
                        pe.transpose(l.ps[0:SLOTS, 0, t * HT:(t + 1) * HT], l.comb[:, t, :], ident[0:HT, 0:HT])
                    for t in range(2):
                        last = pe.transpose(l.ps[0:HT, 1, t * SLOTS:(t + 1) * SLOTS], l.disp[:, t * HT:(t + 1) * HT],
                                            ident[0:SLOTS, 0:SLOTS])
                    last.then_inc(l.weights_t, 1)
                if i == SLOT_INPUTS:
                    pe.wait_ge(l.dispT_in, it + 1)
                    for c, n in enumerate(CT):
                        for t, keys in enumerate(TILE_TOK):
                            last = pe.matmul(l.ps[0:n, 1, P + c * SLOTS:P + (c + 1) * SLOTS],
                                             l.xn[0:keys, t, c * P:c * P + n], l.dispT[0:keys, t, :], start=(t == 0), stop=(t == 1))
                    last.then_inc(l.slots_out, 1)
                if i == HIDDEN_UNITS:
                    pe.wait_ge(l.xs_in, it * 2 + 2)
                    for c, n in enumerate(CT):
                        last = pe.matmul(l.ps[0:SLOTS, 1, 0:C], l.xs[0:n, c, :], wd[0:n, c, :],
                                         start=(c == 0), stop=(c == 1))
                    last.then_inc(l.hid_out, 1)
                if i == OWN:
                    pe.wait_ge(l.own_in, it + 1)
                    pe.wait_ge(l.combT_in, it + 1)
                    for c, n in enumerate(CT):
                        last = pe.matmul(l.ps[0:n, 0, c * SLOTS:(c + 1) * SLOTS], l.hid[:, c * P:c * P + n],
                                         ident[0:SLOTS, 0:SLOTS], start=True, stop=True)
                    last.then_inc(l.own_t, 1)
                if i == BACK:
                    pe.wait_ge(l.hidT_in, it * 2 + 2)
                    for c, n in enumerate(CT):
                        last = pe.matmul(l.ps[0:SLOTS, 1, 0:C], l.hidT[0:n, c, :], wu[0:n, c, :],
                                         start=(c == 0), stop=(c == 1))
                    last.then_inc(l.ys_out, 1)
                if i == ADD:
                    pe.wait_ge(l.ys_in, it + 1)
                    for t in range(2):
                        last = pe.matmul(l.ps[0:HT, 0, t * C:(t + 1) * C], l.combT[:, t * HT:(t + 1) * HT], l.ys[:],
                                         start=True, stop=True)
                    last.then_inc(l.y_out, 1)

            lanes_apart(pe, L, stages, count, MIXTURE_LAG)

        @block.scalar
        def _(act):

            def stages(i, it, l):
                if i == TRANSPOSE:
                    act.wait_ge(l.xn_t, it + 1)
                    for c, n in enumerate(CT):
                        act.activation(l.xt[0:n, c, :], l.ps[0:n, c, 0:TP], ACT.Copy).then_inc(l.xt_in, 1)
                if i == LOGITS:
                    act.wait_ge(l.maxima, it * 2 + 2)
                    for t in range(2):
                        act.activation(l.comb[:, t, :], l.ps[0:HT, 0, t * SLOTS:(t + 1) * SLOTS], ACT.Exp,
                                       bias=l.cmax[:, t:t + 1], accum_out=l.csum[:, t:t + 1]).then_inc(l.exps, 1)
                    act.activation(l.disp[:, 0:TOK], l.ps[0:SLOTS, 1, 0:TOK], ACT.Exp, bias=l.dmax[:, 0:1],
                                   accum_out=l.dsum[:, 0:1]).then_inc(l.exps, 1)
                if i == TURNED:
                    act.wait_ge(l.weights_t, it + 1)
                    act.activation(l.combT[:], l.ps[0:SLOTS, 0, 0:TP], ACT.Copy).then_inc(l.combT_in, 1)
                if i == SLOT_INPUTS:
                    act.wait_ge(l.slots_out, it + 1)
                    for c, n in enumerate(CT):
                        act.activation(l.xs[0:n, c, :], l.ps[0:n, 1, P + c * SLOTS:P + (c + 1) * SLOTS], ACT.Copy)\
                           .then_inc(l.xs_in, 1)
                if i == HIDDEN_UNITS:
                    act.wait_ge(l.hid_in, it + 1)
                    act.activation(l.hid[:], l.hid[:], ACT.Gelu).then_inc(l.gelu_in, 1)
                if i == OWN:
                    act.wait_ge(l.own_t, it + 1)
                    for c, n in enumerate(CT):
                        act.activation(l.hidT[0:n, c, :], l.ps[0:n, 0, c * SLOTS:(c + 1) * SLOTS], ACT.Copy)\
                           .then_inc(l.hidT_in, 1)

            lanes_apart(act, L, stages, count, MIXTURE_LAG)

        @block.vector
        def _(dve):
            for l in L:
                dve.memset(l.disp[:, TOK:TP], 0.0).then_inc(l.zeroed, 1)
            dve.wait_ge(loaded, 8 * 16)
            pre = Chain(dve, dve_chain, 0)
            pre.link(dve.tensor_tensor(sq_w[:], sp_w[:], sp_w[:], ALU.mult))
            dve.tensor_reduce(nrm_w[:], sq_w[:].rearrange("d c (n p) -> d c p n", n=EXPERTS), AX_X, ALU.add)\
               .then_inc(sums_in, 1)
            dve.wait_ge(roots, 1)
            pre.link(dve.tensor_scalar(nrm_w[:], nrm_w[:], L2_EPS, None, ALU.add))
            pre.link(dve.reciprocal(nrm_w[:], nrm_w[:]))
            for n in range(EXPERTS):
                at = slice(n * (SLOTS // EXPERTS), (n + 1) * (SLOTS // EXPERTS))
                last = dve.tensor_tensor(sp_w[:, :, at], sp_w[:, :, at], nrm_w[:], ALU.mult)
            pre.link(last)
            dve.tensor_scalar(sp_w[:], sp_w[:], scale[:, 0:1], None, ALU.mult).then_inc(slots_in, 1)
            for l in L:
                l.links = Chain(dve, l.chain, DVE_LINKS, spare=l.spare[:])

            def stages(i, it, l):
                l.links.turn = it
                if i == READ:
                    l.links.begin(it)
                    l.links.link(dve_read(dve, l, hres, it * MIXTURE_LANES + l.lane))
                    dve_norm_stats(dve, l.links, l, l.h, LN_EPS, l.ln_in)
                if i == NORMED:
                    dve.wait_ge(l.ln_rstd, it + 1)
                    l.links.link(dve_norm_apply(dve, l, l.xn, l.h))
                    for t in range(2):
                        last = dve.tensor_tensor_reduce(l.sq[:, t, :], l.xn[:, t, :], l.xn[:, t, :], 1.0, 0.0, ALU.mult,
                                                        ALU.add, l.nsq[:, t:t + 1])
                    last.then_inc(l.squares_in, 1)
                if i == SCALED:
                    dve.wait_ge(l.norm_in, it + 1)
                    l.links.link(dve.tensor_scalar(l.nrm[:], l.nrm[:], L2_EPS, None, ALU.add))
                    l.links.link(dve.reciprocal(l.nrm[:], l.nrm[:]))
                    for t in range(2):
                        last = dve.tensor_scalar(l.xn[:, t, :], l.xn[:, t, :], l.nrm[:, t:t + 1], None, ALU.mult)
                    last.then_inc(l.xn_in, 1)
                if i == LOGITS:
                    dve.wait_ge(l.logits, it + 1)
                    dve.tensor_reduce(l.cmax[:], l.ps[0:HT, 0, 0:2 * SLOTS].rearrange("p (t s) -> p t s", t=2),
                                      AX_X, ALU.max, negate=True).then_inc(l.maxima, 1)
                    dve.tensor_reduce(l.dmax[:], l.ps[0:SLOTS, 1, 0:TOK], AX_X, ALU.max, negate=True)\
                       .then_inc(l.maxima, 1)
                if i == WEIGHTS:
                    dve.wait_ge(l.exps, it * 3 + 3)
                    dve.reciprocal(l.csum[:], l.csum[:])
                    l.links.link(dve.reciprocal(l.dsum[:], l.dsum[:]))
                    for t in range(2):
                        last = dve.tensor_scalar(l.comb[:, t, :], l.comb[:, t, :], l.csum[:, t:t + 1], None, ALU.mult)
                    last.then_inc(l.weights, 1)
                    dve.tensor_scalar(l.disp[:, 0:TOK], l.disp[:, 0:TOK], l.dsum[:, 0:1], None, ALU.mult)\
                       .then_inc(l.weights, 1)
                if i == TURNED:
                    dve.wait_ge(l.weights_t, it + 1)
                    dve.tensor_copy(l.dispT[:].rearrange("p t s -> p (t s)"), l.ps[0:HT, 1, 0:2 * SLOTS])\
                       .then_inc(l.dispT_in, 1)
                if i == HIDDEN_UNITS:
                    dve.wait_ge(l.hid_out, it + 1)
                    dve.tensor_tensor(l.hid[:], l.ps[0:SLOTS, 1, 0:C], bd[:], ALU.add).then_inc(l.hid_in, 1)
                if i == HIDDEN_UNITS:
                    dve.wait_ge(l.gelu_in, it + 1)
                    dve.tensor_tensor(l.hid[:], l.hid[:], own[:], ALU.mult).then_inc(l.own_in, 1)
                if i == BACK:
                    dve.wait_ge(l.ys_out, it + 1)
                    dve.tensor_tensor(l.ys[:], l.ps[0:SLOTS, 1, 0:C], bu[:], ALU.add).then_inc(l.ys_in, 1)
                if i == ADD:
                    dve.wait_ge(l.y_out, it + 1)
                    clip = it * MIXTURE_LANES + l.lane
                    dve.tensor_tensor(hres[:, bass.ds(clip, 1), :, :].rearrange("p b t c -> p (b t c)"),
                                      l.h[:].rearrange("p t c -> p (t c)"), l.ps[0:HT, 0, 0:2 * C],
                                      ALU.add).then_inc(l.h_done, 1)
                    dve.wait_ge(l.h_done, it + 1)
                    l.links.end()

            lanes_apart(dve, L, stages, count, MIXTURE_LAG)




ITERATIONS = 3
HALF_STEPS = 2 * ITERATIONS
SINKHORN_LAG = 5
OUT_LN_EPS = 1e-12


class SinkhornLane:

    def __init__(self, a, ps):
        self.ps = ps
        self.h = a.sb("h", [HT, 2, C])
        self.lnst = a.sb("lnst", [HT, 2, 6])
        self.lnmv = a.sb("lnmv", [HT, 2, 2])
        self.lnr = a.sb("lnr", [HT, 2])
        self.xn = a.sb("xn", [HT, 2, C])
        self.xt = a.sb("xt", [P, 2, TP])
        self.q = a.sb("q", [P, NG, TP])
        self.kpad = a.sb("kpad", [P, HEADS, TP])
        self.v = a.sb("v", [HT, 2, HEADS, SLOT])
        self.kt = a.sb("kt", [HT, NG, HG, 2, TP])
        self.km = a.sb("km", [HT, NG, HG, 2, TP])
        self.spare = a.sb("spare", [1, 1])
        self.row = a.sb("row", [P, NG, TP])
        self.arow = a.sb("arow", [P, NG, TP])
        self.neg = a.sb("neg", [HT, 2, HEADS])
        self.a = a.sb("a", [HT, 2, HEADS])
        self.b = a.sb("b", [HT, 2, HEADS])
        self.ln_in, self.ln_rstd, self.xn_in = a.sems("ln_in", "ln_rstd", "xn_in")
        self.xn_t, self.xt_in, self.q_out = a.sems("xn_t", "xt_in", "q_out")
        self.k_out, self.v_out, self.q_in = a.sems("k_out", "v_out", "q_in")
        self.k_in, self.chain, self.v_in = a.sems("k_in", "chain", "v_in")
        self.s_out, self.s_max, self.zeroed = a.sems("s_out", "s_max", "zeroed")
        self.h_done, self.resid_in, self.shifted = a.sems("h_done", "resid_in", "shifted")
        self.st_out, self.st_max, self.kt_in = a.sems("st_out", "st_max", "kt_in")
        self.b_start, self.km_out, self.km_in_even = a.sems("b_start", "km_out", "km_in_even")
        self.km_in_odd, self.sum_out, self.row_in = a.sems("km_in_odd", "sum_out", "row_in")
        self.row_t, self.col_in, self.arow_out = a.sems("row_t", "col_in", "arow_out")
        self.arow_in, self.v_scaled, self.pv_out = a.sems("arow_in", "v_scaled", "pv_out")
        self.ctx_in, self.proj_out, self.ln2_in = a.sems("ctx_in", "proj_out", "ln2_in")
        self.ln2_rstd = a.sem("ln2_rstd")


def phase_sinkhorn(nc, w, hres):
    DVE_LINKS = 9
    READ, NORMED, TRANSPOSE, PROJECT, VALUES = range(5)
    SCORES = VALUES + 1
    SCORES_T = SCORES + UNITS
    TURNED = SCORES_T + UNITS
    SUMS = TURNED + UNITS
    ROWS = SUMS + 2 * HALF_STEPS
    WEIGHTED, BACK, FINISH = ROWS + 1, ROWS + 2, ROWS + 3
    count = FINISH + 1
    with ExitStack() as st:
        A = Alloc(nc, st, "sink_")
        psum = A.psum()
        wq, wk = (A.sb(n, [P, 2, NG, P]) for n in ("wq", "wk"))
        wv = A.sb("wv", [P, 2, C])
        wo = A.sb("wo", [P, NG, C])
        vb = A.sb("vb", [P, 2 * C])
        qb, kb = A.sb("qb", [P, NG]), A.sb("kb", [P, NG])
        vec = A.sb("vec", [P, 3, 2, C])
        ident = A.sb("ident", [P, P])
        half = A.sb("half", [P, 1])
        loaded, loaded_late, consts, ready = (A.sem(n) for n in ("loaded", "loaded_late", "consts", "ready"))
        L = [SinkhornLane(A.of_lane(lane), psum[:, lane * LANE_BANKS:(lane + 1) * LANE_BANKS, :]) for lane in LANES]
        for lane, l in enumerate(L):
            l.lane = lane
        block = st.enter_context(nc.Block())

        @block.sync
        def _(sp):
            load_all(sp, ((ident[:], w["ident"]), (wq[:], w["s_wq"]), (wk[:], w["s_wk"]), (qb[:], w["s_qb"]),
                          (kb[:], w["s_kb"])), loaded)
            load_all(sp, ((wv[:], w["s_wv"]), (vb[:], w["s_vb"]), (vec[:], w["s_rows"]), (wo[:], w["s_wo"])),
                     loaded_late)

        @block.gpsimd
        def _(pool):
            pool.memset(half[:], -0.5).then_inc(consts, 1)
            pool.wait_ge(consts, 1)

            def stages(i, it, l):
                if i == READ:
                    pool.wait_ge(l.ln_in, it + 1)
                    pool_rstd(pool, l, half).then_inc(l.ln_rstd, 1)
                if i == BACK:
                    pool.wait_ge(l.ln2_in, it + 1)
                    pool_rstd(pool, l, half).then_inc(l.ln2_rstd, 1)

            lanes_apart(pool, L, stages, count, SINKHORN_LAG)

        @block.tensor
        def _(pe):
            pe.wait_ge(loaded, 5 * 16)
            for l in L:
                pe.wait_ge(l.zeroed, 3)

            def stages(i, it, l):
                if i == TRANSPOSE:
                    pe.wait_ge(l.xn_in, it + 1)
                    pe.wait_ge(l.h_done, it)
                    pe_transpose_tokens(pe, l, l.xn, ident).then_inc(l.xn_t, 1)
                if i == PROJECT:
                    pe.wait_ge(l.xt_in, it * 2 + 2)
                    pe_project_padded(pe, l, wq, BANKS_Q).then_inc(l.q_out, 1)
                    pe_project_padded(pe, l, wk, BANKS_K).then_inc(l.k_out, 1)
                if i == VALUES:
                    pe.wait_ge(loaded_late, 4 * 16)
                    pe.wait_ge(l.q_in, it + 1)
                    pe_project_values(pe, l, wv, 2).then_inc(l.v_out, 1)
                u = i - SCORES
                if 0 <= u < UNITS:
                    if u == 0:
                        pe.wait_ge(l.k_in, it + 1)
                        pe.wait_ge(l.v_in, it + 1)
                    elif u > 1:
                        pe.wait_ge(l.shifted, it * UNITS + u - 1)
                    pe_scores(pe, l, u).then_inc(l.s_out, 1)
                u = i - SCORES_T
                if 0 <= u < UNITS:
                    pe.wait_ge(l.shifted, it * UNITS + UNITS)
                    if u > 1:
                        pe.wait_ge(l.kt_in, it * UNITS + u - 1)
                    pe_transpose_scores(pe, l, u, l.km, ident).then_inc(l.st_out, 1)
                u = i - TURNED
                if 0 <= u < UNITS:
                    pe.wait_ge(l.kt_in, it * UNITS + UNITS)
                    if u > 1:
                        pe.wait_ge(l.km_in_odd if u % 2 else l.km_in_even, it * (UNITS // 2) + u // 2)
                    pe_transpose_scores(pe, l, u, l.kt, ident).then_inc(l.km_out, 1)
                s, part = divmod(i - SUMS, 2)
                if part == 0 and 0 <= s < HALF_STEPS:
                    for half in (l.km_in_even, l.km_in_odd):
                        pe.wait_ge(half, (it + 1) * (UNITS // 2))
                    if s == 0:
                        pe.wait_ge(l.b_start, it + 1)
                    else:
                        pe.wait_ge(l.col_in, it * HALF_STEPS + s)
                    pe_column_sums(pe, l, *((l.a, l.km) if s % 2 else (l.b, l.kt))).then_inc(l.sum_out, 1)
                s, part = divmod(i - SUMS, 2)
                if part == 1 and 0 <= s < HALF_STEPS:
                    pe.wait_ge(l.row_in, it * HALF_STEPS + s + 1)
                    for g in range(NG):
                        for t in range(2):
                            last = pe.transpose(l.ps[0:HT, (3, 0)[t], g * P:(g + 1) * P], l.row[:, g, t * HT:(t + 1) * HT],
                                                ident[:])
                    last.then_inc(l.row_t, 1)
                    if s == HALF_STEPS - 1:
                        pe_columns_to_rows(pe, l, l.a, ident, BANKS_ROWS).then_inc(l.arow_out, 1)
                if i == WEIGHTED:
                    pe.wait_ge(l.arow_in, it + 1)
                    pe.wait_ge(l.v_scaled, it + 1)
                    pe_weighted_sum(pe, l, l.v, l.kt).then_inc(l.pv_out, 1)
                if i == BACK:
                    pe.wait_ge(l.ctx_in, it + 1)
                    pe_project_back(pe, l, l.row, wo, 3).then_inc(l.proj_out, 1)

            lanes_apart(pe, L, stages, count, SINKHORN_LAG)

        @block.scalar
        def _(act):
            act.wait_ge(ready, 1)
            for l in L:
                act.wait_ge(l.zeroed, 3)

            def stages(i, it, l):
                if i == TRANSPOSE:
                    act.wait_ge(l.xn_t, it + 1)
                    for c, n in enumerate(CT):
                        act.activation(l.xt[0:n, c, :], l.ps[0:n, c, 0:TP], ACT.Copy).then_inc(l.xt_in, 1)
                if i == PROJECT:
                    act.wait_ge(l.k_out, it + 1)
                    act_keys(act, l, kb, BANKS_K).then_inc(l.k_in, 1)
                u = i - SCORES
                if 0 <= u < UNITS:
                    for g, hq, h in heads_of(u):
                        act.wait_ge(l.s_max, it * HEADS + h + 1)
                        for t in range(2):
                            last = act.activation(l.km[:, g, hq, t, :], l.ps[0:HT, hq, t * TP:(t + 1) * TP],
                                                  ACT.Identity, bias=l.neg[:, t, h:h + 1])
                    last.then_inc(l.shifted, 1)
                u = i - SCORES_T
                if 0 <= u < UNITS:
                    act_unit_exp(act, l, u, l.kt, l.neg, l.st_max, it * HEADS).then_inc(l.kt_in, 1)
                if i == TURNED - 1:
                    act.activation(l.b[:], l.neg[:], ACT.Exp, scale=-1.0).then_inc(l.b_start, 1)
                u = i - TURNED
                if 0 <= u < UNITS:
                    if u % 2:
                        act.wait_ge(l.km_out, it * UNITS + u + 1)
                        act_copy_unit(act, l, u, l.km).then_inc(l.km_in_odd, 1)
                s, part = divmod(i - SUMS, 2)
                if part == 0 and 0 <= s < HALF_STEPS:
                    act.wait_ge(l.sum_out, it * HALF_STEPS + s + 1)
                    act.activation(l.row[:], l.ps[:, 0:NG, 0:TP], ACT.Copy).then_inc(l.row_in, 1)
                if i == ROWS:
                    act.wait_ge(l.arow_out, it + 1)
                    act_rows(act, l, l.arow).then_inc(l.arow_in, 1)

            lanes_apart(act, L, stages, count, SINKHORN_LAG)

        @block.vector
        def _(dve):
            for l in L:
                dve.memset(l.kpad[:], 0.0).then_inc(l.zeroed, 1)
                dve.memset(l.v[:, :, :, D:SLOT], 0.0).then_inc(l.zeroed, 1)
                dve.memset(l.kt[:, :, :, :, TOK:TP], 1.0).then_inc(l.zeroed, 1)
            dve.wait_ge(loaded, 5 * 16)
            dve.tensor_scalar(qb[:], qb[:], D ** -0.5, None, ALU.mult).then_inc(ready, 1)
            dve.wait_ge(ready, 1)
            for l in L:
                l.links = Chain(dve, l.chain, DVE_LINKS, spare=l.spare[:])

            def stages(i, it, l):
                l.links.turn = it
                if i == READ:
                    l.links.begin(it)
                    l.links.link(dve_read(dve, l, hres, it * len(LANES) + l.lane))
                    dve_norm_stats(dve, l.links, l, l.h, LN_EPS, l.ln_in)
                if i == NORMED:
                    dve.wait_ge(l.ln_rstd, it + 1)
                    dve_norm_apply(dve, l, l.xn, l.h).then_inc(l.xn_in, 1)
                if i == PROJECT:
                    dve.wait_ge(loaded_late, 4 * 16)
                    dve.wait_ge(l.xn_t, it + 1)
                    dve.tensor_tensor(l.xn[:], l.xn[:], vec[0:HT, 0, :, :], ALU.add).then_inc(l.resid_in, 1)
                    dve.wait_ge(l.q_out, it + 1)
                    dve_queries(dve, l, qb, BANKS_Q, D ** -0.5).then_inc(l.q_in, 1)
                if i == VALUES:
                    dve.wait_ge(l.v_out, it + 1)
                    dve_values(dve, l, vb, 2).then_inc(l.v_in, 1)
                u = i - SCORES
                if 0 <= u < UNITS:
                    dve.wait_ge(l.s_out, it * UNITS + u + 1)
                    dve_unit_max(dve, l, u, l.neg, l.s_max)
                u = i - SCORES_T
                if 0 <= u < UNITS:
                    dve.wait_ge(l.st_out, it * UNITS + u + 1)
                    if u == 0:
                        dve.wait_ge(l.shifted, it * UNITS + UNITS)
                    dve_unit_max(dve, l, u, l.neg, l.st_max)
                u = i - TURNED
                if 0 <= u < UNITS and u % 2 == 0:
                    dve.wait_ge(l.km_out, it * UNITS + u + 1)
                    dve_copy_unit(dve, l, u, l.km).then_inc(l.km_in_even, 1)
                s, part = divmod(i - SUMS, 2)
                if part == 1 and 0 <= s < HALF_STEPS:
                    dve.wait_ge(l.row_t, it * HALF_STEPS + s + 1)
                    dst = l.b if s % 2 else l.a
                    for t in range(2):
                        sums = l.ps[0:HT, (3, 0)[t], 0:NG * P].rearrange("p (h r) -> p h r", r=SLOT)[:, :, 0]
                        last = dve.reciprocal(dst[:, t, :], sums)
                    last.then_inc(l.col_in, 1)
                if i == ROWS:
                    dve.wait_ge(l.col_in, (it + 1) * HALF_STEPS)
                    for t in range(2):
                        b = l.b[:, t, :].rearrange("p (h o) -> p h o", o=1).to_broadcast([HT, HEADS, D])
                        last = dve.tensor_tensor(l.v[:, t, :, 0:D], l.v[:, t, :, 0:D], b, ALU.mult)
                    last.then_inc(l.v_scaled, 1)
                if i == WEIGHTED:
                    dve.wait_ge(l.pv_out, it + 1)
                    dve.wait_ge(l.arow_in, it + 1)
                    dve.tensor_tensor(l.row[:], l.ps[:, 0:NG, 0:TP], l.arow[:], ALU.mult).then_inc(l.ctx_in, 1)
                if i == BACK:
                    dve.wait_ge(l.proj_out, it + 1)
                    xf = l.xn[:].rearrange("p t c -> p (t c)")
                    l.links.link(dve.tensor_tensor(xf, xf, l.ps[0:HT, 3, 0:2 * C], ALU.add))
                    dve_norm_stats(dve, l.links, l, l.xn, OUT_LN_EPS, l.ln2_in)
                if i == FINISH:
                    clip = it * len(LANES) + l.lane
                    dve.wait_ge(l.ln2_rstd, it + 1)
                    l.links.link(dve_norm_apply(dve, l, l.xn, l.xn))
                    l.links.link(dve.tensor_tensor(l.xn[:], l.xn[:], vec[0:HT, 1, :, :], ALU.mult))
                    l.links.link(dve.tensor_tensor(l.h[:], l.h[:], vec[0:HT, 2, :, :], ALU.add))
                    dve.tensor_tensor(hres[:, bass.ds(clip, 1), :, :].rearrange("p b t c -> p (b t c)"),
                                      l.h[:].rearrange("p t c -> p (t c)"), l.xn[:].rearrange("p t c -> p (t c)"),
                                      ALU.add).then_inc(l.h_done, 1)
                    dve.wait_ge(l.h_done, it + 1)
                    l.links.end()

            lanes_apart(dve, L, stages, count, SINKHORN_LAG)




HIDDEN = 768
FT = HIDDEN // P
ROUTED = max(1, int(round(0.15 * TOK)))
POOL_EPS = 1e-6
BANKS_RK = ((2, 0), (2, TP), (3, 0))
G1, B1, G2, B2, BM, BF2, WR = range(7)


class RoutedLane:

    def __init__(self, a, ps):
        self.ps = ps
        self.h = a.sb("h", [HT, 2, C])
        self.lnst = a.sb("lnst", [HT, 2, 6])
        self.lnmv = a.sb("lnmv", [HT, 2, 2])
        self.lnr = a.sb("lnr", [HT, 2])
        self.xt = a.sb("xt", [P, 2, TP])
        self.kpad = a.sb("kpad", [P, HEADS, TP])
        self.v = a.sb("v", [HT, 2, HEADS, SLOT])
        self.hs = a.sb("hs", [HT, 2, C])
        self.nm = a.sb("nm", [HT, 2, C + 1])
        self.zz = a.sb("zz", [HT, 2, C])
        self.z = a.sb("z", [HT, 2])
        self.s = a.sb("s", [HT, 2])
        self.diag = a.sb("diag", [HT, 2, HT])
        self.cmp = a.sb("cmp", [HT, 4, TOK])
        self.cnt = a.sb("cnt", [HT, 4])
        self.rank = a.sb("rank", [HT, 2])
        self.sel = a.sb("sel", [HT, 2, ROUTED])
        self.rest = a.sb("rest", [HT, 2])
        self.pool = a.sb("pool", [HT, C])
        self.rsum = a.sb("rsum", [HT, 1])
        self.mx = a.sb("mx", [HT, 2, C])
        self.xsel = a.sb("xsel", [P, 2, ROUTED])
        self.selT = a.sb("selT", [ROUTED, TP])
        self.q = a.sb("q", [P, NG, ROUTED])
        self.neg = a.sb("neg", [ROUTED, HEADS])
        self.den = a.sb("den", [HT, HEADS])
        self.eq = a.sb("eq", [ROUTED, HEADS, TP])
        self.e = a.sb("e", [HT, 2, HEADS, ROUTED])
        self.ctx = a.sb("ctx", [P, NG, ROUTED])
        self.rden = a.sb("rden", [P, NG * ROUTED])
        self.asel = a.sb("asel", [ROUTED, C])
        self.h1 = a.sb("h1", [HT, 2, C])
        self.spare = a.sb("spare", [1, 1])
        self.gl = a.sb("gl", [P, FT, TP])
        self.o = a.sb("o", [HT, 2, C])
        self.ln_in, self.ln_rstd, self.z_in = a.sems("ln_in", "ln_rstd", "z_in")
        self.ez_in, self.diag_in, self.xn_in = a.sems("ez_in", "diag_in", "xn_in")
        self.srow_out, self.pool_out, self.xn_t = a.sems("srow_out", "pool_out", "xn_t")
        self.xt_in, self.sel_in, self.mx_in = a.sems("xt_in", "sel_in", "mx_in")
        self.sel_out, self.xsel_in, self.selT_in = a.sems("sel_out", "xsel_in", "selT_in")
        self.q_out, self.k_out, self.v_out = a.sems("q_out", "k_out", "v_out")
        self.q_in, self.k_in, self.v_in = a.sems("q_in", "k_in", "v_in")
        self.s_out, self.s_max, self.eq_in = a.sems("s_out", "s_max", "eq_in")
        self.e_out, self.e_in, self.den_in = a.sems("e_out", "e_in", "den_in")
        self.den_out, self.rden_in, self.pv_out = a.sems("den_out", "rden_in", "pv_out")
        self.ctx_in, self.asel_out, self.asel_in = a.sems("ctx_in", "asel_out", "asel_in")
        self.mx_t, self.mxt_in, self.merged = a.sems("mx_t", "mxt_in", "merged")
        self.n2_in, self.n2_t, self.n2t_in = a.sems("n2_in", "n2_t", "n2t_in")
        self.up_out, self.gl_in, self.down_out = a.sems("up_out", "gl_in", "down_out")
        self.o_in, self.stored, self.zeroed = a.sems("o_in", "stored", "zeroed")
        self.chain = a.sem("chain")


def phase_routed(nc, w, hres, out):
    DVE_LINKS = 26
    (READ, NORM_1, NORM_2, TRANSPOSE, RANK, KEYS, SELECT, QUERY, SCORES) = range(9)
    TURNED = SCORES + UNITS
    (ROWS, WEIGHTED, MIXED, BACK, MERGE, NORM_3, TRANSPOSE_2, UP) = range(TURNED + 1, TURNED + 9)
    DOWN = UP + FT // 2
    count = DOWN + 1
    with ExitStack() as st:
        A = Alloc(nc, st, "rout_")
        psum = A.psum()
        wq, wk = (A.sb(n, [P, 2, NG, P]) for n in ("wq", "wk"))
        wv, wm = A.sb("wv", [P, 2, C]), A.sb("wm", [P, 2, C])
        wo = A.sb("wo", [P, NG, C])
        w1, w2 = A.sb("w1", [P, 2, HIDDEN]), A.sb("w2", [P, FT, C])
        vb = A.sb("vb", [P, 2 * C])
        qb, kb = A.sb("qb", [P, NG]), A.sb("kb", [P, NG])
        b1 = A.sb("b1", [P, FT])
        vec = A.sb("vec", [P, 7, 2, C])
        nbr = A.sb("nbr", [P, 1])
        ident = A.sb("ident", [P, P])
        ones = A.sb("ones", [P, P])
        ids = A.sb("ids", [P, ROUTED])
        earlier = A.sb("earlier", [HT, 2, TOK])
        half = A.sb("half", [P, 1])
        loaded, loaded_late, consts, ready = (A.sem(n) for n in ("loaded", "loaded_late", "consts", "ready"))
        L = [RoutedLane(A.of_lane(lane), psum[:, lane * LANE_BANKS:(lane + 1) * LANE_BANKS, :]) for lane in LANES]
        for lane, l in enumerate(L):
            l.lane = lane
        block = st.enter_context(nc.Block())

        @block.sync
        def _(sp):
            load_all(sp, ((vec[:], w["r_rows"]), (nbr[:], w["r_br"]), (ident[:], w["ident"]), (ids[:], w["rank_ids"]),
                          (earlier[:], w["earlier"]), (qb[:], w["r_qb"]), (kb[:], w["r_kb"]), (vb[:], w["r_vb"]),
                          (wk[:], w["r_wk"])), loaded)
            load_all(sp, ((wv[:], w["r_wv"]), (wq[:], w["r_wq"]), (wo[:], w["r_wo"]), (wm[:], w["r_wm"]),
                          (w1[:], w["r_w1"]), (b1[:], w["r_b1"]), (w2[:], w["r_w2"])), loaded_late)
            with sp.Fori(0, PAIRS) as it:
                for lane, l in enumerate(L):
                    clip = it * len(LANES) + l.lane
                    sp.wait_ge(l.o_in, it + 1)
                    dst = out[bass.ds(clip, 1), :, :]
                    sp.dma_start(dst[:, 0:HT, :].rearrange("b p c -> p (b c)"), l.o[:, 0, :]).then_inc(l.stored, 16)
                    sp.dma_start(dst[:, HT:TOK, :].rearrange("b p c -> p (b c)"), l.o[0:TILE_TOK[1], 1, :])\
                      .then_inc(l.stored, 16)
            for l in L:
                sp.wait_ge(l.stored, PAIRS * 32)

        @block.gpsimd
        def _(pool):
            pool.memset(half[:], -0.5).then_inc(consts, 1)
            pool.memset(ones[:], 1.0).then_inc(consts, 1)
            pool.wait_ge(consts, 2)

            def stages(i, it, l):
                if i == READ:
                    pool.wait_ge(l.ln_in, it * 3 + 1)
                    pool_rstd(pool, l, half).then_inc(l.ln_rstd, 1)
                if i == NORM_1:
                    pool.wait_ge(l.ln_in, it * 3 + 2)
                    pool_rstd(pool, l, half).then_inc(l.ln_rstd, 1)
                if i == MERGE:
                    pool.wait_ge(l.ln_in, it * 3 + 3)
                    pool_rstd(pool, l, half).then_inc(l.ln_rstd, 1)

            lanes_ahead(pool, L, stages, count, TRANSPOSE, DOWN)

        @block.tensor
        def _(pe):
            pe.wait_ge(loaded, 9 * 16)
            pe.wait_ge(consts, 2)
            for l in L:
                pe.wait_ge(l.zeroed, 6)

            def stages(i, it, l):
                if i == TRANSPOSE:
                    pe.wait_ge(l.xn_in, it + 1)
                    pe.wait_ge(l.o_in, it)
                    pe_transpose_tokens(pe, l, l.nm, ident, (2, 3)).then_inc(l.xn_t, 1)
                if i == RANK:
                    pe.wait_ge(l.diag_in, it + 1)
                    for t in range(2):
                        last = pe.matmul(l.ps[0:HT, 0, t * HT:(t + 1) * HT], ones[0:HT, 0:HT], l.diag[:, t, :],
                                         start=True, stop=True)
                    last.then_inc(l.srow_out, 1)
                    for t, keys in enumerate(TILE_TOK):
                        last = pe.matmul(l.ps[0:HT, 1, 0:C + 1], l.s[0:keys, t:t + 1].to_broadcast([keys, HT]),
                                         l.nm[0:keys, t, :], start=(t == 0), stop=(t == 1))
                    last.then_inc(l.pool_out, 1)
                if i == KEYS:
                    pe.wait_ge(l.xt_in, it * 2 + 2)
                    pe_project_padded(pe, l, wk, BANKS_RK).then_inc(l.k_out, 1)
                if i == SELECT:
                    pe.wait_ge(loaded_late, 7 * 16)
                    pe.wait_ge(l.sel_in, it + 1)
                    for c, n in enumerate(CT):
                        for t, keys in enumerate(TILE_TOK):
                            pe.matmul(l.ps[0:n, 0, c * ROUTED:(c + 1) * ROUTED], l.nm[0:keys, t, c * P:c * P + n],
                                      l.sel[0:keys, t, :], start=(t == 0), stop=(t == 1))
                    for t in range(2):
                        last = pe.transpose(l.ps[0:ROUTED, 0, P + t * HT:P + (t + 1) * HT], l.sel[:, t, :],
                                            ident[0:HT, 0:HT])
                    last.then_inc(l.sel_out, 1)
                    pe.wait_ge(l.mx_in, it + 1)
                    pe_project_values(pe, l, wv, 1).then_inc(l.v_out, 1)
                if i == QUERY:
                    pe.wait_ge(l.xsel_in, it * 2 + 2)
                    pe.wait_ge(l.selT_in, it + 1)
                    for g in range(NG):
                        for c, n in enumerate(CT):
                            last = pe.matmul(l.ps[:, 0, g * ROUTED:(g + 1) * ROUTED], wq[0:n, c, g, :],
                                             l.xsel[0:n, c, :], start=(c == 0), stop=(c == 1))
                    last.then_inc(l.q_out, 1)
                u = i - SCORES
                if 0 <= u < UNITS:
                    if u == 0:
                        pe.wait_ge(l.q_in, it + 1)
                        pe.wait_ge(l.k_in, it + 1)
                        pe.wait_ge(l.v_in, it + 1)
                    elif u > 1:
                        pe.wait_ge(l.eq_in, it * UNITS + u - 1)
                    for g, hq, h in heads_of(u):
                        last = pe.matmul(l.ps[0:ROUTED, hq, 0:TP], l.q[:, g, :], l.kpad[:, h, :],
                                         start=True, stop=True)
                    last.then_inc(l.s_out, 1)
                if i == TURNED:
                    pe.wait_ge(l.eq_in, it * UNITS + UNITS)
                    for t in range(2):
                        for h in range(HEADS):
                            o = l.ps[0:HT, 1 + t, h * ROUTED:(h + 1) * ROUTED]
                            src, eye = l.eq[:, h, t * HT:(t + 1) * HT], ident[0:ROUTED, 0:ROUTED]
                            if t == h == 0:
                                pe.matmul(o, src, eye, start=True, stop=True)
                            else:
                                last = pe.transpose(o, src, eye)
                    last.then_inc(l.e_out, 1)
                if i == ROWS:
                    pe.wait_ge(l.den_in, it + 1)
                    for h in range(HEADS):
                        at = SLOT * (h % HG)
                        last = pe.matmul(l.ps[at:at + SLOT, 0, h // HG * ROUTED:(h // HG + 1) * ROUTED],
                                         l.den[:, h:h + 1].to_broadcast([HT, SLOT]), ident[0:HT, 0:ROUTED],
                                         start=True, stop=True, skip_group_check=True)
                    last.then_inc(l.den_out, 1)
                if i == WEIGHTED:
                    pe.wait_ge(l.e_in, it + 1)
                    for g in range(NG):
                        for t, keys in enumerate(TILE_TOK):
                            for hq in range(HG):
                                h = HG * g + hq
                                last = pe.matmul(l.ps[SLOT * hq:SLOT * (hq + 1), 3, g * ROUTED:(g + 1) * ROUTED],
                                                 l.v[0:keys, t, h, :], l.e[0:keys, t, h, :], start=(t == 0),
                                                 stop=(t == 1), skip_group_check=True)
                    last.then_inc(l.pv_out, 1)
                if i == MIXED:
                    pe.wait_ge(l.mx_in, it + 1)
                    pe_transpose_tokens(pe, l, l.mx, ident, (1, 2)).then_inc(l.mx_t, 1)
                if i == BACK:
                    pe.wait_ge(l.ctx_in, it + 1)
                    for g in range(NG):
                        last = pe.matmul(l.ps[0:ROUTED, 3, 0:C], l.ctx[:, g, :], wo[:, g, :], start=(g == 0),
                                         stop=(g == NG - 1))
                    last.then_inc(l.asel_out, 1)
                if i == MERGE:
                    pe.wait_ge(l.mxt_in, it * 2 + 2)
                    pe.wait_ge(l.asel_in, it + 1)
                    for t in range(2):
                        at = slice(t * HT, (t + 1) * HT)
                        o = l.ps[0:HT, 0, t * C:(t + 1) * C]
                        pe.matmul(o, l.selT[:, at], l.asel[:], start=True, stop=False)
                        for c, n in enumerate(CT):
                            last = pe.matmul(o, l.xt[0:n, c, at], wm[0:n, c, :], start=False, stop=(c == 1))
                    last.then_inc(l.merged, 1)
                if i == TRANSPOSE_2:
                    pe.wait_ge(l.n2_in, it + 1)
                    pe_transpose_tokens(pe, l, l.mx, ident, (1, 2)).then_inc(l.n2_t, 1)
                k = i - UP
                if 0 <= k < FT // 2:
                    pe.wait_ge(l.n2t_in, it * 2 + 2)
                    for f in (2 * k, 2 * k + 1):
                        for c, n in enumerate(CT):
                            last = pe.matmul(l.ps[:, f // 2, (f % 2) * TP:(f % 2 + 1) * TP],
                                             w1[0:n, c, f * P:(f + 1) * P], l.xt[0:n, c, :],
                                             start=(c == 0), stop=(c == 1))
                        if f % 2:
                            last.then_inc(l.up_out, 1)
                if i == DOWN:
                    pe.wait_ge(l.gl_in, it * FT + FT)
                    for t in range(2):
                        for f in range(FT):
                            last = pe.matmul(l.ps[0:HT, 3, t * C:(t + 1) * C], l.gl[:, f, t * HT:(t + 1) * HT],
                                             w2[:, f, :], start=(f == 0), stop=(f == FT - 1))
                    last.then_inc(l.down_out, 1)

            lanes_ahead(pe, L, stages, count, TRANSPOSE, DOWN)

        @block.scalar
        def _(act):
            act.wait_ge(loaded, 9 * 16)
            act.wait_ge(ready, 2)
            for l in L:
                act.wait_ge(l.zeroed, 6)

            def stages(i, it, l):
                if i == NORM_2:
                    act.wait_ge(l.z_in, it + 1)
                    act.activation(l.z[:], l.z[:], ACT.Exp, bias=nbr[0:HT, :], scale=-1.0).then_inc(l.ez_in, 1)
                if i == TRANSPOSE:
                    act.wait_ge(l.xn_t, it + 1)
                    for c, n in enumerate(CT):
                        act.activation(l.xt[0:n, c, :], l.ps[0:n, 2 + c, 0:TP], ACT.Copy).then_inc(l.xt_in, 1)
                if i == KEYS:
                    act.wait_ge(l.k_out, it + 1)
                    act_keys(act, l, kb, BANKS_RK).then_inc(l.k_in, 1)
                if i == SELECT:
                    act.wait_ge(l.sel_out, it + 1)
                    for c, n in enumerate(CT):
                        act.activation(l.xsel[0:n, c, :], l.ps[0:n, 0, c * ROUTED:(c + 1) * ROUTED], ACT.Copy)\
                           .then_inc(l.xsel_in, 1)
                    act.activation(l.selT[:], l.ps[0:ROUTED, 0, P:P + TP], ACT.Copy).then_inc(l.selT_in, 1)
                u = i - SCORES
                if 0 <= u < UNITS:
                    act.wait_ge(l.s_max, it * UNITS + u + 1)
                    for g, hq, h in heads_of(u):
                        last = act.activation(l.eq[:, h, 0:TOK], l.ps[0:ROUTED, hq, 0:TOK], ACT.Exp,
                                              bias=l.neg[:, h:h + 1], accum_out=l.den[0:ROUTED, h:h + 1])
                    last.then_inc(l.eq_in, 1)
                if i == TURNED:
                    act.wait_ge(l.e_out, it + 1)
                    act.activation(l.e[:].rearrange("p t h r -> p t (h r)"), l.ps[0:HT, 1:3, 0:HEADS * ROUTED],
                                   ACT.Copy).then_inc(l.e_in, 1)
                if i == ROWS:
                    act.wait_ge(l.den_out, it + 1)
                    act.activation(l.rden[:], l.ps[:, 0, 0:NG * ROUTED], ACT.Copy).then_inc(l.rden_in, 1)
                if i == MIXED:
                    act.wait_ge(l.mx_t, it + 1)
                    act.wait_ge(l.v_out, it + 1)
                    for c, n in enumerate(CT):
                        act.activation(l.xt[0:n, c, :], l.ps[0:n, 1 + c, 0:TP], ACT.Copy).then_inc(l.mxt_in, 1)
                if i == BACK:
                    act.wait_ge(l.asel_out, it + 1)
                    act.activation(l.asel[:], l.ps[0:ROUTED, 3, 0:C], ACT.Copy).then_inc(l.asel_in, 1)
                if i == TRANSPOSE_2:
                    act.wait_ge(l.n2_t, it + 1)
                    for c, n in enumerate(CT):
                        act.activation(l.xt[0:n, c, :], l.ps[0:n, 1 + c, 0:TP], ACT.Copy).then_inc(l.n2t_in, 1)
                k = i - UP
                if 0 <= k < FT // 2:
                    act.wait_ge(loaded_late, 7 * 16)
                    for f in (2 * k, 2 * k + 1):
                        act.wait_ge(l.up_out, it * (FT // 2) + f // 2 + 1)
                        act.activation(l.gl[:, f, :], l.ps[:, f // 2, (f % 2) * TP:(f % 2 + 1) * TP], ACT.Gelu,
                                       bias=b1[:, f:f + 1]).then_inc(l.gl_in, 1)

            lanes_ahead(act, L, stages, count, TRANSPOSE, DOWN)

        @block.vector
        def _(dve):
            for l in L:
                dve.memset(l.kpad[:], 0.0).then_inc(l.zeroed, 1)
                dve.memset(l.den[:], 0.0).then_inc(l.zeroed, 1)
                dve.memset(l.eq[:, :, TOK:TP], 1.0).then_inc(l.zeroed, 1)
                dve.memset(l.v[:, :, :, D + 1:SLOT], 0.0).then_inc(l.zeroed, 1)
                dve.memset(l.v[:, :, :, V_ONE], 1.0).then_inc(l.zeroed, 1)
                dve.memset(l.nm[:, :, C:C + 1], 1.0).then_inc(l.zeroed, 1)
            dve.wait_ge(loaded, 9 * 16)
            dve.tensor_scalar(qb[:], qb[:], D ** -0.5, None, ALU.mult).then_inc(ready, 1)
            dve.tensor_scalar(nbr[:], nbr[:], -1.0, None, ALU.mult).then_inc(ready, 1)
            dve.wait_ge(ready, 2)
            for l in L:
                l.links = Chain(dve, l.chain, DVE_LINKS, spare=l.spare[:])
            v_ = lambda k: vec[0:HT, k, :, :]

            def stages(i, it, l):
                l.links.turn = it
                if i == READ:
                    l.links.begin(it)
                    l.links.link(dve_read(dve, l, hres, it * len(LANES) + l.lane))
                    dve_norm_stats(dve, l.links, l, l.h, LN_EPS, l.ln_in)
                if i == NORM_1:
                    dve.wait_ge(l.ln_rstd, it * 3 + 1)
                    l.links.link(dve_norm_apply(dve, l, l.hs, l.h))
                    dve_norm_stats(dve, l.links, l, l.hs, LN_EPS, l.ln_in)
                if i == NORM_2:
                    dve.wait_ge(l.ln_rstd, it * 3 + 2)
                    nm = l.nm[:, :, 0:C]
                    l.links.link(dve_norm_apply(dve, l, nm, l.hs))
                    l.links.link(dve.tensor_tensor(nm, nm, v_(G1), ALU.mult))
                    dve.tensor_tensor(nm, nm, v_(B1), ALU.add).then_inc(l.xn_in, 1)
                    dve.wait_ge(l.xn_in, it + 1)
                    l.links.link(dve.tensor_tensor(l.zz[:], nm, v_(WR), ALU.mult))
                    dve.tensor_reduce(l.z[:], l.zz[:], AX_X, ALU.add).then_inc(l.z_in, 1)
                if i == RANK:
                    dve.wait_ge(l.ez_in, it + 1)
                    l.links.link(dve.tensor_scalar(l.s[:], l.z[:], 1.0, None, ALU.add))
                    l.links.link(dve.reciprocal(l.s[:], l.s[:]))
                    for t in range(2):
                        last = dve.tensor_scalar(l.diag[:, t, :], ident[0:HT, 0:HT], l.s[:, t:t + 1], None, ALU.mult)
                    last.then_inc(l.diag_in, 1)
                if i == SELECT:
                    dve.wait_ge(l.srow_out, it + 1)
                    srow = l.ps[0:HT, 0, 0:TOK]
                    for t in range(2):
                        dve.tensor_scalar(l.cmp[:, t, :], srow, l.s[:, t:t + 1], None, ALU.is_lt)
                        last = dve.scalar_tensor_tensor(l.cmp[:, 2 + t, :], srow, l.s[:, t:t + 1], earlier[:, t, :],
                                                        ALU.is_equal, ALU.mult)
                    l.links.link(last)
                    l.links.link(dve.tensor_reduce(l.cnt[:], l.cmp[:], AX_X, ALU.add))
                    l.links.link(dve.tensor_tensor(l.rank[:], l.cnt[:, 0:2], l.cnt[:, 2:4], ALU.add))
                    dve.tensor_scalar(l.rest[:], l.rank[:], float(ROUTED), None, ALU.is_ge)
                    for t in range(2):
                        last = dve.tensor_scalar(l.sel[:, t, :], ids[0:HT, :], l.rank[:, t:t + 1], None, ALU.is_equal)
                    last.then_inc(l.sel_in, 1)
                    dve.wait_ge(l.sel_in, it + 1)
                    dve.wait_ge(l.pool_out, it + 1)
                    l.links.link(dve.tensor_scalar(l.rsum[:], l.ps[0:HT, 1, C:C + 1], POOL_EPS, None, ALU.add))
                    l.links.link(dve.reciprocal(l.rsum[:], l.rsum[:]))
                    l.links.link(dve.tensor_scalar(l.pool[:], l.ps[0:HT, 1, 0:C], l.rsum[:, 0:1], None, ALU.mult))
                    for t in range(2):
                        last = dve.scalar_tensor_tensor(l.mx[:, t, :], l.pool[:], l.s[:, t:t + 1], l.nm[:, t, 0:C],
                                                        ALU.mult, ALU.add)
                    l.links.link(last)
                    for t in range(2):
                        last = dve.tensor_scalar(l.mx[:, t, :], l.mx[:, t, :], l.rest[:, t:t + 1], None, ALU.mult)
                    last.then_inc(l.mx_in, 1)
                    for t in range(2):
                        last = dve.scalar_tensor_tensor(l.hs[:, t, :], vec[0:HT, BM, t, :], l.rest[:, t:t + 1],
                                                        l.hs[:, t, :], ALU.mult, ALU.add)
                    l.links.link(last)
                if i == QUERY:
                    dve.wait_ge(l.v_out, it + 1)
                    dve_values(dve, l, vb, 1).then_inc(l.v_in, 1)
                    dve.wait_ge(l.q_out, it + 1)
                    for g in range(NG):
                        last = dve.tensor_scalar(l.q[:, g, :], l.ps[:, 0, g * ROUTED:(g + 1) * ROUTED], D ** -0.5,
                                                 qb[:, g:g + 1], ALU.mult, ALU.add)
                    last.then_inc(l.q_in, 1)
                u = i - SCORES
                if 0 <= u < UNITS:
                    dve.wait_ge(l.s_out, it * UNITS + u + 1)
                    dve.tensor_reduce(l.neg[:, UNIT * u:UNIT * (u + 1)], unit_banks(l, u)[0:ROUTED, :, 0:TOK], AX_X,
                                      ALU.max, negate=True).then_inc(l.s_max, 1)
                if i == TURNED:
                    dve.wait_ge(l.eq_in, it * UNITS + UNITS)
                    dve.reciprocal(l.den[0:ROUTED, :], l.den[0:ROUTED, :]).then_inc(l.den_in, 1)
                if i == WEIGHTED:
                    dve.wait_ge(l.pv_out, it + 1)
                    dve.wait_ge(l.rden_in, it + 1)
                    dve.tensor_tensor(l.ctx[:].rearrange("p g r -> p (g r)"), l.ps[:, 3, 0:NG * ROUTED], l.rden[:],
                                      ALU.mult).then_inc(l.ctx_in, 1)
                if i == MERGE:
                    dve.wait_ge(l.merged, it + 1)
                    l.links.link(dve.tensor_tensor(l.h1[:].rearrange("p t c -> p (t c)"),
                                                 l.hs[:].rearrange("p t c -> p (t c)"), l.ps[0:HT, 0, 0:2 * C],
                                                 ALU.add))
                    dve_norm_stats(dve, l.links, l, l.h1, LN_EPS, l.ln_in)
                if i == NORM_3:
                    dve.wait_ge(l.ln_rstd, it * 3 + 3)
                    l.links.link(dve_norm_apply(dve, l, l.mx, l.h1))
                    l.links.link(dve.tensor_tensor(l.mx[:], l.mx[:], v_(G2), ALU.mult))
                    dve.tensor_tensor(l.mx[:], l.mx[:], v_(B2), ALU.add).then_inc(l.n2_in, 1)
                    l.links.link(dve.tensor_tensor(l.h1[:], l.h1[:], v_(BF2), ALU.add))
                    l.links.link(dve.tensor_tensor(l.h1[:], l.h1[:], l.h[:], ALU.add))
                    l.links.end()
                if i == DOWN:
                    dve.wait_ge(l.down_out, it + 1)
                    dve.wait_ge(l.stored, it * 32)
                    dve.tensor_tensor(l.o[:].rearrange("p t c -> p (t c)"), l.h1[:].rearrange("p t c -> p (t c)"),
                                      l.ps[0:HT, 3, 0:2 * C], ALU.add).then_inc(l.o_in, 1)

            lanes_ahead(dve, L, stages, count, TRANSPOSE, DOWN)




def more_layouts(a, f):
    import numpy as np

    def tiles(m):
        out = np.zeros((P, 2) + m.shape[1:], np.float32)
        out[:, 0], out[:CT[1], 1] = m[:P], m[P:]
        return out

    def slots(m):
        out = np.zeros(m.shape[:-1] + (NG, HG, SLOT), np.float32)
        out[..., :D] = m.reshape(m.shape[:-1] + (NG, HG, D))
        return out.reshape(m.shape[:-1] + (NG, P))

    def back(m, bias):
        out = slots(m.T)
        if bias is not None:
            out[:, 0, V_ONE] = bias
        return out.transpose(2, 1, 0)

    qkv, bias = f["L0_attn_qkv_weight"].T, f["L0_attn_qkv_bias"]
    a["a_wq"], a["a_wk"] = tiles(slots(qkv[:, 0:C])), tiles(slots(qkv[:, C:2 * C]))
    a["a_wv"] = tiles(qkv[:, 2 * C:])
    a["a_qb"], a["a_kb"] = slots(bias[0:C]).T, slots(bias[C:2 * C]).T
    a["a_vb"] = np.tile(bias[2 * C:], (P, 2))
    a["a_wo"] = back(f["L0_attn_proj_weight"].T, f["L0_attn_proj_bias"])
    a["m_slots"] = tiles(f["L0_ffn_slot_params"].reshape(C, SLOTS))
    a["m_scale"] = np.tile(f["L0_ffn_scale"].reshape(1, 1), (P, 1))
    a["m_wd"] = tiles(f["L0_ffn_W_down"].transpose(1, 0, 2).reshape(C, C))
    a["m_wu"] = tiles(f["L0_ffn_W_up"].reshape(C, C))
    a["m_bd"] = np.tile(f["L0_ffn_b_down"].reshape(1, C), (SLOTS, 1))
    a["m_bu"] = np.repeat(f["L0_ffn_b_up"], SLOTS // EXPERTS, 0)
    a["m_own"] = np.kron(np.eye(EXPERTS, dtype=np.float32),
                         np.ones((SLOTS // EXPERTS, C // EXPERTS), np.float32))
    p = "L1_attn_"
    a["s_wq"], a["s_wk"] = tiles(slots(f[p + "Wq"])), tiles(slots(f[p + "Wk"]))
    a["s_wv"] = tiles(f[p + "Wv"])
    a["s_qb"], a["s_kb"] = slots(f[p + "bq"]).T, slots(f[p + "bk"]).T
    a["s_vb"] = np.tile(f[p + "bv"], (P, 2))
    a["s_wo"] = back(f[p + "Wo"], None)
    a["s_rows"] = np.stack([np.tile(f[p + n], (P, 2)).reshape(P, 2, C) for n in ("bo", "ln_g", "ln_b")], 1)
    p = "L1_ffn_"
    a["r_wq"], a["r_wk"] = tiles(slots(f[p + "Wq"])), tiles(slots(f[p + "Wk"]))
    a["r_wv"], a["r_wm"], a["r_w1"] = tiles(f[p + "Wv"]), tiles(f[p + "Wm"]), tiles(f[p + "W1"])
    a["r_w2"] = f[p + "W2"].reshape(HIDDEN // P, P, C).transpose(1, 0, 2)
    a["r_qb"], a["r_kb"] = slots(f[p + "bq"]).T, slots(f[p + "bk"]).T
    a["r_vb"] = np.tile(f[p + "bv"], (P, 2))
    a["r_wo"] = back(f[p + "Wo"], f[p + "bo"])
    a["r_b1"] = f[p + "bf1"].reshape(HIDDEN // P, P).T
    a["r_rows"] = np.stack([np.tile(f[p + n], (P, 2)).reshape(P, 2, C)
                            for n in ("g1", "b1", "g2", "b2", "bm", "bf2", "Wr")], 1)
    a["r_br"] = np.tile(f[p + "br"].reshape(1, 1), (P, 1))
    a["rank_ids"] = np.tile(np.arange(ROUTED, dtype=np.float32), (P, 1))
    i, j = np.arange(TP).reshape(2, HT), np.arange(TOK)
    a["earlier"] = (j[None, None, :] < i[:, :, None]).astype(np.float32).transpose(1, 0, 2)


def audio_tower(nc, w, out):
    with ExitStack() as st:
        hres = st.enter_context(nc.sbuf_tensor("hres", [HT, CLIPS, 2, C], F32))
        gmax = st.enter_context(nc.sbuf_tensor("gmax", [P, 2], F32))
        phase_tokenizer(nc, w, hres, gmax)
        phase_attention(nc, w, hres, gmax)
        phase_mixture(nc, w, hres)
        phase_sinkhorn(nc, w, hres)
        phase_routed(nc, w, hres, out)


def layouts(inputs):
    import numpy as np

    f = {k: np.asarray(v) for k, v in inputs.items()}
    a = {"x": f["x"]}
    w0 = np.zeros((COPIES, WTAPS, WIN, CH), np.float32)
    for v in range(WIN):
        w0[:, S0 * v:S0 * v + K0, v, :] = f["L0_tok_cw0"][:, 0, :].T
    a["w0"] = w0.reshape(WK, WIN * CH)
    masks = np.zeros((COPIES, WTAPS, 3), np.float32)
    for c, part in enumerate(W_PART):
        masks[c, :, part] = 1.0
    a["w0_masks"] = masks.reshape(WK, 3)
    cw = [f[f"L0_tok_cw{l}"].transpose(1, 2, 0) for l in range(1, 6)]
    a["cw"] = np.ascontiguousarray(np.concatenate(cw, axis=1))
    a["conv_vecs"] = np.stack([np.stack([f[f"L0_tok_{n}{l}"] for n in ("cb", "gw", "gb")], 1)
                               for l in range(6)], 1)
    a["pw"] = np.ascontiguousarray(f["L0_tok_pw"].T)
    a["pb"] = np.tile(f["L0_tok_pb"], (P, 2))
    a["gavg"] = np.kron(np.eye(CH // GROUP), np.full((GROUP, GROUP), 1 / GROUP)).astype(np.float32)
    a["ident"] = np.eye(P, dtype=np.float32)
    more_layouts(a, f)
    return a


def kernel(**inputs):
    import numpy as _np
    import concourse.bacc as _bacc
    from concourse import mybir as _mybir
    from concourse.bass_utils import run_bass_kernel_spmd as _run

    nc = _bacc.Bacc("TRN2", target_bir_lowering=False, num_devices=1)
    arrays, w = {}, {}
    for name, a in layouts(inputs).items():
        a = _np.ascontiguousarray(a)
        arrays[f"in_{name}"] = a
        w[name] = nc.dram_tensor(f"in_{name}", a.shape, _mybir.dt.from_np(a.dtype), kind="ExternalInput").ap()
    out = nc.dram_tensor("out_h", (CLIPS, TOK, C), F32, kind="ExternalOutput").ap()
    audio_tower(nc, w, out)
    r = _run(nc, [arrays], core_ids=[0])
    return r.results[0]["out_h"]
```
